# Optimizing a Trainium2 kernel written in Bass

```python
import numpy as np
import jax
import jax.numpy as jnp

def _softmax(x, axis=-1):
    return jax.nn.softmax(x, axis=axis)

def _gelu(x):
    return jax.nn.gelu(x, approximate=True)

def _silu(x):
    return jax.nn.silu(x)

def _sigmoid(x):
    return jax.nn.sigmoid(x)

def _layernorm(x, axis=-1, eps=1e-05):
    m = jnp.mean(x, axis=axis, keepdims=True)
    v = jnp.var(x, axis=axis, keepdims=True)
    return (x - m) / jnp.sqrt(v + eps)

def _scatter_add(tgt, idx, src, axis=0):
    return tgt.at[idx].add(src)

def _segment_sum(src, seg, n):
    return jax.ops.segment_sum(src, seg, n)
kernel_name = 'mk_decoder_postln_d4_seqx_r8_6d6d22'

def setup_inputs(seed: int=0):
    np.random.seed(seed)
    _w = jnp.asarray

    def _rec_inputs():
        import jax
        import jax.numpy as jnp
        _rk = jax.random.key(seed)
        x = -0.0002928 + 1 * jax.random.normal(jax.random.fold_in(_rk, 1), (4, 512, 128), jnp.float32)
        _lenS = 512 - jax.random.randint(jax.random.fold_in(_rk, 7), (4,), 0, max(1, 512 // 4) + 1, jnp.int32)
        _lenS2 = 154 - jax.random.randint(jax.random.fold_in(_rk, 8), (4,), 0, max(1, 154 // 4) + 1, jnp.int32)
        _ctx_1024P = jax.random.normal(jax.random.fold_in(_rk, 11), (4, 16, 128), jnp.float32)
        _ctx_1024c = jax.random.dirichlet(jax.random.fold_in(_rk, 511), 0.3 * jnp.ones((16,), jnp.float32), (4, 154))
        _ctx_1024t = jnp.einsum('bsk,bkd->bsd', _ctx_1024c, _ctx_1024P)
        _ctx_1024t = _ctx_1024t * jax.lax.rsqrt(jnp.mean(jnp.square(_ctx_1024t)) + 1e-12) * 0.953939
        ctx_1024 = -1.39393e-06 + 0.999914 * (_ctx_1024t + 0.3 * jax.random.normal(jax.random.fold_in(_rk, 611), (4, 154, 128), jnp.float32))
        _validS = jnp.arange(512)[None, :] < _lenS[:, None]
        _validS2 = jnp.arange(154)[None, :] < _lenS2[:, None]
        _causal = jnp.tril(jnp.ones((512, 512), dtype=bool))
        mask_BxS2_if1 = jnp.where(jnp.ones((4, 154), dtype=bool), 1, 0).astype(jnp.int32)
        mask_BxSxS2_ik0 = jnp.where(jnp.broadcast_to(_validS2[:, None, :], (4, 512, 154)), 0, 1).astype(jnp.int32)
        mask_BxS2_bk0 = jnp.logical_not(jnp.broadcast_to(_validS2[:, :], (4, 154)))
        return (x, ctx_1024, mask_BxS2_if1, mask_BxSxS2_ik0, mask_BxS2_bk0)
    x, ctx_1024, mask_BxS2_if1, mask_BxSxS2_ik0, mask_BxS2_bk0 = _rec_inputs()

    def _L0_attn_setup():
        import jax, jax.numpy as jnp
        import numpy as np
        HIDDEN = 128
        BETA = 1.0
        SPARSITY_THRESHOLD = 1.0

        def _sparsemax(x):
            n = x.shape[-1]
            z = x - jnp.max(x, axis=-1, keepdims=True)
            sum_z = jnp.sum(z, axis=-1, keepdims=True)
            step = (sum_z - 1.0) / n
            sorted_z = -jnp.sort(-z, axis=-1)
            cumsum_z = jnp.cumsum(sorted_z, axis=-1)
            is_gt = sorted_z > step
            rng = jnp.arange(1, n + 1, dtype=jnp.int32)
            k = jnp.max(rng * is_gt, axis=-1, keepdims=True).astype(x.dtype)
            tau = (cumsum_z - 1.0 - step * k) / k
            return jnp.clip(z - tau, 0.0)
        key = jax.random.key(seed)
        kx, kq, kk, kv = jax.random.split(key, 4)
        B, S, D = (4, 256, 128)
        x = jax.random.normal(kx, (B, S, D), dtype=jnp.float32)
        scale = 1.0 / np.sqrt(D)
        Wq = jax.random.normal(kq, (HIDDEN, D), dtype=jnp.float32) * scale
        Wk = jax.random.normal(kk, (HIDDEN, D), dtype=jnp.float32) * scale
        Wv = jax.random.normal(kv, (HIDDEN, D), dtype=jnp.float32) * scale
        return {'x': x, 'Wq': Wq, 'Wk': Wk, 'Wv': Wv}
    _L0_attn_all = _L0_attn_setup()
    _L0_attn_in = {k: v for k, v in _L0_attn_all.items() if k in ('Wq', 'Wk', 'Wv')}
    del _L0_attn_all

    def _L0_xattn_setup():
        import jax, jax.numpy as jnp
        import numpy as np
        D_MODEL = 128
        H = 16
        D_K = D_MODEL // H
        NEG = -1000000000.0
        key = jax.random.key(seed)
        ks = jax.random.split(key, 8)
        B, S = (2, 256)
        q = jax.random.normal(ks[0], (B, S, D_MODEL), dtype=jnp.float32)
        k = jax.random.normal(ks[1], (B, S, D_MODEL), dtype=jnp.float32)
        v = jax.random.normal(ks[2], (B, S, D_MODEL), dtype=jnp.float32)
        mask = jnp.ones((B, S), dtype=jnp.int32)
        s = 1.0 / np.sqrt(D_MODEL)
        w_q = jax.random.normal(ks[3], (D_MODEL, D_MODEL), dtype=jnp.float32) * s
        w_k = jax.random.normal(ks[4], (D_MODEL, D_MODEL), dtype=jnp.float32) * s
        w_v = jax.random.normal(ks[5], (D_MODEL, D_MODEL), dtype=jnp.float32) * s
        w_o = jax.random.normal(ks[6], (D_MODEL, D_MODEL), dtype=jnp.float32) * s
        return {'q': q, 'k': k, 'v': v, 'mask': mask, 'w_q': w_q, 'w_k': w_k, 'w_v': w_v, 'w_o': w_o}
    _L0_xattn_all = _L0_xattn_setup()
    _L0_xattn_in = {k: v for k, v in _L0_xattn_all.items() if k in ('w_q', 'w_k', 'w_v', 'w_o')}
    del _L0_xattn_all

    def _L0_ffn_setup():
        import jax, jax.numpy as jnp
        import numpy as np
        TOP_K = 4
        N_GROUP = 4
        TOPK_GROUP = 2
        ROUTED_SCALING = 1.0

        def _route(x_flat, gate_weight, e_bias):
            T = x_flat.shape[0]
            E = gate_weight.shape[0]
            logits = jnp.einsum('th,eh->te', x_flat, gate_weight)
            scores = jax.nn.sigmoid(logits)
            scores_for_choice = scores + e_bias[None, :]
            grp = scores_for_choice.reshape(T, N_GROUP, E // N_GROUP)
            top2, _ = jax.lax.top_k(grp, 2)
            group_scores = top2.sum(axis=-1)
            _, group_idx = jax.lax.top_k(group_scores, TOPK_GROUP)
            group_mask = jax.nn.one_hot(group_idx, N_GROUP, dtype=scores.dtype).sum(axis=1)
            score_mask = jnp.repeat(group_mask, E // N_GROUP, axis=1)
            tmp_scores = jnp.where(score_mask > 0, scores_for_choice, 0.0)
            _, topk_idx = jax.lax.top_k(tmp_scores, TOP_K)
            topk_weight = jnp.take_along_axis(scores, topk_idx, axis=1)
            denom = topk_weight.sum(axis=-1, keepdims=True) + 1e-20
            topk_weight = topk_weight / denom * ROUTED_SCALING
            return (topk_idx, topk_weight)
        key = jax.random.key(seed)
        k1, k2, k3, k4, k5 = jax.random.split(key, 5)
        B, S, H, I, E = (1, 256, 128, 64, 16)
        hidden_states = jax.random.normal(k1, (B, S, H), dtype=jnp.float32)
        gate_weight = jax.random.normal(k2, (E, H), dtype=jnp.float32) * (1.0 / np.sqrt(H))
        e_bias = jnp.zeros((E,), dtype=jnp.float32)
        gate_proj = jax.random.normal(k3, (E, I, H), dtype=jnp.float32) * 0.02
        up_proj = jax.random.normal(k4, (E, I, H), dtype=jnp.float32) * 0.02
        down_proj = jax.random.normal(k5, (E, H, I), dtype=jnp.float32) * 0.02
        return {'hidden_states': hidden_states, 'gate_weight': gate_weight, 'e_bias': e_bias, 'gate_proj': gate_proj, 'up_proj': up_proj, 'down_proj': down_proj}
    _L0_ffn_all = _L0_ffn_setup()
    _L0_ffn_in = {k: v for k, v in _L0_ffn_all.items() if k in ('gate_weight', 'e_bias', 'gate_proj', 'up_proj', 'down_proj')}
    del _L0_ffn_all

    def _L1_attn_setup():
        import jax, jax.numpy as jnp
        import numpy as np
        from math import sqrt
        D_MODEL = 128
        NUM_HEADS = 16
        MASK_VAL = -100000000.0

        def _proj_heads(x, w, h):
            d = w.shape[0] // h
            w = w.reshape(h, d, w.shape[1])
            return jnp.einsum('bsi,hdi->bhsd', x, w)
        key = jax.random.key(seed)
        k1, k2, k3, k4, k5 = jax.random.split(key, 5)
        scale = 1.0 / sqrt(D_MODEL)
        return {'in_features': jax.random.normal(k1, (2, 256, D_MODEL), dtype=jnp.float32), 'q_proj_weight': jax.random.normal(k2, (D_MODEL, D_MODEL), dtype=jnp.float32) * scale, 'k_proj_weight': jax.random.normal(k3, (D_MODEL, D_MODEL), dtype=jnp.float32) * scale, 'v_proj_weight': jax.random.normal(k4, (D_MODEL, D_MODEL), dtype=jnp.float32) * scale, 'o_proj_weight': jax.random.normal(k5, (D_MODEL, D_MODEL), dtype=jnp.float32) * scale}
    _L1_attn_all = _L1_attn_setup()
    _L1_attn_in = {k: v for k, v in _L1_attn_all.items() if k in ('q_proj_weight', 'k_proj_weight', 'v_proj_weight', 'o_proj_weight')}
    del _L1_attn_all

    def _L1_xattn_setup():
        import jax, jax.numpy as jnp
        import numpy as np
        N_HEAD = 16
        key = jax.random.key(seed)
        ks = jax.random.split(key, 5)
        b, l, d = (4, 256, 128)
        dh = d // N_HEAD
        return {'q': jax.random.normal(ks[0], (b, l, d), dtype=jnp.float32), 'kv': jax.random.normal(ks[1], (b, l, d), dtype=jnp.float32), 'Wq': jax.random.normal(ks[2], (d, d), dtype=jnp.float32) * 0.02, 'Wkv': jax.random.normal(ks[3], (2 * dh, d), dtype=jnp.float32) * 0.02, 'Wc': jax.random.normal(ks[4], (d, d), dtype=jnp.float32) * 0.02}
    _L1_xattn_all = _L1_xattn_setup()
    _L1_xattn_in = {k: v for k, v in _L1_xattn_all.items() if k in ('Wq', 'Wkv', 'Wc')}
    del _L1_xattn_all

    def _L1_ffn_setup():
        import jax, jax.numpy as jnp
        import numpy as np
        MICRO_BATCHES = 2
        TOP_K = 2
        LN_EPS = 1e-05
        B, S, D = (4, 512, 128)
        E = 8
        DFF = 4 * D

        def _layernorm(x, g, b):
            mu = jnp.mean(x, axis=-1, keepdims=True)
            var = jnp.mean(jnp.square(x - mu), axis=-1, keepdims=True)
            return (x - mu) * jax.lax.rsqrt(var + LN_EPS) * g + b
        key = jax.random.key(seed)
        ks = jax.random.split(key, 12)
        sd = 1.0 / np.sqrt(D)
        sf = 1.0 / np.sqrt(DFF)
        return {'x': jax.random.normal(ks[0], (B, S, D), dtype=jnp.float32), 'ln_g': jnp.ones((D,), jnp.float32), 'ln_b': jnp.zeros((D,), jnp.float32), 'attn_w': jax.random.normal(ks[1], (D, D), jnp.float32) * sd, 'attn_b': jnp.zeros((D,), jnp.float32), 'gate_w': jax.random.normal(ks[2], (D, E), jnp.float32) * sd, 'w1': jax.random.normal(ks[3], (E, D, DFF), jnp.float32) * sd, 'b1': jnp.zeros((E, DFF), jnp.float32), 'w2': jax.random.normal(ks[4], (E, DFF, D), jnp.float32) * sf, 'b2': jnp.zeros((E, D), jnp.float32), 'next_w': jax.random.normal(ks[5], (D, D), jnp.float32) * sd, 'next_b': jnp.zeros((D,), jnp.float32)}
    _L1_ffn_all = _L1_ffn_setup()
    _L1_ffn_in = {k: v for k, v in _L1_ffn_all.items() if k in ('ln_g', 'ln_b', 'attn_w', 'attn_b', 'gate_w', 'w1', 'b1', 'w2', 'b2', 'next_w', 'next_b')}
    del _L1_ffn_all

    def _L2_attn_setup():
        import jax, jax.numpy as jnp
        import numpy as np
        EPS = 1e-05
        key = jax.random.key(seed)
        ks = jax.random.split(key, 8)
        B, T, C, H = (2, 256, 128, 16)
        hs = C // H
        scale = 1.0 / np.sqrt(C)
        x = jax.random.normal(ks[0], (B, T, C), dtype=jnp.float32)
        wq1 = jax.random.normal(ks[1], (H, C, hs), dtype=jnp.float32) * scale
        wk1 = jax.random.normal(ks[2], (H, C, hs), dtype=jnp.float32) * scale
        wq2 = jax.random.normal(ks[3], (H, C, hs), dtype=jnp.float32) * scale
        wk2 = jax.random.normal(ks[4], (H, C, hs), dtype=jnp.float32) * scale
        wv = jax.random.normal(ks[5], (H, C, hs), dtype=jnp.float32) * scale
        ln_gamma = jnp.ones((C,), dtype=jnp.float32)
        ln_beta = jnp.zeros((C,), dtype=jnp.float32)
        lamb = jnp.float32(0.8)
        return {'x': x, 'wq1': wq1, 'wk1': wk1, 'wq2': wq2, 'wk2': wk2, 'wv': wv, 'ln_gamma': ln_gamma, 'ln_beta': ln_beta, 'lamb': lamb}
    _L2_attn_all = _L2_attn_setup()
    _L2_attn_in = {k: v for k, v in _L2_attn_all.items() if k in ('wq1', 'wk1', 'wq2', 'wk2', 'wv', 'ln_gamma', 'ln_beta', 'lamb')}
    del _L2_attn_all

    def _L2_xattn_setup():
        import jax, jax.numpy as jnp
        import numpy as np
        B, NKV, NQ, D, H = (4, 256, 128, 128, 16)
        HD = D // H
        key = jax.random.key(seed)
        ks = jax.random.split(key, 9)
        s = 0.02
        return {'x': jax.random.normal(ks[0], (B, NKV, D), jnp.float32), 'y': jax.random.normal(ks[1], (B, NQ, D), jnp.float32), 'mask': jax.random.randint(ks[2], (B, NQ, NKV), 0, 2, jnp.int32), 'W_kv': jax.random.normal(ks[3], (D, 2 * D), jnp.float32) * s, 'b_kv': jnp.zeros((2 * D,), jnp.float32), 'W_q': jax.random.normal(ks[4], (D, D), jnp.float32) * s, 'b_q': jnp.zeros((D,), jnp.float32), 'W_o': jax.random.normal(ks[5], (D, D), jnp.float32) * s, 'b_o': jnp.zeros((D,), jnp.float32)}
    _L2_xattn_all = _L2_xattn_setup()
    _L2_xattn_in = {k: v for k, v in _L2_xattn_all.items() if k in ('W_kv', 'b_kv', 'W_q', 'b_q', 'W_o', 'b_o')}
    del _L2_xattn_all

    def _L2_ffn_setup():
        import jax, jax.numpy as jnp
        import numpy as np
        TOP_K = 8
        CAPACITY = 64

        def _silu(x):
            return x * jax.nn.sigmoid(x)
        key = jax.random.key(seed)
        ks = jax.random.split(key, 7)
        B, S, H, E, I, Is = (2, 128, 128, 64, 64, 256)
        s = 0.05
        return {'hidden_states': jax.random.normal(ks[0], (B, S, H), jnp.float32), 'gate_w': jax.random.normal(ks[1], (H, E), jnp.float32) * s, 'shared_gate_w': jax.random.normal(ks[2], (H, 1), jnp.float32) * s, 'shared_gate_up_w': jax.random.normal(ks[3], (H, 2 * Is), jnp.float32) * s, 'shared_down_w': jax.random.normal(ks[4], (Is, H), jnp.float32) * s, 'expert_gate_up_w': jax.random.normal(ks[5], (E, H, 2 * I), jnp.float32) * s, 'expert_down_w': jax.random.normal(ks[6], (E, I, H), jnp.float32) * s}
    _L2_ffn_all = _L2_ffn_setup()
    _L2_ffn_in = {k: v for k, v in _L2_ffn_all.items() if k in ('gate_w', 'shared_gate_w', 'shared_gate_up_w', 'shared_down_w', 'expert_gate_up_w', 'expert_down_w')}
    del _L2_ffn_all

    def _L3_attn_setup():
        import jax, jax.numpy as jnp
        import numpy as np
        N_EMBD = 128
        N_HEAD = 16
        HEAD_SIZE = N_EMBD // N_HEAD
        B, T = (8, 512)
        EPS = 0.001
        key = jax.random.key(seed)
        k1, k2, k3 = jax.random.split(key, 3)
        x = jax.random.normal(k1, (B, T, N_EMBD), dtype=jnp.float32)
        Wqkv = jax.random.normal(k2, (3 * N_EMBD, N_EMBD), dtype=jnp.float32) * 0.02
        bqkv = jnp.zeros((3 * N_EMBD,), dtype=jnp.float32)
        Wproj = jax.random.normal(k3, (N_EMBD, N_EMBD), dtype=jnp.float32) * 0.02
        bproj = jnp.zeros((N_EMBD,), dtype=jnp.float32)
        scale = jnp.asarray(1.0 / np.sqrt(HEAD_SIZE), dtype=jnp.float32)
        return {'x': x, 'Wqkv': Wqkv, 'bqkv': bqkv, 'Wproj': Wproj, 'bproj': bproj, 'scale': scale}
    _L3_attn_all = _L3_attn_setup()
    _L3_attn_in = {k: v for k, v in _L3_attn_all.items() if k in ('Wqkv', 'bqkv', 'Wproj', 'bproj', 'scale')}
    del _L3_attn_all

    def _L3_xattn_setup():
        import jax, jax.numpy as jnp
        import numpy as np
        DIM = 128
        DIM_LATENT = 128
        DIM_HEAD = 64
        INNER = max(DIM, DIM_LATENT)
        HEADS = INNER // DIM_HEAD
        SCALE = DIM_HEAD ** (-0.5)
        LN_EPS = 1e-05
        RMS_EPS = 1e-08

        def layernorm(x, g, b):
            mu = jnp.mean(x, axis=-1, keepdims=True)
            var = jnp.mean(jnp.square(x - mu), axis=-1, keepdims=True)
            return (x - mu) * jax.lax.rsqrt(var + LN_EPS) * g + b

        def rmsnorm(x, gamma):
            n = jnp.linalg.norm(x, axis=-1, keepdims=True) * x.shape[-1] ** (-0.5)
            return x / jnp.maximum(n, RMS_EPS) * gamma
        key = jax.random.key(seed)
        ks = jax.random.split(key, 8)
        b, n, nl = (8, 256, 64)
        x = jax.random.normal(ks[0], (b, n, DIM), dtype=jnp.float32)
        latents = jax.random.normal(ks[1], (b, nl, DIM_LATENT), dtype=jnp.float32)
        mask = jax.random.randint(ks[2], (b, n), 0, 2).astype(bool)
        init = lambda k, shape, fan_in: jax.random.normal(k, shape, jnp.float32) * fan_in ** (-0.5)
        return {'x': x, 'latents': latents, 'mask': mask, 'ln_x_g': jnp.ones((DIM,), jnp.float32), 'ln_x_b': jnp.zeros((DIM,), jnp.float32), 'ln_l_g': jnp.ones((DIM_LATENT,), jnp.float32), 'ln_l_b': jnp.zeros((DIM_LATENT,), jnp.float32), 'q_gamma': jnp.ones((DIM_HEAD,), jnp.float32), 'k_gamma': jnp.ones((DIM_HEAD,), jnp.float32), 'W_q': init(ks[3], (DIM_LATENT, INNER), DIM_LATENT), 'W_kv': init(ks[4], (DIM, 2 * INNER), DIM), 'W_out': init(ks[5], (INNER, DIM_LATENT), INNER), 'b_out': jnp.zeros((DIM_LATENT,), jnp.float32)}
    _L3_xattn_all = _L3_xattn_setup()
    _L3_xattn_in = {k: v for k, v in _L3_xattn_all.items() if k in ('ln_x_g', 'ln_x_b', 'ln_l_g', 'ln_l_b', 'q_gamma', 'k_gamma', 'W_q', 'W_kv', 'W_out', 'b_out')}
    del _L3_xattn_all

    def _L3_ffn_setup():
        import jax, jax.numpy as jnp
        import numpy as np
        DIM = 128
        DEPTH = 6
        HEADS = 16
        DIM_HEAD = 64
        WINDOW = 32
        INNER = HEADS * DIM_HEAD
        DIM_INNER = int(DIM * 4 * 2 / 3)
        QK_SCALE = 8.0

        def shift_tokens(t):
            a, s = jnp.split(t, 2, -1)
            s = jnp.pad(s, ((0, 0), (1, 0), (0, 0)))[:, :-1]
            return jnp.concatenate([a, s], -1)

        def l2norm(t):
            return t / jnp.maximum(jnp.linalg.norm(t, axis=-1, keepdims=True), 1e-12)

        def rotate_half(x):
            x1, x2 = jnp.split(x, 2, -1)
            return jnp.concatenate([-x2, x1], -1)

        def rotary_tables(n):
            half = jnp.arange(0, DIM_HEAD, 2, dtype=jnp.float32)
            inv_freq = 1.0 / 10000.0 ** (half / DIM_HEAD)
            t = jnp.arange(n, dtype=jnp.float32)
            freqs = t[:, None] * inv_freq[None, :]
            freqs = jnp.concatenate([freqs, freqs], -1)
            base_scale = (half + 0.4 * DIM_HEAD) / (1.4 * DIM_HEAD)
            power = (t - n // 2) / (WINDOW // 2)
            scale = base_scale[None, :] ** power[:, None]
            scale = jnp.concatenate([scale, scale], -1)
            return (freqs, scale)

        def local_attention(q, k, v):
            b, h, n, d = q.shape
            w = WINDOW
            nw = n // w
            bq = q.reshape(b, h, nw, w, d)
            bk = k.reshape(b, h, nw, w, d)
            bv = v.reshape(b, h, nw, w, d)

            def look(t):
                p = jnp.pad(t, ((0, 0), (0, 0), (1, 0), (0, 0), (0, 0)))
                return jnp.concatenate([p[:, :, :nw], p[:, :, 1:]], axis=3)
            bk2, bv2 = (look(bk), look(bv))
            seq = jnp.arange(n).reshape(nw, w)
            seq_p = jnp.pad(seq, ((1, 0), (0, 0)), constant_values=-1)
            jt = jnp.concatenate([seq_p[:nw], seq_p[1:]], axis=1)
            it = seq[:, :, None]
            jb = jt[:, None, :]
            mask = (it < jb) | (it > jb + w) | (jb == -1)
            sim = jnp.einsum('bhwie,bhwje->bhwij', bq, bk2) * QK_SCALE
            sim = jnp.where(mask, -jnp.finfo(sim.dtype).max, sim)
            attn = jax.nn.softmax(sim, -1)
            out = jnp.einsum('bhwij,bhwje->bhwie', attn, bv2)
            return out.reshape(b, h, n, d)

        def attn_layer(x, Wqkv, qs, ksc, Wo):
            b, n, _ = x.shape
            qkv = x @ Wqkv
            q, k, v = jnp.split(qkv, 3, -1)
            sh = lambda t: t.reshape(b, n, HEADS, DIM_HEAD).transpose(0, 2, 1, 3)
            q, k, v = (sh(q), sh(k), sh(v))
            q = l2norm(q) * qs
            k = l2norm(k) * ksc
            freqs, scale = rotary_tables(n)
            cos, sin = (jnp.cos(freqs), jnp.sin(freqs))
            q = q * cos * scale + rotate_half(q) * sin * scale
            inv = 1.0 / scale
            k = k * cos * inv + rotate_half(k) * sin * inv
            out = local_attention(q, k, v)
            out = out.transpose(0, 2, 1, 3).reshape(b, n, INNER)
            return out @ Wo

        def ffn_layer(x, g, bln, W1, b1, W2, b2):
            mu = x.mean(-1, keepdims=True)
            var = ((x - mu) ** 2).mean(-1, keepdims=True)
            xn = (x - mu) / jnp.sqrt(var + 1e-05) * g + bln
            hg = xn @ W1 + b1
            a, gate = jnp.split(hg, 2, -1)
            return a * jax.nn.gelu(gate, approximate=False) @ W2 + b2
        key = jax.random.key(seed)
        ks = jax.random.split(key, 8)
        B, N = (2, 256)
        init = lambda k, shape: jax.random.normal(k, shape, jnp.float32) * 0.02
        return {'x': jax.random.normal(ks[0], (B, N, DIM), jnp.float32), 'Wqkv': init(ks[1], (DEPTH, DIM, 3 * INNER)), 'q_scale': jnp.ones((DEPTH, DIM_HEAD), jnp.float32), 'k_scale': jnp.ones((DEPTH, DIM_HEAD), jnp.float32), 'Wo': init(ks[2], (DEPTH, INNER, DIM)), 'ln_g': jnp.ones((DEPTH, DIM), jnp.float32), 'ln_b': jnp.zeros((DEPTH, DIM), jnp.float32), 'W1': init(ks[3], (DEPTH, DIM, 2 * DIM_INNER)), 'b1': jnp.zeros((DEPTH, 2 * DIM_INNER), jnp.float32), 'W2': init(ks[4], (DEPTH, DIM_INNER, DIM)), 'b2': jnp.zeros((DEPTH, DIM), jnp.float32)}
    _L3_ffn_all = _L3_ffn_setup()
    _L3_ffn_in = {k: v for k, v in _L3_ffn_all.items() if k in ('Wqkv', 'q_scale', 'k_scale', 'Wo', 'ln_g', 'ln_b', 'W1', 'b1', 'W2', 'b2')}
    del _L3_ffn_all
    return {'x': x, 'ctx_1024': ctx_1024, 'mask_BxS2_if1': mask_BxS2_if1, 'mask_BxSxS2_ik0': mask_BxSxS2_ik0, 'mask_BxS2_bk0': mask_BxS2_bk0, 'L0_attn_Wq': _L0_attn_in['Wq'], 'L0_attn_Wk': _L0_attn_in['Wk'], 'L0_attn_Wv': _L0_attn_in['Wv'], 'L0_xattn_w_q': _L0_xattn_in['w_q'], 'L0_xattn_w_k': _L0_xattn_in['w_k'], 'L0_xattn_w_v': _L0_xattn_in['w_v'], 'L0_xattn_w_o': _L0_xattn_in['w_o'], 'L0_ffn_gate_weight': _L0_ffn_in['gate_weight'], 'L0_ffn_e_bias': _L0_ffn_in['e_bias'], 'L0_ffn_gate_proj': _L0_ffn_in['gate_proj'], 'L0_ffn_up_proj': _L0_ffn_in['up_proj'], 'L0_ffn_down_proj': _L0_ffn_in['down_proj'], 'L1_attn_q_proj_weight': _L1_attn_in['q_proj_weight'], 'L1_attn_k_proj_weight': _L1_attn_in['k_proj_weight'], 'L1_attn_v_proj_weight': _L1_attn_in['v_proj_weight'], 'L1_attn_o_proj_weight': _L1_attn_in['o_proj_weight'], 'L1_xattn_Wq': _L1_xattn_in['Wq'], 'L1_xattn_Wkv': _L1_xattn_in['Wkv'], 'L1_xattn_Wc': _L1_xattn_in['Wc'], 'L1_ffn_ln_g': _L1_ffn_in['ln_g'], 'L1_ffn_ln_b': _L1_ffn_in['ln_b'], 'L1_ffn_attn_w': _L1_ffn_in['attn_w'], 'L1_ffn_attn_b': _L1_ffn_in['attn_b'], 'L1_ffn_gate_w': _L1_ffn_in['gate_w'], 'L1_ffn_w1': _L1_ffn_in['w1'], 'L1_ffn_b1': _L1_ffn_in['b1'], 'L1_ffn_w2': _L1_ffn_in['w2'], 'L1_ffn_b2': _L1_ffn_in['b2'], 'L1_ffn_next_w': _L1_ffn_in['next_w'], 'L1_ffn_next_b': _L1_ffn_in['next_b'], 'L2_attn_wq1': _L2_attn_in['wq1'], 'L2_attn_wk1': _L2_attn_in['wk1'], 'L2_attn_wq2': _L2_attn_in['wq2'], 'L2_attn_wk2': _L2_attn_in['wk2'], 'L2_attn_wv': _L2_attn_in['wv'], 'L2_attn_ln_gamma': _L2_attn_in['ln_gamma'], 'L2_attn_ln_beta': _L2_attn_in['ln_beta'], 'L2_attn_lamb': _L2_attn_in['lamb'], 'L2_xattn_W_kv': _L2_xattn_in['W_kv'], 'L2_xattn_b_kv': _L2_xattn_in['b_kv'], 'L2_xattn_W_q': _L2_xattn_in['W_q'], 'L2_xattn_b_q': _L2_xattn_in['b_q'], 'L2_xattn_W_o': _L2_xattn_in['W_o'], 'L2_xattn_b_o': _L2_xattn_in['b_o'], 'L2_ffn_gate_w': _L2_ffn_in['gate_w'], 'L2_ffn_shared_gate_w': _L2_ffn_in['shared_gate_w'], 'L2_ffn_shared_gate_up_w': _L2_ffn_in['shared_gate_up_w'], 'L2_ffn_shared_down_w': _L2_ffn_in['shared_down_w'], 'L2_ffn_expert_gate_up_w': _L2_ffn_in['expert_gate_up_w'], 'L2_ffn_expert_down_w': _L2_ffn_in['expert_down_w'], 'L3_attn_Wqkv': _L3_attn_in['Wqkv'], 'L3_attn_bqkv': _L3_attn_in['bqkv'], 'L3_attn_Wproj': _L3_attn_in['Wproj'], 'L3_attn_bproj': _L3_attn_in['bproj'], 'L3_attn_scale': _L3_attn_in['scale'], 'L3_xattn_ln_x_g': _L3_xattn_in['ln_x_g'], 'L3_xattn_ln_x_b': _L3_xattn_in['ln_x_b'], 'L3_xattn_ln_l_g': _L3_xattn_in['ln_l_g'], 'L3_xattn_ln_l_b': _L3_xattn_in['ln_l_b'], 'L3_xattn_q_gamma': _L3_xattn_in['q_gamma'], 'L3_xattn_k_gamma': _L3_xattn_in['k_gamma'], 'L3_xattn_W_q': _L3_xattn_in['W_q'], 'L3_xattn_W_kv': _L3_xattn_in['W_kv'], 'L3_xattn_W_out': _L3_xattn_in['W_out'], 'L3_xattn_b_out': _L3_xattn_in['b_out'], 'L3_ffn_Wqkv': _L3_ffn_in['Wqkv'], 'L3_ffn_q_scale': _L3_ffn_in['q_scale'], 'L3_ffn_k_scale': _L3_ffn_in['k_scale'], 'L3_ffn_Wo': _L3_ffn_in['Wo'], 'L3_ffn_ln_g': _L3_ffn_in['ln_g'], 'L3_ffn_ln_b': _L3_ffn_in['ln_b'], 'L3_ffn_W1': _L3_ffn_in['W1'], 'L3_ffn_b1': _L3_ffn_in['b1'], 'L3_ffn_W2': _L3_ffn_in['W2'], 'L3_ffn_b2': _L3_ffn_in['b2']}

def reference(x, ctx_1024, mask_BxS2_if1, mask_BxSxS2_ik0, mask_BxS2_bk0, L0_attn_Wq, L0_attn_Wk, L0_attn_Wv, L0_xattn_w_q, L0_xattn_w_k, L0_xattn_w_v, L0_xattn_w_o, L0_ffn_gate_weight, L0_ffn_e_bias, L0_ffn_gate_proj, L0_ffn_up_proj, L0_ffn_down_proj, L1_attn_q_proj_weight, L1_attn_k_proj_weight, L1_attn_v_proj_weight, L1_attn_o_proj_weight, L1_xattn_Wq, L1_xattn_Wkv, L1_xattn_Wc, L1_ffn_ln_g, L1_ffn_ln_b, L1_ffn_attn_w, L1_ffn_attn_b, L1_ffn_gate_w, L1_ffn_w1, L1_ffn_b1, L1_ffn_w2, L1_ffn_b2, L1_ffn_next_w, L1_ffn_next_b, L2_attn_wq1, L2_attn_wk1, L2_attn_wq2, L2_attn_wk2, L2_attn_wv, L2_attn_ln_gamma, L2_attn_ln_beta, L2_attn_lamb, L2_xattn_W_kv, L2_xattn_b_kv, L2_xattn_W_q, L2_xattn_b_q, L2_xattn_W_o, L2_xattn_b_o, L2_ffn_gate_w, L2_ffn_shared_gate_w, L2_ffn_shared_gate_up_w, L2_ffn_shared_down_w, L2_ffn_expert_gate_up_w, L2_ffn_expert_down_w, L3_attn_Wqkv, L3_attn_bqkv, L3_attn_Wproj, L3_attn_bproj, L3_attn_scale, L3_xattn_ln_x_g, L3_xattn_ln_x_b, L3_xattn_ln_l_g, L3_xattn_ln_l_b, L3_xattn_q_gamma, L3_xattn_k_gamma, L3_xattn_W_q, L3_xattn_W_kv, L3_xattn_W_out, L3_xattn_b_out, L3_ffn_Wqkv, L3_ffn_q_scale, L3_ffn_k_scale, L3_ffn_Wo, L3_ffn_ln_g, L3_ffn_ln_b, L3_ffn_W1, L3_ffn_b1, L3_ffn_W2, L3_ffn_b2):
    import jax
    import jax.numpy as jnp

    def _L0_attn_ref(x, Wq, Wk, Wv):
        import jax, jax.numpy as jnp
        import numpy as np
        HIDDEN = 128
        BETA = 1.0
        SPARSITY_THRESHOLD = 1.0

        def _sparsemax(x):
            n = x.shape[-1]
            z = x - jnp.max(x, axis=-1, keepdims=True)
            sum_z = jnp.sum(z, axis=-1, keepdims=True)
            step = (sum_z - 1.0) / n
            sorted_z = -jnp.sort(-z, axis=-1)
            cumsum_z = jnp.cumsum(sorted_z, axis=-1)
            is_gt = sorted_z > step
            rng = jnp.arange(1, n + 1, dtype=jnp.int32)
            k = jnp.max(rng * is_gt, axis=-1, keepdims=True).astype(x.dtype)
            tau = (cumsum_z - 1.0 - step * k) / k
            return jnp.clip(z - tau, 0.0)
        Q = jnp.einsum('bsd,hd->bsh', x, Wq)
        K = jnp.einsum('bsd,hd->bsh', x, Wk)
        V = jnp.einsum('bsd,hd->bsh', x, Wv)
        energy = jnp.einsum('bsh,bth->bst', Q, K) / jnp.sqrt(jnp.asarray(HIDDEN, x.dtype))
        scores = energy * BETA
        sparsity = jnp.mean(jnp.abs(x))
        attention = jax.lax.cond(sparsity < SPARSITY_THRESHOLD, _sparsemax, lambda s: jax.nn.softmax(s, axis=-1), scores)
        return jnp.einsum('bst,bth->bsh', attention, V)

    def _L0_xattn_ref(q, k, v, mask, w_q, w_k, w_v, w_o):
        import jax, jax.numpy as jnp
        import numpy as np
        D_MODEL = 128
        H = 16
        D_K = D_MODEL // H
        NEG = -1000000000.0
        B, S, _ = q.shape

        def proj(x, w):
            return (x @ w.T).reshape(B, -1, H, D_K).transpose(0, 2, 1, 3)
        Q, K, V = (proj(q, w_q), proj(k, w_k), proj(v, w_v))
        scores = jnp.einsum('bhqd,bhkd->bhqk', Q, K) / jnp.sqrt(jnp.float32(D_K))
        keep = (mask != 0)[:, None, None, :]
        scores = jnp.where(keep, scores, NEG)
        attn = jax.nn.softmax(scores, axis=-1)
        x = jnp.einsum('bhqk,bhkd->bhqd', attn, V)
        x = x.transpose(0, 2, 1, 3).reshape(B, -1, H * D_K)
        return x @ w_o.T

    def _L0_ffn_ref(hidden_states, gate_weight, e_bias, gate_proj, up_proj, down_proj):
        import jax, jax.numpy as jnp
        import numpy as np
        TOP_K = 4
        N_GROUP = 4
        TOPK_GROUP = 2
        ROUTED_SCALING = 1.0

        def _route(x_flat, gate_weight, e_bias):
            T = x_flat.shape[0]
            E = gate_weight.shape[0]
            logits = jnp.einsum('th,eh->te', x_flat, gate_weight)
            scores = jax.nn.sigmoid(logits)
            scores_for_choice = scores + e_bias[None, :]
            grp = scores_for_choice.reshape(T, N_GROUP, E // N_GROUP)
            top2, _ = jax.lax.top_k(grp, 2)
            group_scores = top2.sum(axis=-1)
            _, group_idx = jax.lax.top_k(group_scores, TOPK_GROUP)
            group_mask = jax.nn.one_hot(group_idx, N_GROUP, dtype=scores.dtype).sum(axis=1)
            score_mask = jnp.repeat(group_mask, E // N_GROUP, axis=1)
            tmp_scores = jnp.where(score_mask > 0, scores_for_choice, 0.0)
            _, topk_idx = jax.lax.top_k(tmp_scores, TOP_K)
            topk_weight = jnp.take_along_axis(scores, topk_idx, axis=1)
            denom = topk_weight.sum(axis=-1, keepdims=True) + 1e-20
            topk_weight = topk_weight / denom * ROUTED_SCALING
            return (topk_idx, topk_weight)
        B, S, H = hidden_states.shape
        E = gate_proj.shape[0]
        x = hidden_states.reshape(-1, H).astype(jnp.float32)
        topk_idx, topk_weight = _route(x, gate_weight, e_bias)
        combine = (jax.nn.one_hot(topk_idx, E, dtype=x.dtype) * topk_weight[..., None]).sum(axis=1)
        g = jnp.einsum('th,eih->tei', x, gate_proj)
        u = jnp.einsum('th,eih->tei', x, up_proj)
        act = jax.nn.silu(g) * u
        expert_out = jnp.einsum('tei,ehi->teh', act, down_proj)
        y = jnp.einsum('teh,te->th', expert_out, combine)
        return y.reshape(B, S, H)

    def _L1_attn_ref(in_features, q_proj_weight, k_proj_weight, v_proj_weight, o_proj_weight):
        import jax, jax.numpy as jnp
        import numpy as np
        from math import sqrt
        D_MODEL = 128
        NUM_HEADS = 16
        MASK_VAL = -100000000.0

        def _proj_heads(x, w, h):
            d = w.shape[0] // h
            w = w.reshape(h, d, w.shape[1])
            return jnp.einsum('bsi,hdi->bhsd', x, w)
        h = NUM_HEADS
        b, s, _ = in_features.shape
        q = _proj_heads(in_features, q_proj_weight, h)
        k = _proj_heads(in_features, k_proj_weight, h)
        v = _proj_heads(in_features, v_proj_weight, h)
        d_k = q.shape[-1]
        mask = jnp.triu(jnp.full((s, s), MASK_VAL, dtype=q.dtype), k=1)[None, None]
        scores = jnp.einsum('bhqd,bhkd->bhqk', q, k) / sqrt(d_k) + mask
        attn = jax.nn.softmax(scores, axis=-1)
        out = jnp.einsum('bhqk,bhkd->bhqd', attn, v)
        out = out.transpose(0, 2, 1, 3).reshape(b, s, -1)
        return jnp.einsum('bsv,mv->bsm', out, o_proj_weight)

    def _L1_xattn_ref(q, kv, Wq, Wkv, Wc):
        import jax, jax.numpy as jnp
        import numpy as np
        N_HEAD = 16
        b, l, d = q.shape
        h = N_HEAD
        dh = d // h
        qp = jnp.einsum('bld,ed->ble', q, Wq)
        scores = jnp.einsum('bld,bmd->blm', qp, kv)
        idx = jnp.argmax(scores, axis=-1)
        mem = jnp.take_along_axis(kv, idx[..., None], axis=1)
        mkv = jnp.einsum('bld,ed->ble', mem, Wkv)
        mk, mv = jnp.split(mkv, 2, axis=-1)
        qh = qp.reshape(b, l, h, dh).transpose(0, 2, 1, 3)
        scale = 1.0 / np.sqrt(dh).astype(np.float32)
        logits = jnp.einsum('bhld,bmd->bhlm', qh, mk) * scale
        attn = jax.nn.softmax(logits, axis=-1)
        out = jnp.einsum('bhlm,bmd->bhld', attn, mv)
        out = out.transpose(0, 2, 1, 3).reshape(b, l, d)
        return jnp.einsum('bld,ed->ble', out, Wc)

    def _L1_ffn_ref(x, ln_g, ln_b, attn_w, attn_b, gate_w, w1, b1, w2, b2, next_w, next_b):
        import jax, jax.numpy as jnp
        import numpy as np
        MICRO_BATCHES = 2
        TOP_K = 2
        LN_EPS = 1e-05
        B, S, D = (4, 512, 128)
        E = 8
        DFF = 4 * D

        def _layernorm(x, g, b):
            mu = jnp.mean(x, axis=-1, keepdims=True)
            var = jnp.mean(jnp.square(x - mu), axis=-1, keepdims=True)
            return (x - mu) * jax.lax.rsqrt(var + LN_EPS) * g + b
        Bx, Sx, Dx = x.shape
        N = Bx * Sx
        x_flat = x.reshape(N, Dx)
        x_attn = _layernorm(x_flat, ln_g, ln_b) @ attn_w + attn_b + x_flat
        logits = x_attn @ gate_w
        _ = jax.lax.top_k(logits, TOP_K)
        tpe = N // (MICRO_BATCHES * E)
        g = x_attn.reshape(MICRO_BATCHES, E, tpe, Dx)
        h = jax.nn.gelu(jnp.einsum('metd,edf->metf', g, w1) + b1[None, :, None, :], approximate=False)
        y = jnp.einsum('metf,efd->metd', h, w2) + b2[None, :, None, :]
        out = jax.nn.gelu(y @ next_w + next_b, approximate=False)
        return out.reshape(Bx, Sx, Dx)

    def _L2_attn_ref(x, wq1, wk1, wq2, wk2, wv, ln_gamma, ln_beta, lamb):
        import jax, jax.numpy as jnp
        import numpy as np
        EPS = 1e-05
        B, T, C = x.shape
        H, _, hs = wq1.shape
        inv_sqrt_d = jnp.asarray(hs, x.dtype) ** (-0.5)
        q1 = jnp.einsum('btc,hcd->bhtd', x, wq1)
        k1 = jnp.einsum('btc,hcd->bhtd', x, wk1)
        q2 = jnp.einsum('btc,hcd->bhtd', x, wq2)
        k2 = jnp.einsum('btc,hcd->bhtd', x, wk2)
        v = jnp.einsum('btc,hcd->bhtd', x, wv)
        w1 = jax.nn.softmax(jnp.einsum('bhtd,bhsd->bhts', q1, k1) * inv_sqrt_d, axis=-1)
        w2 = jax.nn.softmax(jnp.einsum('bhtd,bhsd->bhts', q2, k2) * inv_sqrt_d, axis=-1)
        wei = w1 - lamb * w2
        out = jnp.einsum('bhts,bhsd->bhtd', wei, v)
        out = out.transpose(0, 2, 1, 3).reshape(B, T, H * hs)
        mu = out.mean(axis=-1, keepdims=True)
        var = out.var(axis=-1, keepdims=True)
        out = (out - mu) * jax.lax.rsqrt(var + EPS) * ln_gamma + ln_beta
        return (1.0 - lamb) * out

    def _L2_xattn_ref(x, y, mask, W_kv, b_kv, W_q, b_q, W_o, b_o):
        import jax, jax.numpy as jnp
        import numpy as np
        B, NKV, NQ, D, H = (4, 256, 128, 128, 16)
        HD = D // H
        b, nkv, _ = x.shape
        nq = y.shape[1]
        kv = x @ W_kv + b_kv
        q = y @ W_q + b_q
        kv = kv.reshape(b, nkv, H, 2 * HD).transpose(0, 2, 1, 3)
        q = q.reshape(b, nq, H, HD).transpose(0, 2, 1, 3)
        k, v = (kv[..., :HD], kv[..., HD:])
        scores = jnp.einsum('bhqd,bhkd->bhqk', q, k) / jnp.sqrt(jnp.float32(HD))
        scores = jnp.where(mask[:, None, :, :] == 0, jnp.float32(-1e+20), scores)
        attn = jax.nn.softmax(scores, axis=-1)
        vals = jnp.einsum('bhqk,bhkd->bhqd', attn, v)
        vals = vals.transpose(0, 2, 1, 3).reshape(b, nq, D)
        return vals @ W_o + b_o

    def _L2_ffn_ref(hidden_states, gate_w, shared_gate_w, shared_gate_up_w, shared_down_w, expert_gate_up_w, expert_down_w):
        import jax, jax.numpy as jnp
        import numpy as np
        TOP_K = 8
        CAPACITY = 64

        def _silu(x):
            return x * jax.nn.sigmoid(x)
        B, S, H = hidden_states.shape
        x = hidden_states.reshape(-1, H)
        T = x.shape[0]
        E = gate_w.shape[1]
        Is = shared_gate_up_w.shape[1] // 2
        I = expert_gate_up_w.shape[2] // 2
        gu = x @ shared_gate_up_w
        shared = _silu(gu[:, :Is]) * gu[:, Is:] @ shared_down_w
        shared = shared * jax.nn.sigmoid(x @ shared_gate_w)
        logits = x @ gate_w
        probs = jax.nn.softmax(logits.astype(jnp.float32), axis=-1)
        w, idx = jax.lax.top_k(probs, TOP_K)
        w = (w / jnp.sum(w, axis=-1, keepdims=True)).astype(x.dtype)
        e_flat = idx.reshape(-1)
        w_flat = w.reshape(-1)
        A = e_flat.shape[0]
        tok = jnp.arange(A) // TOP_K
        onehot = jax.nn.one_hot(e_flat, E, dtype=jnp.int32)
        pos = jnp.take_along_axis(jnp.cumsum(onehot, axis=0) - 1, e_flat[:, None], axis=1)[:, 0]
        slot = jnp.minimum(pos, CAPACITY)
        buf = jnp.zeros((E, CAPACITY + 1, H), x.dtype).at[e_flat, slot].set(x[tok])
        gu_e = jnp.einsum('ech,ehf->ecf', buf, expert_gate_up_w)
        act = _silu(gu_e[..., :I]) * gu_e[..., I:]
        out_e = jnp.einsum('eci,eih->ech', act, expert_down_w)
        y = out_e[e_flat, slot] * w_flat[:, None]
        y = jnp.where((pos < CAPACITY)[:, None], y, jnp.zeros_like(y))
        y = y.reshape(T, TOP_K, H).sum(axis=1)
        return (y + shared).reshape(B, S, H)

    def _L3_attn_ref(x, Wqkv, bqkv, Wproj, bproj, scale):
        import jax, jax.numpy as jnp
        import numpy as np
        N_EMBD = 128
        N_HEAD = 16
        HEAD_SIZE = N_EMBD // N_HEAD
        B, T = (8, 512)
        EPS = 0.001
        Bsz, Tlen, C = x.shape
        H, D = (N_HEAD, HEAD_SIZE)
        qkv = jnp.einsum('btc,ec->bte', x, Wqkv) + bqkv
        q, k, v = jnp.split(qkv, 3, axis=-1)
        q = q.reshape(Bsz, Tlen, H, D) * scale
        k = k.reshape(Bsz, Tlen, H, D) * scale
        v = v.reshape(Bsz, Tlen, H, D)
        q = jax.nn.elu(q) + 1.0
        k = jax.nn.elu(k) + 1.0
        kv = k * v
        k_cumsum = jnp.cumsum(k, axis=1)
        kv_cumsum = jnp.cumsum(kv, axis=1)
        denom = jnp.einsum('bthd,bthd->bth', q, k_cumsum)
        denom = jnp.clip(denom, EPS, None)[..., None]
        y = q * kv_cumsum / denom
        y = y.reshape(Bsz, Tlen, C)
        return jnp.einsum('btc,ec->bte', y, Wproj) + bproj

    def _L3_xattn_ref(x, latents, mask, ln_x_g, ln_x_b, ln_l_g, ln_l_b, q_gamma, k_gamma, W_q, W_kv, W_out, b_out):
        import jax, jax.numpy as jnp
        import numpy as np
        DIM = 128
        DIM_LATENT = 128
        DIM_HEAD = 64
        INNER = max(DIM, DIM_LATENT)
        HEADS = INNER // DIM_HEAD
        SCALE = DIM_HEAD ** (-0.5)
        LN_EPS = 1e-05
        RMS_EPS = 1e-08

        def layernorm(x, g, b):
            mu = jnp.mean(x, axis=-1, keepdims=True)
            var = jnp.mean(jnp.square(x - mu), axis=-1, keepdims=True)
            return (x - mu) * jax.lax.rsqrt(var + LN_EPS) * g + b

        def rmsnorm(x, gamma):
            n = jnp.linalg.norm(x, axis=-1, keepdims=True) * x.shape[-1] ** (-0.5)
            return x / jnp.maximum(n, RMS_EPS) * gamma
        b, n, _ = x.shape
        nl = latents.shape[1]
        xn = layernorm(x, ln_x_g, ln_x_b)
        ln = layernorm(latents, ln_l_g, ln_l_b)
        q = ln @ W_q
        kv = jnp.concatenate([xn @ W_kv, ln @ W_kv], axis=1)
        k, v = (kv[..., :INNER], kv[..., INNER:])
        to_heads = lambda t: t.reshape(t.shape[0], t.shape[1], HEADS, DIM_HEAD).transpose(0, 2, 1, 3)
        q, k, v = (to_heads(q), to_heads(k), to_heads(v))
        qn = rmsnorm(q, q_gamma) * SCALE
        kn = rmsnorm(k, k_gamma)
        sim = jnp.einsum('bhid,bhjd->bhij', qn, kn)
        full_mask = jnp.pad(mask, ((0, 0), (0, nl)), constant_values=True)
        neg = -jnp.finfo(sim.dtype).max
        sim = jnp.where(full_mask[:, None, None, :], sim, neg)
        attn = jax.nn.softmax(sim.astype(jnp.float32), axis=-1).astype(sim.dtype)
        out = jnp.einsum('bhij,bhjd->bhid', attn, v)
        out = out.transpose(0, 2, 1, 3).reshape(b, nl, INNER)
        return out @ W_out + b_out

    def _L3_ffn_ref(x, Wqkv, q_scale, k_scale, Wo, ln_g, ln_b, W1, b1, W2, b2):
        import jax, jax.numpy as jnp
        import numpy as np
        DIM = 128
        DEPTH = 6
        HEADS = 16
        DIM_HEAD = 64
        WINDOW = 32
        INNER = HEADS * DIM_HEAD
        DIM_INNER = int(DIM * 4 * 2 / 3)
        QK_SCALE = 8.0

        def shift_tokens(t):
            a, s = jnp.split(t, 2, -1)
            s = jnp.pad(s, ((0, 0), (1, 0), (0, 0)))[:, :-1]
            return jnp.concatenate([a, s], -1)

        def l2norm(t):
            return t / jnp.maximum(jnp.linalg.norm(t, axis=-1, keepdims=True), 1e-12)

        def rotate_half(x):
            x1, x2 = jnp.split(x, 2, -1)
            return jnp.concatenate([-x2, x1], -1)

        def rotary_tables(n):
            half = jnp.arange(0, DIM_HEAD, 2, dtype=jnp.float32)
            inv_freq = 1.0 / 10000.0 ** (half / DIM_HEAD)
            t = jnp.arange(n, dtype=jnp.float32)
            freqs = t[:, None] * inv_freq[None, :]
            freqs = jnp.concatenate([freqs, freqs], -1)
            base_scale = (half + 0.4 * DIM_HEAD) / (1.4 * DIM_HEAD)
            power = (t - n // 2) / (WINDOW // 2)
            scale = base_scale[None, :] ** power[:, None]
            scale = jnp.concatenate([scale, scale], -1)
            return (freqs, scale)

        def local_attention(q, k, v):
            b, h, n, d = q.shape
            w = WINDOW
            nw = n // w
            bq = q.reshape(b, h, nw, w, d)
            bk = k.reshape(b, h, nw, w, d)
            bv = v.reshape(b, h, nw, w, d)

            def look(t):
                p = jnp.pad(t, ((0, 0), (0, 0), (1, 0), (0, 0), (0, 0)))
                return jnp.concatenate([p[:, :, :nw], p[:, :, 1:]], axis=3)
            bk2, bv2 = (look(bk), look(bv))
            seq = jnp.arange(n).reshape(nw, w)
            seq_p = jnp.pad(seq, ((1, 0), (0, 0)), constant_values=-1)
            jt = jnp.concatenate([seq_p[:nw], seq_p[1:]], axis=1)
            it = seq[:, :, None]
            jb = jt[:, None, :]
            mask = (it < jb) | (it > jb + w) | (jb == -1)
            sim = jnp.einsum('bhwie,bhwje->bhwij', bq, bk2) * QK_SCALE
            sim = jnp.where(mask, -jnp.finfo(sim.dtype).max, sim)
            attn = jax.nn.softmax(sim, -1)
            out = jnp.einsum('bhwij,bhwje->bhwie', attn, bv2)
            return out.reshape(b, h, n, d)

        def attn_layer(x, Wqkv, qs, ksc, Wo):
            b, n, _ = x.shape
            qkv = x @ Wqkv
            q, k, v = jnp.split(qkv, 3, -1)
            sh = lambda t: t.reshape(b, n, HEADS, DIM_HEAD).transpose(0, 2, 1, 3)
            q, k, v = (sh(q), sh(k), sh(v))
            q = l2norm(q) * qs
            k = l2norm(k) * ksc
            freqs, scale = rotary_tables(n)
            cos, sin = (jnp.cos(freqs), jnp.sin(freqs))
            q = q * cos * scale + rotate_half(q) * sin * scale
            inv = 1.0 / scale
            k = k * cos * inv + rotate_half(k) * sin * inv
            out = local_attention(q, k, v)
            out = out.transpose(0, 2, 1, 3).reshape(b, n, INNER)
            return out @ Wo

        def ffn_layer(x, g, bln, W1, b1, W2, b2):
            mu = x.mean(-1, keepdims=True)
            var = ((x - mu) ** 2).mean(-1, keepdims=True)
            xn = (x - mu) / jnp.sqrt(var + 1e-05) * g + bln
            hg = xn @ W1 + b1
            a, gate = jnp.split(hg, 2, -1)
            return a * jax.nn.gelu(gate, approximate=False) @ W2 + b2
        for i in range(DEPTH):
            x = attn_layer(shift_tokens(x), Wqkv[i], q_scale[i], k_scale[i], Wo[i]) + x
            x = ffn_layer(shift_tokens(x), ln_g[i], ln_b[i], W1[i], b1[i], W2[i], b2[i]) + x
        return x
    x = _layernorm(x + _L0_attn_ref(x, L0_attn_Wq, L0_attn_Wk, L0_attn_Wv), axis=-1)
    x = _layernorm(x + _L0_xattn_ref(x, ctx_1024, ctx_1024, mask_BxS2_if1, L0_xattn_w_q, L0_xattn_w_k, L0_xattn_w_v, L0_xattn_w_o), axis=-1)
    x = _layernorm(x + _L0_ffn_ref(x, L0_ffn_gate_weight, L0_ffn_e_bias, L0_ffn_gate_proj, L0_ffn_up_proj, L0_ffn_down_proj), axis=-1)
    x = _layernorm(x + _L1_attn_ref(x, L1_attn_q_proj_weight, L1_attn_k_proj_weight, L1_attn_v_proj_weight, L1_attn_o_proj_weight), axis=-1)
    x = _layernorm(x + _L1_xattn_ref(x, ctx_1024, L1_xattn_Wq, L1_xattn_Wkv, L1_xattn_Wc), axis=-1)
    x = _layernorm(x + _L1_ffn_ref(x, L1_ffn_ln_g, L1_ffn_ln_b, L1_ffn_attn_w, L1_ffn_attn_b, L1_ffn_gate_w, L1_ffn_w1, L1_ffn_b1, L1_ffn_w2, L1_ffn_b2, L1_ffn_next_w, L1_ffn_next_b), axis=-1)
    x = _layernorm(x + _L2_attn_ref(x, L2_attn_wq1, L2_attn_wk1, L2_attn_wq2, L2_attn_wk2, L2_attn_wv, L2_attn_ln_gamma, L2_attn_ln_beta, L2_attn_lamb), axis=-1)
    x = _layernorm(x + _L2_xattn_ref(ctx_1024, x, mask_BxSxS2_ik0, L2_xattn_W_kv, L2_xattn_b_kv, L2_xattn_W_q, L2_xattn_b_q, L2_xattn_W_o, L2_xattn_b_o), axis=-1)
    x = _layernorm(x + _L2_ffn_ref(x, L2_ffn_gate_w, L2_ffn_shared_gate_w, L2_ffn_shared_gate_up_w, L2_ffn_shared_down_w, L2_ffn_expert_gate_up_w, L2_ffn_expert_down_w), axis=-1)
    x = _layernorm(x + _L3_attn_ref(x, L3_attn_Wqkv, L3_attn_bqkv, L3_attn_Wproj, L3_attn_bproj, L3_attn_scale), axis=-1)
    x = _layernorm(x + _L3_xattn_ref(ctx_1024, x, mask_BxS2_bk0, L3_xattn_ln_x_g, L3_xattn_ln_x_b, L3_xattn_ln_l_g, L3_xattn_ln_l_b, L3_xattn_q_gamma, L3_xattn_k_gamma, L3_xattn_W_q, L3_xattn_W_kv, L3_xattn_W_out, L3_xattn_b_out), axis=-1)
    x = _layernorm(x + _L3_ffn_ref(x, L3_ffn_Wqkv, L3_ffn_q_scale, L3_ffn_k_scale, L3_ffn_Wo, L3_ffn_ln_g, L3_ffn_ln_b, L3_ffn_W1, L3_ffn_b1, L3_ffn_W2, L3_ffn_b2), axis=-1)
    return x

_drawn_inputs = setup_inputs


def setup_inputs(seed=0):
    import zlib

    import numpy as np

    out = dict(_drawn_inputs(seed))
    spreads = {'L0_ffn_e_bias': (0.0, 0.8),
     'L1_ffn_ln_g': (1.0, 0.2),
     'L1_ffn_ln_b': (0.0, 0.1),
     'L1_ffn_attn_b': (0.0, 0.1),
     'L1_ffn_b1': (0.0, 0.1),
     'L1_ffn_b2': (0.0, 0.1),
     'L1_ffn_next_b': (0.0, 0.1),
     'L2_attn_ln_gamma': (1.0, 0.2),
     'L2_attn_ln_beta': (0.0, 0.338),
     'L2_xattn_b_kv': (0.0, 0.276),
     'L2_xattn_b_q': (0.0, 0.8),
     'L2_xattn_b_o': (0.0, 0.1),
     'L3_attn_bqkv': (0.0, 0.8),
     'L3_attn_bproj': (0.0, 0.1),
     'L3_xattn_ln_x_g': (1.0, 0.6),
     'L3_xattn_ln_x_b': (0.0, 0.8),
     'L3_xattn_ln_l_g': (1.0, 0.2),
     'L3_xattn_ln_l_b': (0.0, 0.1),
     'L3_xattn_q_gamma': (1.0, 0.6),
     'L3_xattn_k_gamma': (1.0, 0.6),
     'L3_xattn_b_out': (0.0, 0.1),
     'L3_ffn_q_scale': (1.0, 0.6),
     'L3_ffn_k_scale': (1.0, 0.6),
     'L3_ffn_ln_g': (1.0, 0.6),
     'L3_ffn_ln_b': (0.0, 0.8),
     'L3_ffn_b1': (0.0, 0.8),
     'L3_ffn_b2': (0.0, 0.1)}
    factors = {'L0_ffn_gate_weight': 8.0,
     'L0_ffn_gate_proj': 8.0,
     'L0_ffn_up_proj': 8.0,
     'L0_ffn_down_proj': 8.0,
     'L2_xattn_W_q': 8.0,
     'L2_ffn_gate_w': 5.948,
     'L2_ffn_shared_gate_w': 2.918,
     'L2_ffn_expert_gate_up_w': 5.679,
     'L2_ffn_expert_down_w': 5.668,
     'L3_attn_Wqkv': 8.0,
     'L3_attn_Wproj': 8.0,
     'L3_ffn_W1': 3.79,
     'L3_ffn_W2': 3.742}
    for name, (base, spread) in spreads.items():
        noise = np.random.default_rng([zlib.crc32(name.encode()), seed]).standard_normal(out[name].shape)
        drawn = base * np.exp(spread * noise) if base else spread * noise
        out[name] = jnp.asarray(drawn.astype(out[name].dtype))
    for name, factor in factors.items():
        out[name] = (out[name] * factor).astype(out[name].dtype)
    return out
```

```python
from contextlib import ExitStack

import concourse.bass as bass
from concourse import mybir

F32 = mybir.dt.float32
BF16 = mybir.dt.bfloat16
I32 = mybir.dt.int32
U32 = mybir.dt.uint32
ALU = mybir.AluOpType
ACT = mybir.ActivationFunctionType
AX = mybir.AxisListType

P = 128
B, S, D = 4, 512, 128
CTX = 154
T = B * S
QT = S // P
NT = T // P
WINDOW = 32
H, DH = 16, 8
PAIRS = H // 2
EPS = 1e-5
MASKED = -1e20
KT_CTX = ((0, P), (P, CTX - P))
KT_SELF = tuple((P * i, P) for i in range(QT))
STAGES = tuple(range(12))

Q_PIECES = (0, 0, 1, 1, 0, 2)
K_PIECES = (0, 1, 0, 1, 2, 0)
MAX_ROW = DH * len(Q_PIECES)
KEY_BIAS_ROW = MAX_ROW + 3


def ds(start, size):
    return bass.ds(start, size)


_USED = {}


def room(nc, stack):
    def sbuf(name, shape, dtype=F32):
        _USED[name] = n = _USED.get(name, 0) + 1
        return stack.enter_context(nc.sbuf_tensor(f"{name}_{n}", shape, dtype))

    return sbuf


def signals(nc, stack, *names):
    handles = {}
    for name in (*names, "held"):
        _USED[name] = n = _USED.get(name, 0) + 1
        handles[name] = stack.enter_context(nc.semaphore(f"{name}_{n}"))
    return handles


def clear(nc, s):
    with nc.Block() as block:
        @block.sync
        def _(sp):
            for handle in s.values():
                sp.sem_clear(handle)


def hold(engine, s, sem, value):
    engine.wait_ge(sem, value)
    engine.sem_inc(s["held"], 1)


class Chain:

    def __init__(self, engine, sem, before=0):
        self.engine, self.sem, self.before, self.n = engine, sem, before, 0

    def step(self, instruction):
        self.n += 1
        instruction.then_inc(self.sem, 1)
        self.engine.wait_ge(self.sem, self.before + self.n)


class Chip:
    pass


def open_chip(nc, stack):
    g = Chip()

    sbuf = room(nc, stack)

    g.x = sbuf("x_tokens", [P, NT, D])
    g.xT = sbuf("x_transposed", [P, T])
    g.ctxT = sbuf("ctx_transposed", [P, B * CTX])
    g.ident = sbuf("identity", [P, P])
    g.ident_bf = sbuf("identity_bf", [P, P], BF16)
    g.power = sbuf("minus_half", [P, 16])
    g.warm = sbuf("warm", [P, 1])
    g.zero = sbuf("zero_column", [P, 1])
    g.ones = sbuf("ones_row", [1, S])
    g.select_q = sbuf("select_q", [P, 3, PAIRS * P], BF16)
    g.select_k = sbuf("select_k", [P, 3, PAIRS * P], BF16)
    g.ones_pattern = sbuf("ones_pattern", [1, P], BF16)
    g.max_pattern = sbuf("max_pattern", [6, P], BF16)
    g.ones_bf = sbuf("ones_bf", [1, S], BF16)
    g.causal_q = sbuf("causal_q", [P, P], BF16)
    g.causal_k = sbuf("causal_k", [P, P], BF16)
    g.band = sbuf("local_band", [P, 2, 2, WINDOW + P], BF16)
    g.cast_loaded = stack.enter_context(nc.semaphore("cast_loaded"))
    g.bank = [stack.enter_context(nc.psum_tensor(f"bank{i}", [P, S], F32)) for i in range(8)]
    return g


def load_chip(nc, g, io):
    with ExitStack() as stack:
        s = signals(nc, stack, "loaded", "cast_done", "filled")
        with nc.Block() as block:
            @block.sync
            def _(sp):
                sp.dma_start(g.x[:, :, :], io["x"].rearrange("b (t p) d -> p (b t) d", p=P)).then_inc(s["loaded"], 16)
                sp.dma_start(g.xT[:, :], io["xT"]).then_inc(s["loaded"], 16)
                sp.dma_start(g.ctxT[:, :], io["ctxT"]).then_inc(s["loaded"], 16)
                sp.dma_start(g.ident[:, :], io["c_ident"]).then_inc(s["loaded"], 16)
                sp.wait_ge(s["loaded"], 64)

            @block.gpsimd
            def _(pool):
                for dst, name in ((g.select_q[:, :, :], "c_select_q"), (g.select_k[:, :, :], "c_select_k"),
                                  (g.ones_pattern[:, :], "c_ones_pattern"), (g.max_pattern[:, :], "c_max_pattern"),
                                  (g.causal_q[:, :], "c_causal_q"), (g.causal_k[:, :], "c_causal_k"),
                                  (g.band[:, :, :, :], "c_band")):
                    pool.dma_start(dst, io[name]).then_inc(g.cast_loaded, 16)
                pool.wait_ge(g.cast_loaded, 112)

            @block.vector
            def _(dve):
                nc.vector.memset(g.ones_bf[:, :], 1.0).then_inc(s["filled"], 1)
                nc.vector.memset(g.power[:, :], -0.5).then_inc(s["filled"], 1)
                nc.vector.memset(g.zero[:, :], 0.0).then_inc(s["filled"], 1)
                nc.vector.memset(g.ones[:, :], 1.0).then_inc(s["filled"], 1)
                dve.wait_ge(s["loaded"], 64)
                nc.vector.tensor_copy(g.ident_bf[:, :], g.ident[:, :]).then_inc(s["cast_done"], 1)

            @block.scalar
            def _(act):
                act.wait_ge(s["filled"], 4)
                nc.scalar.activation(g.warm[:, :], g.zero[:, :], ACT.Exp).then_inc(s["filled"], 1)
        clear(nc, s)


def finish(nc, g, source, y, w_out=None, bias_row=None):
    moved = source != "tokens"
    with ExitStack() as stack:
        sbuf = room(nc, stack)

        y_now = sbuf("fin_y", [P, 2, S])
        yT = sbuf("fin_yT", [P, 2, S])
        z = sbuf("fin_z", [P, 2, QT, D])
        stats = sbuf("fin_stats", [P, 2, QT, 6])
        moments = sbuf("fin_moments", [P, 2, QT, 2])
        shifted = sbuf("fin_shifted", [P, 2, QT])
        rstd = sbuf("fin_rstd", [P, 2, QT])
        new = sbuf("fin_new", [P, 2, QT, D])
        s = signals(nc, stack, "y_copied", "yT_ready", "yT_evacuated", "f_ready", "z_ready", "stats_ready",
                    "moments_ready", "shift_ready", "rstd_ready", "new_ready", "new_stored", "newT_ready",
                    "newT_stored")

        with nc.Block() as block:
            @block.gpsimd
            def _(pool):
                with pool.Fori(0, B // 2) as i:
                    for u in range(2):
                        b = i * 2 + u
                        if moved:
                            src = y[:, ds(b * S, S)] if source == "transposed" else y[:, ds(b * QT, QT), :]
                            dst = y_now[:, u, :]
                            if source == "heads":
                                dst = dst.rearrange("p (t d) -> p t d", t=QT)
                            nc.gpsimd.tensor_copy(dst, src).then_inc(s["y_copied"], 1)
                    for u in range(2):
                        b = i * 2 + u
                        hold(pool, s, s["moments_ready"], b * QT + QT)
                        nc.gpsimd.tensor_scalar(shifted[:, u, :], moments[:, u, :, 1], EPS, None,
                                                ALU.add).then_inc(s["shift_ready"], 1)
                        hold(pool, s, s["shift_ready"], b + 1)
                        nc.gpsimd.tensor_tensor(rstd[:, u, :], shifted[:, u, :], g.power[:, 0:QT],
                                                ALU.pow).then_inc(s["rstd_ready"], 1)
                    for u in range(2):
                        b = i * 2 + u
                        hold(pool, s, s["new_ready"], b * QT + QT)
                        nc.gpsimd.tensor_copy(g.x[:, ds(b * QT, QT), :], new[:, u]).then_inc(s["new_stored"], 1)

            @block.tensor
            def _(pe):
                with pe.Fori(0, B // 2) as i:
                    for u in range(2):
                        b = i * 2 + u
                        if source == "heads":
                            pe.wait_ge(s["y_copied"], b + 1)
                            for t in range(QT):
                                ins = nc.tensor.transpose(g.bank[u][:, t * P:(t + 1) * P],
                                                          y_now[:, u, t * P:(t + 1) * P], g.ident[:, :])
                            ins.then_inc(s["yT_ready"], 1)
                            pe.wait_ge(s["yT_evacuated"], b + 1)
                            for t in range(QT):
                                ins = nc.tensor.matmul(g.bank[2 + u][:, t * P:(t + 1) * P],
                                                       yT[:, u, t * P:(t + 1) * P], w_out[:, :],
                                                       start=True, stop=bias_row is None)
                                if bias_row is not None:
                                    ins = nc.tensor.matmul(g.bank[2 + u][:, t * P:(t + 1) * P],
                                                           g.ones[0:1, 0:P], bias_row[0:1, :],
                                                           start=False, stop=True)
                            ins.then_inc(s["f_ready"], 1)
                        if source == "transposed":
                            pe.wait_ge(s["y_copied"], b + 1)
                            for t in range(QT):
                                ins = nc.tensor.transpose(g.bank[2 + u][:, t * P:(t + 1) * P],
                                                          y_now[:, u, t * P:(t + 1) * P], g.ident[:, :])
                            ins.then_inc(s["f_ready"], 1)
                    for u in range(2):
                        b = i * 2 + u
                        pe.wait_ge(s["new_ready"], b * QT + QT)
                        for t in range(QT):
                            ins = nc.tensor.transpose(g.bank[4 + u][:, t * P:(t + 1) * P], new[:, u, t, :],
                                                      g.ident[:, :])
                        ins.then_inc(s["newT_ready"], 1)
                    pe.wait_ge(s["newT_stored"], i * 2 + 2)

            @block.scalar
            def _(act):
                with act.Fori(0, B // 2) as i:
                    if source == "heads":
                        for u in range(2):
                            act.wait_ge(s["yT_ready"], i * 2 + u + 1)
                            nc.scalar.activation(yT[:, u, :], g.bank[u][:, :], ACT.Copy).then_inc(s["yT_evacuated"], 1)
                    for u in range(2):
                        b = i * 2 + u
                        act.wait_ge(s["newT_ready"], b + 1)
                        nc.scalar.activation(g.xT[:, ds(b * S, S)], g.bank[4 + u][:, :],
                                             ACT.Copy).then_inc(s["newT_stored"], 1)

            @block.vector
            def _(dve):
                with dve.Fori(0, B // 2) as i:
                    for u in range(2):
                        b = i * 2 + u
                        if moved:
                            dve.wait_ge(s["f_ready"], b + 1)
                            f = g.bank[2 + u][:, :].rearrange("p (t d) -> p t d", t=QT)
                        else:
                            f = y[:, ds(b * QT, QT), :]
                        nc.vector.tensor_tensor(z[:, u], f, g.x[:, ds(b * QT, QT), :], ALU.add).then_inc(s["z_ready"], 1)
                        dve.wait_ge(s["z_ready"], b + 1)
                        for t in range(QT):
                            nc.vector.bn_stats(stats[:, u, t, :], z[:, u, t, :]).then_inc(s["stats_ready"], 1)
                        hold(dve, s, s["stats_ready"], b * QT + QT)
                        for t in range(QT):
                            nc.vector.bn_aggr(moments[:, u, t, :], stats[:, u, t, :]).then_inc(s["moments_ready"], 1)
                    for u in range(2):
                        b = i * 2 + u
                        dve.wait_ge(s["rstd_ready"], b + 1)
                        dve.wait_ge(s["moments_ready"], b * QT + QT)
                        for t in range(QT):
                            nc.vector.tensor_scalar(new[:, u, t, :], z[:, u, t, :], moments[:, u, t, 0:1],
                                                    rstd[:, u, t:t + 1], ALU.subtract, ALU.mult).then_inc(s["new_ready"], 1)
                    dve.wait_ge(s["newT_stored"], i * 2 + 2)
                    dve.wait_ge(s["new_stored"], i * 2 + 2)
        clear(nc, s)


class Projection:

    def __init__(self, w, context, parts, bias=None):
        self.w, self.context, self.parts, self.bias = w, context, parts, bias


class Values:

    def __init__(self, w, context, rows, bias_row=None):
        self.w, self.context, self.rows, self.bias_row = w, context, rows, bias_row


def project(nc, g, projections, values):
    with ExitStack() as stack:
        sbuf = room(nc, stack)

        src = sbuf("proj_src", [P, S])
        src_ctx = sbuf("proj_src_ctx", [P, CTX])
        full = sbuf("proj_full", [P, 2, S])
        rest = sbuf("proj_rest", [P, 2, S])
        n = len(projections)
        s = signals(nc, stack, "src_copied", "product_ready", "full_ready", "first_ready", "rest_ready",
                    "second_ready", "third_ready", "values_ready", "values_stored")
        nk = CTX if values.context else S
        tiles = KT_CTX if values.context else KT_SELF

        with nc.Block() as block:
            @block.gpsimd
            def _(pool):
                with pool.Fori(0, B) as b:
                    nc.gpsimd.tensor_copy(src[:, :], g.xT[:, ds(b * S, S)]).then_inc(s["src_copied"], 1)
                    nc.gpsimd.tensor_copy(src_ctx[:, :], g.ctxT[:, ds(b * CTX, CTX)]).then_inc(s["src_copied"], 1)
                    hold(pool, s, s["product_ready"], b * n + n)
                    hold(pool, s, s["values_ready"], b + 1)

            @block.tensor
            def _(pe):
                with pe.Fori(0, B) as b:
                    pe.wait_ge(s["src_copied"], b * 2 + 2)
                    for j, job in enumerate(projections):
                        u = j % 2
                        if j >= 2:
                            pe.wait_ge(s["full_ready"], b * n + (j - 1))
                            pe.wait_ge(s["first_ready"], b * n + (j - 1))
                        rhs = src_ctx[:, :] if job.context else src[:, :]
                        nc.tensor.matmul(g.bank[u][:, 0:rhs.shape[1]], job.w[:, :], rhs,
                                         start=True, stop=True).then_inc(s["product_ready"], 1)
                    for t, (first, count) in enumerate(tiles):
                        lhs = (src_ctx if values.context else src)[:, first:first + count]
                        plain = values.bias_row is None
                        ins = nc.tensor.matmul(g.bank[2][0:count, t * P:(t + 1) * P], lhs, values.w[:, :],
                                               start=True, stop=plain)
                        if not plain:
                            ins = nc.tensor.matmul(g.bank[2][0:count, t * P:(t + 1) * P], g.ones[0:1, 0:count],
                                                   values.bias_row[0:1, :], start=False, stop=True)
                    ins.then_inc(s["values_ready"], 1)
                    pe.wait_ge(s["values_stored"], b * len(tiles) + len(tiles))
                    pe.wait_ge(s["full_ready"], b * n + n)
                    pe.wait_ge(s["first_ready"], b * n + n)

            @block.scalar
            def _(act):
                with act.Fori(0, B) as b:
                    for j, job in enumerate(projections):
                        u, k = j % 2, (CTX if job.context else S)
                        bias = g.zero[:, 0:1] if job.bias is None else job.bias[:, 0:1]
                        act.wait_ge(s["product_ready"], b * n + (j + 1))
                        if j >= 2:
                            act.wait_ge(s["rest_ready"], b * n + (j - 1))
                        nc.scalar.activation(full[:, u, 0:k], g.bank[u][:, 0:k], ACT.Identity,
                                             bias=bias).then_inc(s["full_ready"], 1)
                        nc.scalar.activation(job.parts[:, 0, ds(b * k, k)], g.bank[u][:, 0:k], ACT.Identity,
                                             bias=bias).then_inc(s["first_ready"], 1)
                        act.wait_ge(s["rest_ready"], b * n + (j + 1))
                        nc.scalar.activation(job.parts[:, 1, ds(b * k, k)], rest[:, u, 0:k],
                                             ACT.Copy).then_inc(s["second_ready"], 1)

            @block.vector
            def _(dve):
                with dve.Fori(0, B) as b:
                    for j, job in enumerate(projections):
                        u, k = j % 2, (CTX if job.context else S)
                        here = ds(b * k, k)
                        dve.wait_ge(s["full_ready"], b * n + (j + 1))
                        dve.wait_ge(s["first_ready"], b * n + (j + 1))
                        nc.vector.tensor_tensor(rest[:, u, 0:k], full[:, u, 0:k], job.parts[:, 0, here],
                                                ALU.subtract).then_inc(s["rest_ready"], 1)
                        dve.wait_ge(s["second_ready"], b * n + (j + 1))
                        nc.vector.tensor_tensor(job.parts[:, 2, here], rest[:, u, 0:k], job.parts[:, 1, here],
                                                ALU.subtract).then_inc(s["third_ready"], 1)
                        dve.wait_ge(s["third_ready"], b * n + (j + 1))
                    dve.wait_ge(s["values_ready"], b + 1)
                    for t, (first, count) in enumerate(tiles):
                        src_v = g.bank[2][0:count, t * P:(t + 1) * P].rearrange("p (h d) -> p h d", h=H)
                        dst = values.rows[0:count, ds((b * len(tiles) + t) * H, H), 0:DH]
                        nc.vector.tensor_copy(dst, src_v).then_inc(s["values_stored"], 1)
        clear(nc, s)


def attend(nc, g, q_parts, k_parts, rows, out, context, causal=False, key_bias=None, mask=None):
    nk = CTX if context else S
    ktiles = KT_CTX if context else KT_SELF
    direct_steps = [(e, (2 * q, 2 * q + 1)) for e in range(2) for q in range(2)] if context else \
                   [(e, (q,)) for e in range(2) for q in range(QT)]
    turned_steps = [(e, k) for e in range(2) for k in range(len(ktiles))]
    nd, nt = len(direct_steps), len(turned_steps)
    assert nd == nt
    plain = not (causal or mask or key_bias is not None)
    scale = 1.0 / float(DH) ** 0.5

    with ExitStack() as stack:
        sbuf = room(nc, stack)

        q_stack = [sbuf(f"q_stack{u}", [P, S], BF16) for u in range(2)]
        k_stack = [sbuf(f"k_stack{u}", [P, len(ktiles) * P], BF16) for u in range(2)]
        minus_max = sbuf("minus_max", [P, 2, 2, QT])
        max_left = sbuf("max_left", [P, 2, 2, QT])
        max_parts = sbuf("max_parts", [P, 2, 3, 2, QT], BF16)
        max_rows = sbuf("max_rows", [6, S], BF16)
        probs = [sbuf(f"probs{i}", [P, S]) for i in range(4)]
        recip = sbuf("recip", [P, QT, 2])
        s = signals(nc, stack, "stack_ready", "q_stacked", "k_stacked", "direct_ready", "max_done",
                    "first_done", "left_done", "second_done", "third_done", "max_turned", "max_rows_done",
                    "q_max_ready", "q_max_stacked", "turned_ready", "exp_done", "values_done", "recip_done",
                    "out_done", "filled")
        q_bank, k_bank = (g.bank[0], g.bank[1]), g.bank[2]
        d_bank, t_bank, o_bank = (g.bank[3], g.bank[4]), (g.bank[5], g.bank[6]), g.bank[7]
        o_view = o_bank[:, 0:QT * 2 * 16].rearrange("p (q e d) -> p q e d", q=QT, e=2)

        def pe_build(pe, b, a, u, n):
            pe.wait_ge(s["max_rows_done"], n + 1)
            cols = ds(b * S, S)
            for part in range(3):
                nc.tensor.matmul(q_bank[u][:, :], g.select_q[:, part, ds(a * P, P)], q_parts[:, part, cols],
                                 start=(part == 0), stop=(part == 2), skip_group_check=True)
            cols = ds(b * nk, nk)
            for part in range(3):
                nc.tensor.matmul(k_bank[:, 0:nk], g.select_k[:, part, ds(a * P, P)], k_parts[:, part, cols],
                                 start=(part == 0), stop=False, skip_group_check=True)
            ins = nc.tensor.matmul(k_bank[:, 0:nk], g.ones_pattern[0:1, :], g.ones_bf[0:1, 0:nk],
                                   start=False, stop=True, skip_group_check=True)
            ins.then_inc(s["stack_ready"], 1)

        def pe_direct(pe, b, u, n, step):
            e, qs = direct_steps[step]
            rows_e = slice(64 * e, 64 * e + 64)
            if step == 0:
                pe.wait_ge(s["q_stacked"], n + 1)
                pe.wait_ge(s["k_stacked"], n + 1)
            pe.wait_ge(s["max_done"], n * nd + (step + 1))
            bank = d_bank[step % 2]
            for i, q in enumerate(qs):
                keys = (q + 1) * P if causal else nk
                dst = bank[:, i * nk:i * nk + keys]
                ins = nc.tensor.matmul(dst, q_stack[u][rows_e, q * P:(q + 1) * P], k_stack[u][rows_e, 0:keys],
                                       start=True, stop=plain, skip_group_check=True)
                if causal:
                    ins = nc.tensor.matmul(bank[:, q * P:(q + 1) * P], g.ident_bf[:, :], g.causal_q[:, :],
                                           start=False, stop=True, skip_group_check=True)
                if mask:
                    for k, (k0, kn) in enumerate(ktiles):
                        ins = nc.tensor.matmul(bank[:, i * nk + k0:i * nk + k0 + kn],
                                               mask[k][0:kn, ds(b * S + q * P, P)], g.ident_bf[0:kn, 0:kn],
                                               start=False, stop=True, skip_group_check=True)
                if key_bias is not None:
                    ins = nc.tensor.matmul(dst, g.ones_bf[0:1, 0:P], key_bias[0:1, ds(b * len(ktiles) * P, nk)],
                                           start=False, stop=True, skip_group_check=True)
            ins.then_inc(s["direct_ready"], 1)

        def pe_max(pe, u, n):
            pe.wait_ge(s["third_done"], n + 3)
            for q in range(QT):
                lhs = max_parts[:, u, :, :, q].rearrange("p a e -> p (a e)")
                ins = nc.tensor.matmul(k_bank[0:6, q * P:(q + 1) * P], lhs, g.ident_bf[:, :],
                                       start=True, stop=True, skip_group_check=True)
            ins.then_inc(s["max_turned"], 1)
            pe.wait_ge(s["max_rows_done"], n + 2)
            nc.tensor.matmul(q_bank[u][:, :], g.max_pattern[0:6, :], max_rows[0:6, :],
                             start=False, stop=True, skip_group_check=True).then_inc(s["q_max_ready"], 1)

        def pe_turned(pe, b, u, n, step):
            e, k = turned_steps[step]
            k0, kn = ktiles[k]
            q0 = k0 if causal else 0
            rows_e = slice(64 * e, 64 * e + 64)
            if step == 0:
                pe.wait_ge(s["q_max_stacked"], n + 1)
            pe.wait_ge(s["exp_done"], n * nt + (step + 1))
            bank = t_bank[step % 2]
            ins = nc.tensor.matmul(bank[:, q0:S], k_stack[u][rows_e, k0:k0 + P], q_stack[u][rows_e, q0:S],
                                   start=True, stop=plain, skip_group_check=True)
            if causal:
                ins = nc.tensor.matmul(bank[:, q0:q0 + P], g.ident_bf[:, :], g.causal_k[:, :],
                                       start=False, stop=True, skip_group_check=True)
            if mask:
                ins = nc.tensor.matmul(bank[:, :], g.ident_bf[0:kn, :], mask[k][0:kn, ds(b * S, S)],
                                       start=False, stop=True, skip_group_check=True)
            if key_bias is not None:
                ins = nc.tensor.matmul(bank[:, :], key_bias[0:1, ds(b * len(ktiles) * P + k0, P)], g.ones_bf[0:1, :],
                                       start=False, stop=True, skip_group_check=True)
            ins.then_inc(s["turned_ready"], 1)

        def pe_values(pe, b, a, n, step):
            e, k = turned_steps[step]
            k0, kn = ktiles[k]
            if step == 0:
                pe.wait_ge(s["out_done"], n + 1)
            pe.wait_ge(s["exp_done"], n * nt + (step + 3))
            for q in range(k if causal else 0, QT):
                ins = nc.tensor.matmul(o_view[:, q, e, 0:DH + 1], probs[step % 4][0:kn, q * P:(q + 1) * P],
                                       rows[0:kn, ds((b * len(ktiles) + k) * H + a * 2 + e, 1), :],
                                       start=(step == 0 and q == 0), stop=True, skip_group_check=True)
            ins.then_inc(s["values_done"], 1)

        def act_step(act, n, step):
            e, k = turned_steps[step]
            k0, kn = ktiles[k]
            q0 = k0 if causal else 0
            act.wait_ge(s["turned_ready"], n * nt + (step + 1))
            act.wait_ge(s["values_done"], n * nt + (step + 1))
            nc.scalar.activation(probs[step % 4][0:kn, q0:S], t_bank[step % 2][0:kn, q0:S], ACT.Exp,
                                 scale=scale).then_inc(s["exp_done"], 1)

        def act_build(act, u, n):
            act.wait_ge(s["stack_ready"], n + 1)
            nc.scalar.activation(q_stack[u][:, :], q_bank[u][:, :], ACT.Copy).then_inc(s["q_stacked"], 1)

        def act_max(act, u, n):
            act.wait_ge(s["q_max_ready"], n + 1)
            nc.scalar.activation(q_stack[u][:, :], q_bank[u][:, :], ACT.Copy).then_inc(s["q_max_stacked"], 1)

        def dve_build(dve, u, n):
            dve.wait_ge(s["stack_ready"], n + 1)
            nc.vector.tensor_copy(k_stack[u][:, 0:nk], k_bank[:, 0:nk]).then_inc(s["k_stacked"], 1)

        def dve_direct(dve, u, n, step):
            e, qs = direct_steps[step]
            if step == 0:
                dve.wait_ge(s["third_done"], n + 1)
            dve.wait_ge(s["direct_ready"], n * nd + (step + 1))
            keys = (qs[0] + 1) * P if causal else nk
            view = d_bank[step % 2][:, 0:len(qs) * keys].rearrange("p (q k) -> p q k", q=len(qs))
            nc.vector.tensor_reduce(minus_max[:, u, e, qs[0]:qs[0] + len(qs)], view, AX.X, ALU.max,
                                    negate=True).then_inc(s["max_done"], 1)

        def dve_max(dve, u, n):
            dve.wait_ge(s["max_turned"], n + 3)
            nc.vector.tensor_copy(max_rows[0:6, :], k_bank[0:6, :]).then_inc(s["max_rows_done"], 1)

        def dve_out(dve, b, a, n):
            dve.wait_ge(s["values_done"], n * nt + (nt + 4))
            nc.vector.reciprocal(recip[:, :, :], o_view[:, :, :, DH]).then_inc(s["recip_done"], 1)
            dve.wait_ge(s["recip_done"], n + 1)
            dst = out[:, ds(b * QT, QT), ds(a * 2 * DH, 2 * DH)].rearrange("p q (e d) -> p q e d", e=2)
            nc.vector.tensor_tensor(dst, o_view[:, :, :, 0:DH],
                                    recip[:, :, :].unsqueeze(3).to_broadcast([P, QT, 2, DH]),
                                    ALU.mult).then_inc(s["out_done"], 1)

        def pool_max(pool, u, n):
            hold(pool, s, s["max_done"], n * nd + (nd + 2))
            hold(pool, s, s["max_turned"], n + 1)
            m, left, parts = minus_max[:, u], max_left[:, u], max_parts[:, u]
            nc.gpsimd.tensor_copy(parts[:, 0], m).then_inc(s["first_done"], 1)
            hold(pool, s, s["first_done"], n + 1)
            nc.gpsimd.tensor_tensor(left, m, parts[:, 0], ALU.subtract).then_inc(s["left_done"], 1)
            hold(pool, s, s["left_done"], n + 1)
            nc.gpsimd.tensor_copy(parts[:, 1], left).then_inc(s["second_done"], 1)
            hold(pool, s, s["second_done"], n + 1)
            nc.gpsimd.tensor_tensor(parts[:, 2], left, parts[:, 1], ALU.subtract).then_inc(s["third_done"], 1)

        with nc.Block() as block:
            @block.tensor
            def _(pe):
                def both(b, a, u, n, more):
                    pe_max(pe, u, n)
                    if more:
                        pe_build(pe, b, a + 1, 1 - u, n + 1)
                    for step in range(nt):
                        pe_turned(pe, b, u, n, step)
                        if more:
                            pe_direct(pe, b, 1 - u, n + 1, step)
                        if step >= 2:
                            pe_values(pe, b, a, n, step - 2)
                    for step in range(nt - 2, nt):
                        pe_values(pe, b, a, n, step)

                pe.sem_inc(s["max_turned"], 2)
                pe.sem_inc(s["values_done"], 4)
                with pe.Fori(0, B) as b:
                    pe_build(pe, b, 0, 0, b * PAIRS)
                    for step in range(nd):
                        pe_direct(pe, b, 0, b * PAIRS, step)
                    with pe.Fori(0, PAIRS // 2 - 1) as m:
                        both(b, m * 2, 0, b * PAIRS + m * 2, True)
                        both(b, m * 2 + 1, 1, b * PAIRS + m * 2 + 1, True)
                    last = PAIRS - 2
                    both(b, last, 0, b * PAIRS + last, True)
                    both(b, last + 1, 1, b * PAIRS + (last + 1), False)

            @block.scalar
            def _(act):
                def both(b, u, n, more):
                    act_max(act, u, n)
                    if more:
                        act_build(act, 1 - u, n + 1)
                    for step in range(nt):
                        act_step(act, n, step)

                act.sem_inc(s["exp_done"], 2)
                with act.Fori(0, B) as b:
                    act_build(act, 0, b * PAIRS)
                    with act.Fori(0, PAIRS // 2 - 1) as m:
                        both(b, 0, b * PAIRS + m * 2, True)
                        both(b, 1, b * PAIRS + m * 2 + 1, True)
                    last = PAIRS - 2
                    both(b, 0, b * PAIRS + last, True)
                    both(b, 1, b * PAIRS + (last + 1), False)

            @block.gpsimd
            def _(pool):
                pool.sem_inc(s["third_done"], 2)
                with pool.Fori(0, B) as b:
                    with pool.Fori(0, PAIRS // 2) as m:
                        for u in range(2):
                            pool_max(pool, u, b * PAIRS + m * 2 + u)

            @block.vector
            def _(dve):
                def both(b, a, u, n, more):
                    dve_max(dve, u, n)
                    if more:
                        dve_build(dve, 1 - u, n + 1)
                        for step in range(nd):
                            dve_direct(dve, 1 - u, n + 1, step)
                    dve_out(dve, b, a, n)

                dve.sem_inc(s["max_done"], 2)
                dve.sem_inc(s["max_rows_done"], 1)
                dve.sem_inc(s["out_done"], 1)
                if context:
                    for u in range(2):
                        nc.vector.memset(k_stack[u][:, nk:], 0.0).then_inc(s["filled"], 1)
                    dve.wait_ge(s["filled"], 2)
                with dve.Fori(0, B) as b:
                    dve_build(dve, 0, b * PAIRS)
                    for step in range(nd):
                        dve_direct(dve, 0, b * PAIRS, step)
                    with dve.Fori(0, PAIRS // 2 - 1) as m:
                        both(b, m * 2, 0, b * PAIRS + m * 2, True)
                        both(b, m * 2 + 1, 1, b * PAIRS + m * 2 + 1, True)
                    last = PAIRS - 2
                    both(b, last, 0, b * PAIRS + last, True)
                    both(b, last + 1, 1, b * PAIRS + (last + 1), False)
        clear(nc, s)


def load(nc, g, copies, ones=(), zeros=()):
    with ExitStack() as stack:
        s = signals(nc, stack, "loaded", "filled")
        with nc.Block() as block:
            @block.sync
            def _(sp):
                for dst, src in copies:
                    sp.dma_start(dst, src).then_inc(s["loaded"], 16)
                sp.wait_ge(s["loaded"], 16 * len(copies))

            @block.vector
            def _(dve):
                for buffers, value in ((ones, 1.0), (zeros, 0.0)):
                    for dst in buffers:
                        nc.vector.memset(dst, value).then_inc(s["filled"], 1)
        clear(nc, s)


def flat_bias(key_bias):
    return key_bias[:, :, :].rearrange("o b k -> o (b k)")


def context_attention_0(nc, g, io):
    with ExitStack() as stack:
        sbuf = room(nc, stack)

        w = {n: sbuf(f"w_{n}", [P, D]) for n in ("q", "k", "v", "o")}
        q_parts = sbuf("q_parts", [P, 3, T], BF16)
        k_parts = sbuf("k_parts", [P, 3, B * CTX], BF16)
        rows = sbuf("value_rows", [P, B * len(KT_CTX) * H, DH + 1])
        out = sbuf("heads_out", [P, NT, D])
        keep = sbuf("keep", [1, B * CTX], I32)
        key_bias = sbuf("key_bias", [1, B, 2 * P], BF16)
        load(nc, g, [(w[n][:, :], io[f"L0_xattn_w_{n}"]) for n in w] +
             [(keep[:, :], io["mask_BxS2_if1"].rearrange("b s -> (b s)").unsqueeze(0))],
             ones=(rows[:, :, :],), zeros=(key_bias[:, :, :],))
        with ExitStack() as inner:
            s = signals(nc, inner, "biased")
            with nc.Block() as block:
                @block.vector
                def _(dve):
                    nc.vector.tensor_scalar(key_bias[:, :, 0:CTX], keep[:, :].rearrange("o (b k) -> o b k", b=B),
                                            0.0, MASKED, ALU.is_equal, ALU.mult).then_inc(s["biased"], 1)
            clear(nc, s)
        project(nc, g, [Projection(w["q"], False, q_parts), Projection(w["k"], True, k_parts)],
                Values(w["v"], True, rows))
        attend(nc, g, q_parts, k_parts, rows, out, context=True, key_bias=flat_bias(key_bias))
        finish(nc, g, "heads", out, w["o"])


def causal_attention_1(nc, g, io):
    with ExitStack() as stack:
        sbuf = room(nc, stack)

        w = {n: sbuf(f"w_{n}", [P, D]) for n in ("q", "k", "v", "o")}
        q_parts = sbuf("q_parts", [P, 3, T], BF16)
        k_parts = sbuf("k_parts", [P, 3, T], BF16)
        rows = sbuf("value_rows", [P, NT * H, DH + 1])
        out = sbuf("heads_out", [P, NT, D])
        load(nc, g, [(w[n][:, :], io[f"L1_attn_{n}_proj_weight"]) for n in w], ones=(rows[:, :, :],))
        project(nc, g, [Projection(w["q"], False, q_parts), Projection(w["k"], False, k_parts)],
                Values(w["v"], False, rows))
        attend(nc, g, q_parts, k_parts, rows, out, context=False, causal=True)
        finish(nc, g, "heads", out, w["o"])


def remembered_attention_1(nc, g, io):
    with ExitStack() as stack:
        sbuf = room(nc, stack)

        w = {n: sbuf(f"w_{n}", [P, D]) for n in ("q", "k", "v", "o")}
        q_parts = sbuf("q_parts", [P, 3, T], BF16)
        k_parts = sbuf("k_parts", [P, 3, B * CTX], BF16)
        rows = sbuf("value_rows", [P, B * len(KT_CTX) * H, DH + 1])
        out = sbuf("heads_out", [P, NT, D])
        key_bias = sbuf("key_bias", [1, B, 2 * P], BF16)
        taken = sbuf("taken", [P, B * 2])
        iota = sbuf("iota", [P, CTX])
        ones_column = sbuf("ones_column", [P, 1], BF16)
        load(nc, g, [(w["q"][:, :], io["L1_xattn_Wq"]), (w["k"][:, :], io["L1_xattn_Wk16"]),
                     (w["v"][:, :], io["L1_xattn_Wv16"]), (w["o"][:, :], io["L1_xattn_Wc"]),
                     (iota[:, :], io["c_iota"])],
             ones=(rows[:, :, :], ones_column[:, :]), zeros=(key_bias[:, :, :], taken[:, :]))
        project(nc, g, [Projection(w["q"], False, q_parts), Projection(w["k"], True, k_parts)],
                Values(w["v"], True, rows))
        count_best_rows(nc, g, w["q"], iota, ones_column, key_bias, taken)
        with ExitStack() as inner:
            s = signals(nc, inner, "weighted")
            with nc.Block() as block:
                @block.vector
                def _(dve):
                    for i in range(B * 2):
                        n = KT_CTX[i % 2][1]
                        v = rows[0:n, i * H:(i + 1) * H, :]
                        nc.vector.tensor_scalar(v, v, taken[0:n, i:i + 1], None, ALU.mult).then_inc(s["weighted"], 1)
            clear(nc, s)
        attend(nc, g, q_parts, k_parts, rows, out, context=True, key_bias=flat_bias(key_bias))
        finish(nc, g, "heads", out, w["o"])


def count_best_rows(nc, g, w_q, iota, ones_column, key_bias, taken):
    with ExitStack() as stack:
        sbuf = room(nc, stack)

        qT = sbuf("best_qT", [P, S])
        top = sbuf("best_top", [P, QT, 8])
        where = sbuf("best_where", [P, QT, 8], U32)
        at = sbuf("best_at", [P, QT])
        onehot = sbuf("best_onehot", [P, QT, CTX], BF16)
        s = signals(nc, stack, "q_ready", "q_copied", "scores_ready", "top_done", "where_done", "at_done",
                    "onehot_done", "counts_ready", "bias_done", "taken_done")
        with nc.Block() as block:
            @block.tensor
            def _(pe):
                with pe.Fori(0, B) as b:
                    nc.tensor.matmul(g.bank[0][:, :], w_q[:, :], g.xT[:, ds(b * S, S)],
                                     start=True, stop=True).then_inc(s["q_ready"], 1)
                    pe.wait_ge(s["q_copied"], b + 1)
                    for t in range(QT):
                        nc.tensor.matmul(g.bank[1 + t][:, 0:CTX], qT[:, t * P:(t + 1) * P],
                                         g.ctxT[:, ds(b * CTX, CTX)], start=True, stop=True).then_inc(s["scores_ready"], 1)
                    pe.wait_ge(s["onehot_done"], b * QT + QT)
                    for t in range(QT):
                        ins = nc.tensor.matmul(g.bank[5][0:1, 0:CTX], ones_column[:, 0:1], onehot[:, t, :],
                                               start=(t == 0), stop=(t == QT - 1))
                    for k, (k0, kn) in enumerate(KT_CTX):
                        for t in range(QT):
                            ins = nc.tensor.matmul(g.bank[6 + k][0:kn, 0:1], onehot[:, t, k0:k0 + kn],
                                                   ones_column[:, 0:1], start=(t == 0), stop=(t == QT - 1))
                    ins.then_inc(s["counts_ready"], 1)
                    pe.wait_ge(s["bias_done"], b + 1)
                    pe.wait_ge(s["taken_done"], b * 2 + 2)

            @block.scalar
            def _(act):
                with act.Fori(0, B) as b:
                    act.wait_ge(s["q_ready"], b + 1)
                    nc.scalar.activation(qT[:, :], g.bank[0][:, :], ACT.Copy).then_inc(s["q_copied"], 1)

            @block.vector
            def _(dve):
                with dve.Fori(0, B) as b:
                    for t in range(QT):
                        hold(dve, s, s["scores_ready"], b * QT + (t + 1))
                        nc.vector.max(top[:, t, :], g.bank[1 + t][:, 0:CTX]).then_inc(s["top_done"], 1)
                    for t in range(QT):
                        hold(dve, s, s["top_done"], b * QT + (t + 1))
                        nc.vector.max_index(where[:, t, :], top[:, t, :], g.bank[1 + t][:, 0:CTX]).then_inc(s["where_done"], 1)
                    dve.wait_ge(s["where_done"], b * QT + QT)
                    nc.vector.tensor_copy(at[:, :], where[:, :, 0]).then_inc(s["at_done"], 1)
                    dve.wait_ge(s["at_done"], b + 1)
                    for t in range(QT):
                        nc.vector.tensor_scalar(onehot[:, t, :], iota[:, :], at[:, t:t + 1], None,
                                                ALU.is_equal).then_inc(s["onehot_done"], 1)
                    dve.wait_ge(s["counts_ready"], b + 1)
                    nc.vector.tensor_scalar(key_bias[:, ds(b, 1), 0:CTX], g.bank[5][0:1, 0:CTX], 0.0, MASKED,
                                            ALU.is_equal, ALU.mult).then_inc(s["bias_done"], 1)
                    for k, (k0, kn) in enumerate(KT_CTX):
                        nc.vector.tensor_copy(taken[0:kn, ds(b * 2 + k, 1)],
                                              g.bank[6 + k][0:kn, 0:1]).then_inc(s["taken_done"], 1)
        clear(nc, s)


def differential_attention_2(nc, g, io):
    with ExitStack() as stack:
        sbuf = room(nc, stack)

        w = {n: sbuf(f"w_{n}", [P, D]) for n in ("q1", "k1", "q2", "k2", "v")}
        parts = {n: sbuf(f"{n}_parts", [P, 3, T], BF16) for n in ("q1", "k1", "q2", "k2")}
        rows = sbuf("value_rows", [P, NT * H, DH + 1])
        out = [sbuf(f"heads_out{i}", [P, NT, D]) for i in range(2)]
        gamma, beta, lamb = sbuf("gamma", [P, D]), sbuf("beta", [P, D]), sbuf("lamb", [P, 1])
        load(nc, g, [(w[n][:, :], io[f"L2_attn_w{n}"]) for n in w] +
             [(gamma[:, :], io["L2_attn_ln_gamma"]), (beta[:, :], io["L2_attn_ln_beta"]),
              (lamb[:, :], io["L2_attn_lamb"])], ones=(rows[:, :, :],))
        project(nc, g, [Projection(w[n], False, parts[n]) for n in parts], Values(w["v"], False, rows))
        for i in range(2):
            attend(nc, g, parts[f"q{i + 1}"], parts[f"k{i + 1}"], rows, out[i], context=False)
        differ(nc, g, out, gamma, beta, lamb)
        finish(nc, g, "tokens", out[0])


def differ(nc, g, out, gamma, beta, lamb):
    with ExitStack() as stack:
        sbuf = room(nc, stack)

        minus_lamb, rest = sbuf("minus_lamb", [P, 1]), sbuf("one_less_lamb", [P, 1])
        z = sbuf("dif_z", [P, QT, D])
        stats, moments = sbuf("dif_stats", [P, QT, 6]), sbuf("dif_moments", [P, QT, 2])
        shifted, rstd = sbuf("dif_shifted", [P, QT]), sbuf("dif_rstd", [P, QT])
        s = signals(nc, stack, "scalars_done", "gamma_done", "z_done", "stats_done", "moments_done", "shift_done",
                    "rstd_done", "normal_done", "scaled", "out_done")
        with nc.Block() as block:
            @block.gpsimd
            def _(pool):
                with pool.Fori(0, B) as b:
                    hold(pool, s, s["moments_done"], b * QT + QT)
                    nc.gpsimd.tensor_scalar(shifted[:, :], moments[:, :, 1], EPS, None, ALU.add).then_inc(s["shift_done"], 1)
                    hold(pool, s, s["shift_done"], b + 1)
                    nc.gpsimd.tensor_tensor(rstd[:, :], shifted[:, :], g.power[:, 0:QT], ALU.pow).then_inc(s["rstd_done"], 1)

            @block.vector
            def _(dve):
                nc.vector.tensor_scalar(minus_lamb[:, :], lamb[:, :], -1.0, None, ALU.mult).then_inc(s["scalars_done"], 1)
                nc.vector.tensor_scalar(rest[:, :], lamb[:, :], -1.0, 1.0, ALU.mult, ALU.add).then_inc(s["scalars_done"], 1)
                dve.wait_ge(s["scalars_done"], 2)
                for v in (gamma, beta):
                    nc.vector.tensor_scalar(v[:, :], v[:, :], rest[:, 0:1], None, ALU.mult).then_inc(s["gamma_done"], 1)
                dve.wait_ge(s["gamma_done"], 2)
                with dve.Fori(0, B) as b:
                    here = ds(b * QT, QT)
                    nc.vector.scalar_tensor_tensor(z[:, :, :], out[1][:, here, :], minus_lamb[:, 0:1],
                                                   out[0][:, here, :], ALU.mult, ALU.add).then_inc(s["z_done"], 1)
                    dve.wait_ge(s["z_done"], b + 1)
                    for t in range(QT):
                        nc.vector.bn_stats(stats[:, t, :], z[:, t, :]).then_inc(s["stats_done"], 1)
                    hold(dve, s, s["stats_done"], b * QT + QT)
                    for t in range(QT):
                        nc.vector.bn_aggr(moments[:, t, :], stats[:, t, :]).then_inc(s["moments_done"], 1)
                    dve.wait_ge(s["moments_done"], b * QT + QT)
                    dve.wait_ge(s["rstd_done"], b + 1)
                    for t in range(QT):
                        nc.vector.tensor_scalar(z[:, t, :], z[:, t, :], moments[:, t, 0:1], rstd[:, t:t + 1],
                                                ALU.subtract, ALU.mult).then_inc(s["normal_done"], 1)
                    dve.wait_ge(s["normal_done"], b * QT + QT)
                    nc.vector.tensor_tensor(z[:, :, :], z[:, :, :], gamma[:, :].unsqueeze(1).to_broadcast([P, QT, D]),
                                            ALU.mult).then_inc(s["scaled"], 1)
                    dve.wait_ge(s["scaled"], b + 1)
                    nc.vector.tensor_tensor(out[0][:, here, :], z[:, :, :],
                                            beta[:, :].unsqueeze(1).to_broadcast([P, QT, D]),
                                            ALU.add).then_inc(s["out_done"], 1)
                    dve.wait_ge(s["out_done"], b + 1)
        clear(nc, s)


def context_attention_2(nc, g, io):
    with ExitStack() as stack:
        sbuf = room(nc, stack)

        w = {n: sbuf(f"w_{n}", [P, D]) for n in ("q", "k", "v", "o")}
        q_parts = sbuf("q_parts", [P, 3, T], BF16)
        k_parts = sbuf("k_parts", [P, 3, B * CTX], BF16)
        rows = sbuf("value_rows", [P, B * len(KT_CTX) * H, DH + 1])
        out = sbuf("heads_out", [P, NT, D])
        b_q, b_k = sbuf("b_q", [P, 1]), sbuf("b_k", [P, 1])
        b_v, b_o = sbuf("b_v", [1, D]), sbuf("b_o", [1, D])
        keep = [sbuf(f"keep{i}", [n, T], I32) for i, (_, n) in enumerate(KT_CTX)]
        mask = [sbuf(f"mask{i}", [n, T], BF16) for i, (_, n) in enumerate(KT_CTX)]
        load(nc, g, [(w[n][:, :], io[f"L2_xattn_W_{n}"]) for n in w] +
             [(b_q[:, :], io["L2_xattn_b_q"].unsqueeze(1)), (b_k[:, :], io["L2_xattn_b_k"].unsqueeze(1)),
              (b_v[:, :], io["L2_xattn_b_v"].unsqueeze(0)), (b_o[:, :], io["L2_xattn_b_o"].unsqueeze(0))] +
             [(keep[i][:, :], io["mask_turned"][k0:k0 + kn, :]) for i, (k0, kn) in enumerate(KT_CTX)],
             ones=(rows[:, :, :],))
        with ExitStack() as inner:
            s = signals(nc, inner, "masked")
            with nc.Block() as block:
                @block.vector
                def _(dve):
                    for i in range(2):
                        nc.vector.tensor_scalar(mask[i][:, :], keep[i][:, :], 0.0, MASKED, ALU.is_equal,
                                                ALU.mult).then_inc(s["masked"], 1)
            clear(nc, s)
        project(nc, g, [Projection(w["q"], False, q_parts, b_q), Projection(w["k"], True, k_parts, b_k)],
                Values(w["v"], True, rows, b_v))
        attend(nc, g, q_parts, k_parts, rows, out, context=True, mask=mask)
        finish(nc, g, "heads", out, w["o"], b_o)


def spread_experts(nc, g, combine, n_experts, parts):
    with ExitStack() as stack:
        sbuf = room(nc, stack)
        split = sbuf("split", [P, 3, NT, n_experts], BF16)
        left = sbuf("split_left", [P, NT, n_experts])
        s = signals(nc, stack, "split_done", "turned", "stored")
        with nc.Block() as block:
            @block.vector
            def _(dve):
                chain = Chain(dve, s["split_done"])
                chain.step(nc.vector.tensor_copy(split[:, 0], combine[:, :, :]))
                chain.step(nc.vector.tensor_tensor(left[:, :, :], combine[:, :, :], split[:, 0], ALU.subtract))
                chain.step(nc.vector.tensor_copy(split[:, 1], left[:, :, :]))
                chain.step(nc.vector.tensor_tensor(split[:, 2], left[:, :, :], split[:, 1], ALU.subtract))

            @block.tensor
            def _(pe):
                pe.wait_ge(s["split_done"], 4)
                for n in range(3 * B):
                    j, b = n % 3, n // 3
                    if n >= 4:
                        pe.wait_ge(s["stored"], n - 3)
                    for t in range(QT):
                        ins = nc.tensor.matmul(g.bank[n % 4][0:n_experts, t * P:(t + 1) * P],
                                               split[:, j, b * QT + t, :], g.ident_bf[:, :],
                                               start=True, stop=True)
                    ins.then_inc(s["turned"], 1)

            @block.scalar
            def _(act):
                for n in range(3 * B):
                    j, b = n % 3, n // 3
                    act.wait_ge(s["turned"], n + 1)
                    nc.scalar.activation(parts[0:n_experts, j, b * S:(b + 1) * S], g.bank[n % 4][0:n_experts, :],
                                         ACT.Copy).then_inc(s["stored"], 1)
        clear(nc, s)


def router_logits(nc, g, w, n_out, logits):
    with ExitStack() as stack:
        s = signals(nc, stack, "ready", "stored")
        with nc.Block() as block:
            @block.tensor
            def _(pe):
                for t in range(NT):
                    ins = nc.tensor.matmul(g.bank[t // QT][:, (t % QT) * P:(t % QT) * P + n_out],
                                           g.xT[:, t * P:(t + 1) * P], w[:, 0:n_out], start=True, stop=True)
                    if t % QT == QT - 1:
                        ins.then_inc(s["ready"], 1)

            @block.vector
            def _(dve):
                for b in range(B):
                    dve.wait_ge(s["ready"], b + 1)
                    src = g.bank[b][:, :].rearrange("p (t e) -> p t e", t=QT)[:, :, 0:n_out]
                    nc.vector.tensor_copy(logits[:, b * QT:(b + 1) * QT, :], src).then_inc(s["stored"], 1)
        clear(nc, s)


def choose_top(nc, step, choice, n_experts, k, top, buf):
    v = choice[:, :, 0:n_experts]

    def wide(x):
        return x.unsqueeze(2).to_broadcast([P, NT, n_experts])

    for t in range(NT):
        step(nc.vector.max(top[:, t, :], choice[:, t, 0:n_experts]))
    least = wide(top[:, :, k - 1])
    step(nc.vector.tensor_tensor(buf.above[:, :, :], v, least, ALU.is_gt))
    step(nc.vector.tensor_tensor(buf.equal[:, :, :], v, least, ALU.is_equal))
    step(nc.vector.tensor_reduce(buf.count[:, :], buf.above[:, :, :], AX.X, ALU.add))
    step(nc.vector.tensor_scalar(buf.count[:, :], buf.count[:, :], -1.0, float(k), ALU.mult, ALU.add))
    step(nc.vector.tensor_tensor_scan(buf.order[:, :, :].rearrange("p t e -> p (t e)"),
                                      buf.goes_on[:, :, :].rearrange("p t e -> p (t e)"),
                                      buf.equal[:, :, :].rearrange("p t e -> p (t e)"), 0.0, ALU.mult, ALU.add))
    step(nc.vector.tensor_tensor(buf.order[:, :, :], buf.order[:, :, :], wide(buf.count[:, :]), ALU.is_le))
    step(nc.vector.tensor_tensor(buf.order[:, :, :], buf.order[:, :, :], buf.equal[:, :, :], ALU.mult))
    step(nc.vector.tensor_tensor(buf.chosen[:, :, :], buf.order[:, :, :], buf.above[:, :, :], ALU.add))


class TopBuffers:
    def __init__(self, sbuf, n_experts):
        self.above = sbuf("top_above", [P, NT, n_experts])
        self.equal = sbuf("top_equal", [P, NT, n_experts])
        self.order = sbuf("top_order", [P, NT, n_experts])
        self.chosen = sbuf("top_chosen", [P, NT, n_experts])
        self.goes_on = sbuf("top_goes_on", [P, NT, n_experts])
        self.count = sbuf("top_count", [P, NT])


def experts(nc, g, weights, n_pairs, n_experts, parts, select, yT):
    half = T // 2
    with ExitStack() as stack:
        sbuf = room(nc, stack)
        w = [sbuf(f"expert_w{u}", [P, 3 * P]) for u in range(2)]
        gated = [sbuf(f"gated{i}", [P, S]) for i in range(2)]
        product = [sbuf(f"product{i}", [P, S]) for i in range(2)]
        hidden = [sbuf(f"hidden{i}", [P, S]) for i in range(2)]
        nothing = sbuf("nothing", [P, S], BF16)
        scrap = sbuf("scrap", [P, 1])
        s = signals(nc, stack, "filled", "w_loaded0", "w_loaded1", "w_used", "up_ready", "gated_done", "product_done",
                    "hidden_done", "y_done", "y_half_done", "y_stored", "warmed")
        w_loaded = (s["w_loaded0"], s["w_loaded1"])
        banks = [g.bank[2:5], g.bank[5:8]]

        with nc.Block() as block:
            @block.sync
            def _(sp):
                with sp.Fori(0, 2) as h:
                    with sp.Fori(0, n_pairs // 2) as i:
                        for u in range(2):
                            m = h * n_pairs + i * 2 + u
                            sp.wait_ge(s["w_used"], m + 1)
                            sp.dma_start(w[u][:, :], weights[ds(i * 2 + u, 1), :, :].rearrange("a p n -> p (a n)")
                                         ).then_inc(w_loaded[u], 16)

            @block.tensor
            def _(pe):
                def up(h, a, m, u, blk):
                    n = m * 2 + blk
                    pe.wait_ge(s["hidden_done"], n + 1)
                    x = g.xT[:, ds(h * half + blk * S, S)]
                    gate_bank, up_bank, weight_bank = banks[blk]
                    nc.tensor.matmul(gate_bank[:, :], w[u][:, 0:P], x, start=True, stop=True)
                    nc.tensor.matmul(up_bank[:, :], w[u][:, P:2 * P], x, start=True, stop=True)
                    for j in range(3):
                        ins = nc.tensor.matmul(weight_bank[:, :], select[0:n_experts, ds(a * P, P)],
                                               parts[0:n_experts, j, ds(h * half + blk * S, S)],
                                               start=(j == 0), stop=(j == 2))
                    ins.then_inc(s["up_ready"], 1)

                def down(m, u, blk):
                    pe.wait_ge(s["hidden_done"], m * 2 + (blk + 3))
                    ins = nc.tensor.matmul(g.bank[blk][:, :], w[u][:, 2 * P:3 * P], hidden[blk][:, :],
                                           start=False, stop=True, skip_group_check=True)
                    ins.then_inc(s["y_done"], 1)

                pe.sem_inc(s["w_used"], 2)
                pe.sem_inc(s["y_done"], 2)
                pe.wait_ge(s["filled"], 1)
                with pe.Fori(0, 2) as h:
                    pe.wait_ge(s["y_stored"], h * 2 + 2)
                    for blk in range(2):
                        nc.tensor.matmul(g.bank[blk][:, :], nothing[:, 0:P], nothing[:, :], start=True, stop=True)
                    with pe.Fori(0, n_pairs // 2) as i:
                        m = h * n_pairs + i * 2
                        pe.wait_ge(w_loaded[0], h * (8 * n_pairs) + i * 16 + 16)
                        up(h, i * 2, m, 0, 0)
                        up(h, i * 2, m, 0, 1)
                        down(m, 0, 0)
                        pe.wait_ge(w_loaded[1], h * (8 * n_pairs) + i * 16 + 16)
                        up(h, i * 2 + 1, m + 1, 1, 0)
                        down(m, 0, 1)
                        pe.drain().then_inc(s["w_used"], 1)
                        up(h, i * 2 + 1, m + 1, 1, 1)
                        down(m + 1, 1, 0)
                        down(m + 1, 1, 1)
                        pe.drain().then_inc(s["w_used"], 1)
                    pe.drain().then_inc(s["y_half_done"], 1)

            @block.scalar
            def _(act):
                act.sem_inc(s["y_stored"], 2)
                nc.scalar.activation(scrap[:, :], g.zero[:, :], ACT.Silu).then_inc(s["warmed"], 1)
                with act.Fori(0, 2) as h:
                    with act.Fori(0, n_pairs) as a:
                        for blk in range(2):
                            n = h * (n_pairs * 2) + a * 2 + blk
                            act.wait_ge(s["up_ready"], n + 1)
                            act.wait_ge(s["product_done"], n + 1)
                            nc.scalar.activation(gated[blk][:, :], banks[blk][0][:, :], ACT.Silu).then_inc(s["gated_done"], 1)
                    act.wait_ge(s["y_half_done"], h + 1)
                    for blk in range(2):
                        nc.scalar.activation(yT[:, ds(h * half + blk * S, S)], g.bank[blk][:, :],
                                             ACT.Copy).then_inc(s["y_stored"], 1)
                act.wait_ge(s["warmed"], 1)
                nc.scalar.activation(scrap[:, :], g.zero[:, :], ACT.Exp).then_inc(s["warmed"], 1)

            @block.vector
            def _(dve):
                nc.vector.memset(nothing[:, :], 0.0).then_inc(s["filled"], 1)
                dve.sem_inc(s["hidden_done"], 2)
                dve.sem_inc(s["product_done"], 2)
                with dve.Fori(0, 2) as h:
                    with dve.Fori(0, n_pairs) as a:
                        for blk in range(2):
                            n = h * (n_pairs * 2) + a * 2 + blk
                            dve.wait_ge(s["gated_done"], n + 1)
                            nc.vector.tensor_tensor(product[blk][:, :], gated[blk][:, :], banks[blk][1][:, :],
                                                    ALU.mult).then_inc(s["product_done"], 1)
                            dve.wait_ge(s["product_done"], n + 3)
                            dve.wait_ge(s["y_done"], n + 1)
                            nc.vector.tensor_tensor(hidden[blk][:, :], product[blk][:, :], banks[blk][2][:, :],
                                                    ALU.mult).then_inc(s["hidden_done"], 1)
        clear(nc, s)


def grouped_experts_0(nc, g, io):
    E, G, K = 16, 4, 4
    with ExitStack() as stack:
        sbuf = room(nc, stack)
        yT = sbuf("yT", [P, T])
        parts = sbuf("combine_parts", [E, 3, T], BF16)
        select = sbuf("expert_select", [E, E // 2 * P], BF16)
        with ExitStack() as inner:
            sbuf = room(nc, inner)
            w, bias, choose_f = sbuf("router_w", [P, E]), sbuf("router_bias", [P, E]), sbuf("select_f", [E, E // 2 * P])
            logits, scores = sbuf("router_logits", [P, NT, E]), sbuf("router_scores", [P, NT, E])
            choice = sbuf("router_choice", [P, NT, E])
            pair, best2 = sbuf("pair_sum", [P, NT, G]), sbuf("best_two", [P, NT, G])
            wins, rank = sbuf("group_wins", [P, NT]), sbuf("group_rank", [P, NT, G])
            top = sbuf("top8", [P, NT, 8])
            total = sbuf("total", [P, NT])
            buf = TopBuffers(sbuf, E)
            load(nc, g, [(w[:, :], io["L0_ffn_gate_weight"]), (bias[:, :], io["L0_ffn_e_bias"]),
                         (choose_f[:, :], io["c_select16"]), (buf.goes_on[:, :, :], io["c_goes_on16"])])
            router_logits(nc, g, w, E, logits)
            s = signals(nc, inner, "exp_done", "routed")
            with nc.Block() as block:
                @block.scalar
                def _(act):
                    nc.scalar.activation(scores[:, :, :], logits[:, :, :], ACT.Exp, scale=-1.0).then_inc(s["exp_done"], 1)

                @block.vector
                def _(dve):
                    step = Chain(dve, s["routed"]).step
                    tt, ts = nc.vector.tensor_tensor, nc.vector.tensor_scalar
                    step(nc.vector.tensor_copy(select[:, :], choose_f[:, :]))
                    dve.wait_ge(s["exp_done"], 1)
                    step(ts(scores[:, :, :], scores[:, :, :], 1.0, None, ALU.add))
                    step(nc.vector.reciprocal(scores[:, :, :], scores[:, :, :]))
                    step(tt(choice[:, :, :], scores[:, :, :], bias[:, :].unsqueeze(1).to_broadcast([P, NT, E]), ALU.add))
                    of = choice[:, :, :].rearrange("p t (g i) -> p t g i", g=G)
                    first = True
                    for i in range(E // G):
                        for j in range(i + 1, E // G):
                            dst = best2 if first else pair
                            step(tt(dst[:, :, :], of[:, :, :, i], of[:, :, :, j], ALU.add))
                            if not first:
                                step(tt(best2[:, :, :], best2[:, :, :], pair[:, :, :], ALU.max))
                            first = False
                    for i in range(G):
                        step(nc.vector.memset(rank[:, :, i], float(G - 1 - i)))
                    for i in range(G):
                        for j in range(i + 1, G):
                            step(tt(wins[:, :], best2[:, :, i], best2[:, :, j], ALU.is_ge))
                            step(tt(rank[:, :, i], rank[:, :, i], wins[:, :], ALU.subtract))
                            step(tt(rank[:, :, j], rank[:, :, j], wins[:, :], ALU.add))
                    step(ts(rank[:, :, :], rank[:, :, :], 1.5, None, ALU.is_lt))
                    step(tt(of, of, rank[:, :, :].unsqueeze(3).to_broadcast([P, NT, G, E // G]), ALU.mult))
                    choose_top(nc, step, choice, E, K, top, buf)
                    step(tt(scores[:, :, :], scores[:, :, :], buf.chosen[:, :, :], ALU.mult))
                    step(nc.vector.tensor_reduce(total[:, :], scores[:, :, :], AX.X, ALU.add))
                    step(ts(total[:, :], total[:, :], 1e-20, None, ALU.add))
                    step(nc.vector.reciprocal(total[:, :], total[:, :]))
                    step(tt(scores[:, :, :], scores[:, :, :], total[:, :].unsqueeze(2).to_broadcast([P, NT, E]), ALU.mult))
            clear(nc, s)
            spread_experts(nc, g, scores, E, parts)
        experts(nc, g, io["L0_ffn_pairs"], E // 2, E, parts, select, yT)
        finish(nc, g, "transposed", yT)


def limited_experts_2(nc, g, io):
    E, K, CAPACITY = 64, 8, 64
    C = E + 1
    n_pairs = E // 2 + 2
    with ExitStack() as stack:
        sbuf = room(nc, stack)
        yT = sbuf("yT", [P, T])
        parts = sbuf("combine_parts", [C, 3, T], BF16)
        select = sbuf("expert_select", [C, n_pairs * P], BF16)
        with ExitStack() as inner:
            sbuf = room(nc, inner)
            w, choose_f = sbuf("router_w", [P, C]), sbuf("select_f", [C, n_pairs * P])
            logits, combine = sbuf("router_logits", [P, NT, C]), sbuf("combine", [P, NT, C])
            probs = sbuf("router_probs", [P, NT, E])
            most, total = sbuf("router_most", [P, NT]), sbuf("total", [P, NT])
            top = sbuf("top8", [P, NT, 8])
            buf = TopBuffers(sbuf, E)
            before_f, before = sbuf("before_f", [P, P]), sbuf("before", [P, P], BF16)
            all_ones = sbuf("all_ones", [P, P], BF16)
            chosen = sbuf("chosen_bf", [P, NT, E], BF16)
            running = sbuf("running", [P, NT, E], BF16)
            load(nc, g, [(w[:, :], io["L2_ffn_router"]), (choose_f[:, :], io["c_select65"]),
                         (buf.goes_on[:, :, :], io["c_goes_on64"]), (before_f[:, :], io["c_before"])],
                 ones=(all_ones[:, :],))
            router_logits(nc, g, w, C, logits)
            s = signals(nc, inner, "shifted", "exp_done", "routed", "chosen_done", "counted")
            with nc.Block() as block:
                @block.scalar
                def _(act):
                    nc.scalar.activation(combine[:, :, E], logits[:, :, E], ACT.Exp, scale=-1.0).then_inc(s["exp_done"], 1)
                    act.wait_ge(s["shifted"], 2)
                    nc.scalar.activation(probs[:, :, :], logits[:, :, 0:E], ACT.Exp).then_inc(s["exp_done"], 1)

                @block.tensor
                def _(pe):
                    pe.wait_ge(s["chosen_done"], 1)
                    for t in range(NT):
                        dst = g.bank[t // 8][:, (t % 8) * E:(t % 8 + 1) * E]
                        nc.tensor.matmul(dst, before[:, :], chosen[:, t, :], start=True, stop=False,
                                         skip_group_check=True)
                        ins = nc.tensor.matmul(dst, all_ones[:, :], running[:, t, :], start=False, stop=True,
                                               skip_group_check=True)
                    ins.then_inc(s["counted"], 1)

                @block.vector
                def _(dve):
                    step = Chain(dve, s["routed"]).step
                    tt, ts = nc.vector.tensor_tensor, nc.vector.tensor_scalar

                    def wide(x, n=E):
                        return x.unsqueeze(2).to_broadcast([P, NT, n])

                    step(nc.vector.tensor_copy(select[:, :], choose_f[:, :]))
                    step(nc.vector.tensor_copy(before[:, :], before_f[:, :]))
                    nc.vector.tensor_reduce(most[:, :], logits[:, :, 0:E], AX.X, ALU.max).then_inc(s["shifted"], 1)
                    dve.wait_ge(s["shifted"], 1)
                    nc.vector.tensor_tensor(logits[:, :, 0:E], logits[:, :, 0:E], wide(most[:, :]),
                                            ALU.subtract).then_inc(s["shifted"], 1)
                    dve.wait_ge(s["exp_done"], 2)
                    step(nc.vector.tensor_reduce(total[:, :], probs[:, :, :], AX.X, ALU.add))
                    step(nc.vector.reciprocal(total[:, :], total[:, :]))
                    step(tt(probs[:, :, :], probs[:, :, :], wide(total[:, :]), ALU.mult))
                    choose_top(nc, step, probs, E, K, top, buf)
                    step(nc.vector.tensor_copy(chosen[:, :, :], buf.chosen[:, :, :]))
                    step(nc.vector.memset(running[:, 0, :], 0.0))
                    for t in range(1, NT):
                        step(tt(running[:, t, :], running[:, t - 1, :], chosen[:, t - 1, :], ALU.add))
                    dve.sem_inc(s["chosen_done"], 1)
                    step(tt(probs[:, :, :], probs[:, :, :], buf.chosen[:, :, :], ALU.mult))
                    step(nc.vector.tensor_reduce(total[:, :], probs[:, :, :], AX.X, ALU.add))
                    step(nc.vector.reciprocal(total[:, :], total[:, :]))
                    step(tt(probs[:, :, :], probs[:, :, :], wide(total[:, :]), ALU.mult))
                    dve.wait_ge(s["counted"], 1)
                    for i in range(2):
                        src = g.bank[i][:, :].rearrange("p (t e) -> p t e", t=8)
                        step(ts(buf.above[:, 8 * i:8 * i + 8, :], src, CAPACITY - 0.5, None, ALU.is_lt))
                    step(tt(combine[:, :, 0:E], probs[:, :, :], buf.above[:, :, :], ALU.mult))
                    step(ts(combine[:, :, E], combine[:, :, E], 1.0, None, ALU.add))
                    step(nc.vector.reciprocal(combine[:, :, E], combine[:, :, E]))
            clear(nc, s)
            spread_experts(nc, g, combine, C, parts)
        experts(nc, g, io["L2_ffn_pairs"], n_pairs, C, parts, select, yT)
        finish(nc, g, "transposed", yT)


def fixed_experts_1(nc, g, io):
    E, F = 8, 4
    PACK = 2 * F * P + F + 1
    with ExitStack() as stack:
        sbuf = room(nc, stack)
        w_in, w_next = sbuf("w_in", [P, D]), sbuf("w_next", [P, D])
        columns = sbuf("columns", [P, 4])
        xaT, outT = sbuf("xaT", [P, T]), sbuf("outT", [P, T])
        load(nc, g, [(w_in[:, :], io["L1_ffn_attn_w"]), (w_next[:, :], io["L1_ffn_next_w"]),
                     (columns[:, :], io["L1_ffn_columns"])])
        with ExitStack() as inner:
            sbuf = room(nc, inner)
            z = sbuf("pre_z", [P, 2, QT, D])
            stats, moments = sbuf("pre_stats", [P, 2, QT, 6]), sbuf("pre_moments", [P, 2, QT, 2])
            shifted, rstd = sbuf("pre_shifted", [P, 2, QT]), sbuf("pre_rstd", [P, 2, QT])
            znT = sbuf("pre_znT", [P, 2, S])
            partial = sbuf("pre_partial", [P, 2, S])
            s = signals(nc, inner, "z_done", "stats_done", "moments_done", "shift_done", "rstd_done", "normal_done",
                        "turned", "scaled", "product_ready", "partial_done", "stored")
            with nc.Block() as block:
                @block.gpsimd
                def _(pool):
                    with pool.Fori(0, B // 2) as i:
                        for u in range(2):
                            b = i * 2 + u
                            hold(pool, s, s["moments_done"], b * QT + QT)
                            nc.gpsimd.tensor_scalar(shifted[:, u, :], moments[:, u, :, 1], EPS, None,
                                                    ALU.add).then_inc(s["shift_done"], 1)
                            hold(pool, s, s["shift_done"], b + 1)
                            nc.gpsimd.tensor_tensor(rstd[:, u, :], shifted[:, u, :], g.power[:, 0:QT],
                                                    ALU.pow).then_inc(s["rstd_done"], 1)

                @block.vector
                def _(dve):
                    with dve.Fori(0, B // 2) as i:
                        for u in range(2):
                            b = i * 2 + u
                            nc.vector.tensor_copy(z[:, u], g.x[:, ds(b * QT, QT), :]).then_inc(s["z_done"], 1)
                            dve.wait_ge(s["z_done"], b + 1)
                            for t in range(QT):
                                nc.vector.bn_stats(stats[:, u, t, :], z[:, u, t, :]).then_inc(s["stats_done"], 1)
                            hold(dve, s, s["stats_done"], b * QT + QT)
                            for t in range(QT):
                                nc.vector.bn_aggr(moments[:, u, t, :], stats[:, u, t, :]).then_inc(s["moments_done"], 1)
                        for u in range(2):
                            b = i * 2 + u
                            dve.wait_ge(s["rstd_done"], b + 1)
                            dve.wait_ge(s["moments_done"], b * QT + QT)
                            for t in range(QT):
                                nc.vector.tensor_scalar(z[:, u, t, :], z[:, u, t, :], moments[:, u, t, 0:1],
                                                        rstd[:, u, t:t + 1], ALU.subtract,
                                                        ALU.mult).then_inc(s["normal_done"], 1)
                        for u in range(2):
                            b = i * 2 + u
                            dve.wait_ge(s["product_ready"], b + 1)
                            nc.vector.tensor_scalar(partial[:, u, :], g.bank[2 + u][:, :], columns[:, 2:3], None,
                                                    ALU.add).then_inc(s["partial_done"], 1)
                            dve.wait_ge(s["partial_done"], b + 1)
                            nc.vector.tensor_tensor(xaT[:, ds(b * S, S)], partial[:, u, :], g.xT[:, ds(b * S, S)],
                                                    ALU.add).then_inc(s["stored"], 1)
                            dve.wait_ge(s["stored"], b + 1)

                @block.tensor
                def _(pe):
                    with pe.Fori(0, B // 2) as i:
                        for u in range(2):
                            b = i * 2 + u
                            pe.wait_ge(s["normal_done"], b * QT + QT)
                            for t in range(QT):
                                ins = nc.tensor.transpose(g.bank[u][:, t * P:(t + 1) * P], z[:, u, t, :], g.ident[:, :])
                            ins.then_inc(s["turned"], 1)
                        for u in range(2):
                            b = i * 2 + u
                            pe.wait_ge(s["scaled"], b + 1)
                            nc.tensor.matmul(g.bank[2 + u][:, :], w_in[:, :], znT[:, u, :], start=True,
                                             stop=True).then_inc(s["product_ready"], 1)
                        pe.wait_ge(s["stored"], i * 2 + 2)

                @block.scalar
                def _(act):
                    with act.Fori(0, B // 2) as i:
                        for u in range(2):
                            act.wait_ge(s["turned"], i * 2 + u + 1)
                            nc.scalar.activation(znT[:, u, :], g.bank[u][:, :], ACT.Identity, bias=columns[:, 1:2],
                                                 scale=columns[:, 0:1]).then_inc(s["scaled"], 1)
            clear(nc, s)
        with ExitStack() as inner:
            sbuf = room(nc, inner)
            w = [sbuf(f"fixed_w{u}", [P, PACK]) for u in range(2)]
            hidden = [sbuf(f"fixed_h{u}", [P, F, 2 * P]) for u in range(2)]
            y = [sbuf(f"fixed_y{u}", [P, 2 * P]) for u in range(2)]
            scrap = sbuf("scrap", [P, 1])
            s = signals(nc, inner, "w_loaded0", "w_loaded1", "h_ready", "h_done", "y_ready", "y_done", "o_ready",
                        "o_done", "warmed")
            w_loaded = (s["w_loaded0"], s["w_loaded1"])
            x_view = xaT[:, :].rearrange("p (m n) -> p m n", m=2)
            o_view = outT[:, :].rearrange("p (m n) -> p m n", m=2)
            with nc.Block() as block:
                @block.sync
                def _(sp):
                    with sp.Fori(0, E // 2) as i:
                        for u in range(2):
                            sp.wait_ge(s["y_done"], i * 2 + u + 1)
                            sp.dma_start(w[u][:, :], io["L1_ffn_experts"][ds(i * 2 + u, 1), :, :].rearrange(
                                "e p n -> p (e n)")).then_inc(w_loaded[u], 16)

                @block.tensor
                def _(pe):
                    with pe.Fori(0, E // 2) as i:
                        for u in range(2):
                            e = i * 2 + u
                            pe.wait_ge(w_loaded[u], i * 16 + 16)
                            for f in range(F):
                                if f % 2 == 0:
                                    pe.wait_ge(s["h_done"], e * F + (f + 2))
                                ins = nc.tensor.matmul(g.bank[2 * u + f // 2][:, (f % 2) * 256:(f % 2) * 256 + 256],
                                                       w[u][:, f * P:(f + 1) * P], x_view[:, :, ds(e * P, P)],
                                                       start=True, stop=True)
                                if f % 2 == 1:
                                    ins.then_inc(s["h_ready"], 1)
                        for u in range(2):
                            e = i * 2 + u
                            pe.wait_ge(s["h_done"], e * F + (F + 8))
                            for f in range(F):
                                ins = nc.tensor.matmul(g.bank[4 + u][:, 0:256], w[u][:, (F + f) * P:(F + f + 1) * P],
                                                       hidden[u][:, f, :], start=(f == 0), stop=(f == F - 1))
                            ins.then_inc(s["y_ready"], 1)
                        for u in range(2):
                            e = i * 2 + u
                            pe.wait_ge(s["y_done"], e + 3)
                            nc.tensor.matmul(g.bank[6 + u][:, 0:256], w_next[:, :], y[u][:, :], start=True,
                                             stop=True).then_inc(s["o_ready"], 1)
                        pe.wait_ge(s["o_done"], i * 2 + 2)

                @block.scalar
                def _(act):
                    act.sem_inc(s["h_done"], 8)
                    act.sem_inc(s["y_done"], 2)
                    nc.scalar.activation(scrap[:, :], g.zero[:, :], ACT.Gelu).then_inc(s["warmed"], 1)
                    with act.Fori(0, E // 2) as i:
                        for u in range(2):
                            e = i * 2 + u
                            for f in range(F):
                                act.wait_ge(s["h_ready"], e * (F // 2) + (f // 2 + 1))
                                nc.scalar.activation(hidden[u][:, f, :],
                                                     g.bank[2 * u + f // 2][:, (f % 2) * 256:(f % 2) * 256 + 256],
                                                     ACT.Gelu, bias=w[u][:, 2 * F * P + f:2 * F * P + f + 1]
                                                     ).then_inc(s["h_done"], 1)
                        for u in range(2):
                            e = i * 2 + u
                            act.wait_ge(s["y_ready"], e + 1)
                            nc.scalar.activation(y[u][:, :], g.bank[4 + u][:, 0:256], ACT.Identity,
                                                 bias=w[u][:, PACK - 1:PACK]).then_inc(s["y_done"], 1)
                        for u in range(2):
                            e = i * 2 + u
                            act.wait_ge(s["o_ready"], e + 1)
                            nc.scalar.activation(o_view[:, :, ds(e * P, P)],
                                                 g.bank[6 + u][:, 0:256].rearrange("p (m n) -> p m n", m=2),
                                                 ACT.Gelu, bias=columns[:, 3:4]).then_inc(s["o_done"], 1)
                    act.wait_ge(s["warmed"], 1)
                    nc.scalar.activation(scrap[:, :], g.zero[:, :], ACT.Exp).then_inc(s["warmed"], 1)
            clear(nc, s)
        finish(nc, g, "transposed", outT)


def linear_attention_3(nc, g, io):
    SMALL = 1e-3
    with ExitStack() as stack:
        sbuf = room(nc, stack)
        w = sbuf("w_qkv", [P, 3 * D])
        w_o = sbuf("w_proj", [P, D])
        columns = sbuf("columns", [P, 5])
        same_head = sbuf("same_head", [P, P])
        outT = sbuf("outT", [P, T])
        lin = [sbuf(f"lin_{n}", [P, S]) for n in "qkv"]
        low = [sbuf(f"low_{n}", [P, S]) for n in "qk"]
        feat = [sbuf(f"feat_{n}", [P, S]) for n in "qk"]
        kv, k_sum, kv_sum = sbuf("kv", [P, S]), sbuf("k_sum", [P, S]), sbuf("kv_sum", [P, S])
        match, above, y = sbuf("match", [P, S]), sbuf("above", [P, S]), sbuf("y", [P, S])
        ones = sbuf("ones", [P, S])
        load(nc, g, [(w[:, :], io["L3_attn_Wqkv"]), (w_o[:, :], io["L3_attn_Wproj"]),
                     (columns[:, :], io["L3_attn_columns"]), (same_head[:, :], io["c_same_head"])],
             ones=(ones[:, :],))
        s = signals(nc, stack, "qkv_ready", "lin_done", "low_done", "exp_done", "chain", "match_done", "denom_ready",
                    "y_done", "out_ready", "out_done")
        with nc.Block() as block:
            @block.tensor
            def _(pe):
                with pe.Fori(0, B) as b:
                    for j in range(3):
                        pe.wait_ge(s["lin_done"], b * 3 + (j + 1))
                        nc.tensor.matmul(g.bank[j][:, :], w[:, j * D:(j + 1) * D], g.xT[:, ds(b * S, S)],
                                         start=True, stop=True).then_inc(s["qkv_ready"], 1)
                    pe.wait_ge(s["match_done"], b + 1)
                    nc.tensor.matmul(g.bank[3][:, :], same_head[:, :], match[:, :], start=True,
                                     stop=True).then_inc(s["denom_ready"], 1)
                    pe.wait_ge(s["y_done"], b * 2 + 2)
                    pe.wait_ge(s["out_done"], b + 1)
                    nc.tensor.matmul(g.bank[4][:, :], w_o[:, :], y[:, :], start=True, stop=True).then_inc(s["out_ready"], 1)

            @block.scalar
            def _(act):
                act.sem_inc(s["out_done"], 1)
                with act.Fori(0, B) as b:
                    for j in range(2):
                        act.wait_ge(s["low_done"], b * 2 + (j + 1))
                        nc.scalar.activation(low[j][:, :], low[j][:, :], ACT.Exp).then_inc(s["exp_done"], 1)
                    act.wait_ge(s["out_ready"], b + 1)
                    nc.scalar.activation(outT[:, ds(b * S, S)], g.bank[4][:, :], ACT.Identity,
                                         bias=columns[:, 3:4]).then_inc(s["out_done"], 1)

            @block.vector
            def _(dve):
                dve.sem_inc(s["lin_done"], 3)
                with dve.Fori(0, B) as b:
                    for j in range(3):
                        dve.wait_ge(s["qkv_ready"], b * 3 + (j + 1))
                        if j < 2:
                            nc.vector.tensor_scalar(lin[j][:, :], g.bank[j][:, :], columns[:, j:j + 1],
                                                    columns[:, 4:5], ALU.add, ALU.mult).then_inc(s["lin_done"], 1)
                        else:
                            nc.vector.tensor_scalar(lin[j][:, :], g.bank[j][:, :], columns[:, j:j + 1], None,
                                                    ALU.add).then_inc(s["lin_done"], 1)
                    dve.wait_ge(s["lin_done"], b * 3 + 6)
                    for j in range(2):
                        nc.vector.tensor_scalar(low[j][:, :], lin[j][:, :], 0.0, None, ALU.min).then_inc(s["low_done"], 1)
                    step = Chain(dve, s["chain"], b * 7).step
                    dve.wait_ge(s["exp_done"], b * 2 + 2)
                    for j in range(2):
                        step(nc.vector.scalar_tensor_tensor(feat[j][:, :], lin[j][:, :], 0.0, low[j][:, :],
                                                            ALU.max, ALU.add))
                    step(nc.vector.tensor_tensor(kv[:, :], feat[1][:, :], lin[2][:, :], ALU.mult))
                    step(nc.vector.tensor_tensor_scan(k_sum[:, :], ones[:, :], feat[1][:, :], 0.0, ALU.mult, ALU.add))
                    nc.vector.tensor_tensor(match[:, :], feat[0][:, :], k_sum[:, :], ALU.mult).then_inc(s["match_done"], 1)
                    step(nc.vector.tensor_tensor_scan(kv_sum[:, :], ones[:, :], kv[:, :], 0.0, ALU.mult, ALU.add))
                    dve.wait_ge(s["denom_ready"], b + 1)
                    step(nc.vector.tensor_scalar(above[:, :], g.bank[3][:, :], SMALL, None, ALU.max))
                    step(nc.vector.reciprocal(above[:, :], above[:, :]))
                    nc.vector.tensor_tensor(kv[:, :], feat[0][:, :], kv_sum[:, :], ALU.mult).then_inc(s["y_done"], 1)
                    dve.wait_ge(s["y_done"], b * 2 + 1)
                    nc.vector.tensor_tensor(y[:, :], kv[:, :], above[:, :], ALU.mult).then_inc(s["y_done"], 1)
        clear(nc, s)
        finish(nc, g, "transposed", outT)


def sparse_or_soft_attention_0(nc, g, io):
    with ExitStack() as stack:
        sbuf = room(nc, stack)
        w = {n: sbuf(f"w_{n}", [P, D]) for n in "qkv"}
        flag, no_flag = sbuf("flag", [P, 1]), sbuf("no_flag", [P, 1])
        y = sbuf("attended", [P, NT, D])
        load(nc, g, [(w[n][:, :], io[f"L0_attn_W{n}"]) for n in w])
        with ExitStack() as inner:
            sbuf = room(nc, inner)
            absolute, all_ones = sbuf("absolute", [P, 1]), sbuf("all_ones", [P, P])
            s = signals(nc, inner, "summed", "total", "flagged")
            with nc.Block() as block:
                @block.vector
                def _(dve):
                    nc.vector.memset(all_ones[:, :], 1.0).then_inc(s["summed"], 1)
                    nc.vector.tensor_reduce(absolute[:, :], g.x[:, :, :].rearrange("p t d -> p (t d)"), AX.X,
                                            ALU.add, apply_absolute_value=True).then_inc(s["summed"], 1)
                    dve.wait_ge(s["total"], 1)
                    step = Chain(dve, s["flagged"]).step
                    step(nc.vector.tensor_scalar(flag[:, :], g.bank[0][:, 0:1], 1.0 / (T * D), 1.0, ALU.mult, ALU.is_lt))
                    step(nc.vector.tensor_scalar(no_flag[:, :], flag[:, :], -1.0, 1.0, ALU.mult, ALU.add))

                @block.tensor
                def _(pe):
                    pe.wait_ge(s["summed"], 2)
                    nc.tensor.matmul(g.bank[0][:, 0:1], all_ones[:, :], absolute[:, :], start=True,
                                     stop=True).then_inc(s["total"], 1)
            clear(nc, s)
        sorted_attention(nc, g, w, flag, no_flag, y)
        finish(nc, g, "tokens", y)


def sorting_steps():
    size = 2
    while size <= S:
        yield size, True
        block = size // 2
        while block > 1:
            yield block, False
            block //= 2
        size *= 2


def backwards(view, first, count):
    part = view[:, :, first:first + count]
    dims = [list(d) for d in part.ap]
    offset = part.offset + (count - 1) * dims[-1][0]
    dims[-1][0] = -dims[-1][0]
    return bass.AP(tensor=part.tensor, offset=offset, ap=dims)


def sorted_attention(nc, g, w, flag, no_flag, y):
    steps = list(sorting_steps())
    with ExitStack() as stack:
        sbuf = room(nc, stack)
        src = [sbuf(f"srt_src{u}", [P, S]) for u in range(2)]
        qT, kT = sbuf("srt_qT", [P, S]), sbuf("srt_kT", [P, S])
        v = [sbuf(f"srt_v{u}", [P, S]) for u in range(2)]
        scores = [sbuf(f"srt_scores{u}", [P, QT, S]) for u in range(2)]
        buf_a, buf_b, buf_c = (sbuf(f"srt_{n}", [P, QT, S]) for n in "abc")
        soft = sbuf("srt_soft", [P, QT, S])
        ones = sbuf("srt_ones", [P, S])
        weightsT = [sbuf(f"srt_weightsT{i}", [P, S]) for i in range(2)]
        minus_max, threshold, count = (sbuf(f"srt_{n}", [P, QT]) for n in ("minus_max", "threshold", "count"))
        inverse, offset = sbuf("srt_inverse", [P, QT]), sbuf("srt_offset", [P, QT])
        soft_sum, soft_scale = sbuf("srt_soft_sum", [P, QT]), sbuf("srt_soft_scale", [P, QT])
        s = signals(nc, stack, "src_copied", "qk_ready", "qk_copied", "v_ready", "v_copied", "scores_ready",
                    "scores_copied", "chain", "max_done", "shifted", "soft_done", "scale_done", "soft_scaled",
                    "weights_done", "turned", "turned_copied", "y_ready", "y_copied", "filled")
        n_chain = 2 * len(steps) + 1 + QT + 5 + QT + 3

        with nc.Block() as block:
            @block.gpsimd
            def _(pool):
                with pool.Fori(0, B // 2) as i:
                    for u in range(2):
                        nc.gpsimd.tensor_copy(src[u][:, :], g.xT[:, ds((i * 2 + u) * S, S)]).then_inc(s["src_copied"], 1)
                    hold(pool, s, s["v_ready"], i * 2 + 2)

            @block.tensor
            def _(pe):
                def front(b, u):
                    pe.wait_ge(s["src_copied"], b + 1)
                    pe.wait_ge(s["qk_copied"], b * 2 + 1)
                    nc.tensor.matmul(g.bank[0][:, :], w["q"][:, :], src[u][:, :], start=True,
                                     stop=True).then_inc(s["qk_ready"], 1)
                    nc.tensor.matmul(g.bank[1][:, :], w["k"][:, :], src[u][:, :], start=True,
                                     stop=True).then_inc(s["qk_ready"], 1)
                    pe.wait_ge(s["v_copied"], b + 1)
                    for t in range(QT):
                        ins = nc.tensor.matmul(g.bank[2][:, t * P:(t + 1) * P], src[u][:, t * P:(t + 1) * P],
                                               w["v"][:, :], start=True, stop=True)
                    ins.then_inc(s["v_ready"], 1)
                    pe.wait_ge(s["qk_copied"], b * 2 + 3)
                    for t in range(QT):
                        pe.wait_ge(s["scores_copied"], b * QT + (t + 1))
                        nc.tensor.matmul(g.bank[3 + t % 2][:, :], qT[:, t * P:(t + 1) * P], kT[:, :],
                                         start=True, stop=True).then_inc(s["scores_ready"], 1)

                def product(b, u, t):
                    pe.wait_ge(s["turned_copied"], b * QT + (t + 3))
                    if t == 0:
                        pe.wait_ge(s["y_copied"], b + 1)
                    for k in range(QT):
                        ins = nc.tensor.matmul(g.bank[7][:, t * P:(t + 1) * P],
                                               weightsT[t % 2][:, k * P:(k + 1) * P],
                                               v[u][:, k * P:(k + 1) * P], start=(k == 0), stop=(k == QT - 1))
                    ins.then_inc(s["y_ready"], 1)

                def turn(b, t):
                    if t == 0:
                        pe.wait_ge(s["weights_done"], b + 1)
                    pe.wait_ge(s["turned_copied"], b * QT + (t + 1))
                    for k in range(QT):
                        ins = nc.tensor.transpose(g.bank[5 + t % 2][:, k * P:(k + 1) * P],
                                                  buf_c[:, t, k * P:(k + 1) * P], g.ident[:, :])
                    ins.then_inc(s["turned"], 1)

                with pe.Fori(0, B // 2) as i:
                    for u in range(2):
                        front(i * 2 + u, u)
                    for u in range(2):
                        b = i * 2 + u
                        turn(b, 0)
                        for t in range(QT):
                            if t + 1 < QT:
                                turn(b, t + 1)
                            product(b, u, t)

            @block.scalar
            def _(act):
                def front(b, u):
                    for j, dst in enumerate((qT, kT)):
                        act.wait_ge(s["qk_ready"], b * 2 + (j + 1))
                        nc.scalar.activation(dst[:, :], g.bank[j][:, :], ACT.Copy).then_inc(s["qk_copied"], 1)
                    act.wait_ge(s["v_ready"], b + 1)
                    nc.scalar.activation(v[u][:, :], g.bank[2][:, :], ACT.Copy).then_inc(s["v_copied"], 1)
                    for t in range(QT):
                        act.wait_ge(s["scores_ready"], b * QT + (t + 1))
                        nc.scalar.activation(scores[u][:, t, :], g.bank[3 + t % 2][:, :], ACT.Copy,
                                             scale=1.0 / float(D) ** 0.5).then_inc(s["scores_copied"], 1)

                def middle(b, u):
                    act.wait_ge(s["max_done"], b + 1)
                    for t in range(QT):
                        nc.scalar.activation(scores[u][:, t, :], scores[u][:, t, :], ACT.Identity,
                                             bias=minus_max[:, t:t + 1]).then_inc(s["shifted"], 1)
                    act.wait_ge(s["shifted"], b * QT + QT)
                    for t in range(QT):
                        nc.scalar.activation(soft[:, t, :], scores[u][:, t, :], ACT.Exp,
                                             accum_out=soft_sum[:, t:t + 1]).then_inc(s["soft_done"], 1)
                    act.wait_ge(s["scale_done"], b * 2 + 2)
                    for t in range(QT):
                        nc.scalar.activation(soft[:, t, :], soft[:, t, :], ACT.Copy,
                                             scale=soft_scale[:, t:t + 1]).then_inc(s["soft_scaled"], 1)

                def back(b):
                    for t in range(QT):
                        act.wait_ge(s["turned"], b * QT + (t + 2))
                        act.wait_ge(s["y_ready"], b * QT + (t + 1))
                        nc.scalar.activation(weightsT[t % 2][:, :], g.bank[5 + t % 2][:, :],
                                             ACT.Copy).then_inc(s["turned_copied"], 1)
                    act.wait_ge(s["y_ready"], b * QT + (QT + 2))
                    nc.scalar.activation(y[:, ds(b * QT, QT), :], g.bank[7][:, :].rearrange("p (t d) -> p t d", t=QT),
                                         ACT.Copy).then_inc(s["y_copied"], 1)

                act.sem_inc(s["qk_copied"], 1)
                act.sem_inc(s["v_copied"], 1)
                act.sem_inc(s["scores_copied"], 2)
                act.sem_inc(s["turned_copied"], 2)
                act.sem_inc(s["y_copied"], 1)
                act.sem_inc(s["y_ready"], 2)
                with act.Fori(0, B // 2) as i:
                    for u in range(2):
                        front(i * 2 + u, u)
                    for u in range(2):
                        middle(i * 2 + u, u)
                        back(i * 2 + u)

            @block.vector
            def _(dve):
                def sort(b, u, step, chain):
                    src_buf, dst = scores[u], buf_a
                    for size, mirrored in steps:
                        half = size // 2
                        a = src_buf[:, :, :].rearrange("p t (n m) -> p (t n) m", m=size)
                        o = dst[:, :, :].rearrange("p t (n m) -> p (t n) m", m=size)
                        low, high = a[:, :, 0:half], a[:, :, half:size]
                        if mirrored:
                            low_back, high_back = backwards(a, 0, half), backwards(a, half, half)
                        else:
                            low_back, high_back = low, high
                        nc.vector.tensor_tensor(o[:, :, 0:half], low, high_back, ALU.max).then_inc(s["chain"], 1)
                        nc.vector.tensor_tensor(o[:, :, half:size], low_back, high, ALU.min).then_inc(s["chain"], 1)
                        chain.n += 2
                        dve.wait_ge(s["chain"], chain.before + chain.n)
                        src_buf, dst = dst, (buf_b if dst is buf_a else buf_a)
                    assert src_buf is buf_a

                nc.vector.memset(ones[:, :], 1.0).then_inc(s["filled"], 1)
                dve.wait_ge(s["filled"], 1)
                dve.sem_inc(s["soft_scaled"], 1)
                dve.sem_inc(s["turned"], 1)
                with dve.Fori(0, B // 2) as i:
                    for u in range(2):
                        b = i * 2 + u
                        chain = Chain(dve, s["chain"], b * n_chain)
                        step = chain.step
                        dve.wait_ge(s["scores_copied"], b * QT + (QT + 2))
                        sort(b, u, step, chain)
                        first = buf_a[:, :, 0]
                        dve.wait_ge(s["soft_scaled"], b * QT + 1)
                        nc.vector.tensor_scalar(minus_max[:, :], first, -1.0, None, ALU.mult).then_inc(s["max_done"], 1)
                        step(nc.vector.tensor_tensor(buf_b[:, :, :], buf_a[:, :, :],
                                                     first.unsqueeze(2).to_broadcast([P, QT, S]), ALU.subtract))
                        dve.wait_ge(s["turned"], b * QT + 1)
                        for t in range(QT):
                            step(nc.vector.tensor_tensor_scan(buf_c[:, t, :], ones[:, :], buf_b[:, t, :], 0.0,
                                                              ALU.mult, ALU.add))
                        step(nc.vector.tensor_scalar(threshold[:, :], buf_c[:, :, S - 1], -1.0, 1.0 / S,
                                                     ALU.add, ALU.mult))
                        step(nc.vector.tensor_tensor(buf_a[:, :, :], buf_b[:, :, :],
                                                     threshold[:, :].unsqueeze(2).to_broadcast([P, QT, S]), ALU.is_gt))
                        step(nc.vector.tensor_reduce(count[:, :], buf_a[:, :, :], AX.X, ALU.add))
                        step(nc.vector.reciprocal(inverse[:, :], count[:, :]))
                        step(nc.vector.tensor_tensor(offset[:, :], threshold[:, :], count[:, :], ALU.mult))
                        nc.vector.tensor_scalar(offset[:, :], offset[:, :], 1.0, None, ALU.add).then_inc(s["scale_done"], 1)
                        dve.wait_ge(s["scale_done"], b * 2 + 1)
                        for t in range(QT):
                            step(nc.vector.tensor_scalar(buf_b[:, t, :], buf_c[:, t, :], offset[:, t:t + 1],
                                                         inverse[:, t:t + 1], ALU.subtract, ALU.mult))
                        dve.wait_ge(s["soft_done"], b * QT + QT)
                        step(nc.vector.reciprocal(soft_scale[:, :], soft_sum[:, :]))
                        nc.vector.tensor_scalar(soft_scale[:, :], soft_scale[:, :], no_flag[:, 0:1], None,
                                                ALU.mult).then_inc(s["scale_done"], 1)
                        step(nc.vector.tensor_tensor(buf_a[:, :, :], scores[u][:, :, :], buf_b[:, :, :], ALU.subtract))
                        step(nc.vector.tensor_scalar(buf_a[:, :, :], buf_a[:, :, :], 0.0, flag[:, 0:1], ALU.max, ALU.mult))
                        dve.wait_ge(s["soft_scaled"], b * QT + (QT + 1))
                        nc.vector.tensor_tensor(buf_c[:, :, :], buf_a[:, :, :], soft[:, :, :],
                                                ALU.add).then_inc(s["weights_done"], 1)
                        dve.wait_ge(s["weights_done"], b + 1)
                        assert chain.n == n_chain, chain.n
        clear(nc, s)


def latent_attention_3(nc, g, io):
    HEADS, WIDE = 2, 64
    TILES = QT + 2
    SELF, ALL = S, S + CTX
    with ExitStack() as stack:
        sbuf = room(nc, stack)
        w_q, w_kv, w_out = sbuf("w_q", [P, D]), sbuf("w_kv", [P, 2 * D]), sbuf("w_out", [P, D])
        columns = sbuf("columns", [P, 6])
        q_scale = sbuf("q_scale", [P, 1])
        b_out = sbuf("b_out", [1, D])
        valid = sbuf("valid", [1, B * CTX], mybir.dt.uint8)
        key_bias = sbuf("key_bias", [1, B * CTX])
        context = sbuf("context", [P, B, 2, D])
        out = sbuf("heads_out", [P, NT, D])
        z = sbuf("lat_z", [P, TILES, D])
        stats, moments = sbuf("lat_stats", [P, TILES, 6]), sbuf("lat_moments", [P, TILES, 2])
        shifted, rstd = sbuf("lat_shifted", [P, TILES]), sbuf("lat_rstd", [P, TILES])
        zT = sbuf("lat_zT", [P, TILES * P])
        NG = (QT + TILES) * HEADS
        qk = sbuf("lat_qk", [P, QT + TILES, D])
        square = sbuf("lat_square", [P, QT + TILES, D])
        mean_sq, inv_rms, power = sbuf("lat_mean_sq", [P, NG]), sbuf("lat_inv_rms", [P, NG]), sbuf("lat_power", [P, NG])
        qkT = sbuf("lat_qkT", [P, (QT + TILES) * P])
        v = sbuf("lat_v", [P, TILES, HEADS, WIDE + 1])
        maxima, minus_max = sbuf("lat_maxima", [P, 2, 2]), sbuf("lat_minus_max", [P, 2])
        probs = [sbuf(f"lat_probs{u}", [P, ALL]) for u in range(2)]
        probsT = [sbuf(f"lat_probsT{u}", [P, TILES * P]) for u in range(2)]
        recip = sbuf("lat_recip", [P, 2])
        load(nc, g, [(w_q[:, :], io["L3_xattn_W_q"]), (w_kv[:, :], io["L3_xattn_W_kv"]),
                     (w_out[:, :], io["L3_xattn_W_out"]), (columns[:, :], io["L3_xattn_columns"]),
                     (b_out[:, :], io["L3_xattn_b_out"].unsqueeze(0)),
                     (valid[:, :], io["mask_BxS2_bk0"].rearrange("b s -> (b s)").unsqueeze(0)),
                     (context[:, :, 0, :], io["ctx_1024"][:, 0:P, :].rearrange("b p d -> p b d")),
                     (context[0:CTX - P, :, 1, :], io["ctx_1024"][:, P:CTX, :].rearrange("b p d -> p b d"))],
             ones=(v[:, :, :, :],))
        s = signals(nc, stack, "setup", "z_copied", "stats_done", "moments_done", "shift_done", "rstd_done",
                    "normal_done", "zT_ready", "zT_copied", "qkv_ready", "qk_copied", "v_copied", "square_chain",
                    "inv_done", "qk_scaled", "qkT_ready", "qkT_copied", "scores_ready", "max_done", "minus_done",
                    "exp_done", "probsT_ready", "probsT_copied", "out_ready", "recip_done", "out_done")
        UNITS = QT * HEADS
        with nc.Block() as block:
            @block.gpsimd
            def _(pool):
                nc.gpsimd.memset(power[:, :], -0.5).then_inc(s["setup"], 1)
                with pool.Fori(0, B) as b:
                    hold(pool, s, s["moments_done"], b * TILES + TILES)
                    nc.gpsimd.tensor_scalar(shifted[:, :], moments[:, :, 1], EPS, None, ALU.add).then_inc(s["shift_done"], 1)
                    hold(pool, s, s["shift_done"], b + 1)
                    nc.gpsimd.tensor_tensor(rstd[:, :], shifted[:, :], g.power[:, 0:TILES], ALU.pow).then_inc(s["rstd_done"], 1)
                    hold(pool, s, s["square_chain"], b * 3 + 3)
                    pool.wait_ge(s["setup"], 1)
                    nc.gpsimd.tensor_tensor(inv_rms[:, :], mean_sq[:, :], power[:, :], ALU.pow).then_inc(s["inv_done"], 1)

            @block.tensor
            def _(pe):
                def scores(n, i, b):
                    q, h, u = i // HEADS, i % HEADS, i % 2
                    rows_h = slice(h * WIDE, (h + 1) * WIDE)
                    pe.wait_ge(s["exp_done"], n * 2 + 2)
                    lhs = qkT[rows_h, q * P:(q + 1) * P]
                    nc.tensor.matmul(g.bank[2 * u][:, 0:SELF], lhs, qkT[rows_h, QT * P:2 * QT * P],
                                     start=True, stop=True)
                    nc.tensor.matmul(g.bank[2 * u + 1][:, 0:CTX], lhs, qkT[rows_h, 2 * QT * P:2 * QT * P + CTX],
                                     start=True, stop=False)
                    nc.tensor.matmul(g.bank[2 * u + 1][:, 0:CTX], g.ones[0:1, 0:P], key_bias[0:1, ds(b * CTX, CTX)],
                                     start=False, stop=True).then_inc(s["scores_ready"], 1)

                def back(n, i, b):
                    q, h, u = i // HEADS, i % HEADS, i % 2
                    pe.wait_ge(s["exp_done"], n * 2 + 6)
                    pe.wait_ge(s["probsT_copied"], n * 3 + 3)
                    for t in range(TILES):
                        kn = P if t < TILES - 1 else CTX - P
                        ins = nc.tensor.transpose(g.bank[4 + t // QT][0:kn, (t % QT) * P:(t % QT) * P + P],
                                                  probs[u][:, t * P:t * P + kn], g.ident[:, :])
                    ins.then_inc(s["probsT_ready"], 1)
                    pe.wait_ge(s["probsT_copied"], n * 3 + 6)
                    pe.wait_ge(s["out_done"], n + 1)
                    for t in range(TILES):
                        kn = P if t < TILES - 1 else CTX - P
                        ins = nc.tensor.matmul(g.bank[6 + u][:, 0:WIDE + 1], probsT[u][0:kn, t * P:(t + 1) * P],
                                               v[0:kn, t, h, :], start=(t == 0), stop=(t == TILES - 1))
                    ins.then_inc(s["out_ready"], 1)

                with pe.Fori(0, B) as b:
                    pe.wait_ge(s["normal_done"], b * TILES + TILES)
                    for t in range(TILES):
                        ins = nc.tensor.transpose(g.bank[t // QT][:, (t % QT) * P:(t % QT + 1) * P], z[:, t, :],
                                                  g.ident[:, :])
                    ins.then_inc(s["zT_ready"], 1)
                    pe.wait_ge(s["zT_copied"], b * 2 + 2)
                    for t in range(QT):
                        nc.tensor.matmul(g.bank[2][:, t * P:(t + 1) * P], zT[:, t * P:(t + 1) * P], w_q[:, :],
                                         start=True, stop=True)
                    for t in range(TILES):
                        c = slice((t % QT) * P, (t % QT + 1) * P)
                        nc.tensor.matmul(g.bank[3 + t // QT][:, c], zT[:, t * P:(t + 1) * P], w_kv[:, 0:D],
                                         start=True, stop=True)
                        ins = nc.tensor.matmul(g.bank[5 + t // QT][:, c], zT[:, t * P:(t + 1) * P], w_kv[:, D:2 * D],
                                               start=True, stop=True)
                    ins.then_inc(s["qkv_ready"], 1)
                    pe.wait_ge(s["qk_scaled"], b + 1)
                    pe.wait_ge(s["v_copied"], b * 2 + 2)
                    for t in range(QT + TILES):
                        ins = nc.tensor.transpose(g.bank[t // QT][:, (t % QT) * P:(t % QT + 1) * P], qk[:, t, :],
                                                  g.ident[:, :])
                    ins.then_inc(s["qkT_ready"], 1)
                    pe.wait_ge(s["qkT_copied"], b * 3 + 3)
                    pe.wait_ge(s["setup"], 3)
                    scores(b * UNITS, 0, b)
                    for i in range(UNITS):
                        if i + 1 < UNITS:
                            scores(b * UNITS + (i + 1), i + 1, b)
                        back(b * UNITS + i, i, b)
                    pe.wait_ge(s["out_done"], b * UNITS + (UNITS + 2))

            @block.scalar
            def _(act):
                act.sem_inc(s["exp_done"], 4)
                with act.Fori(0, B) as b:
                    act.wait_ge(s["zT_ready"], b + 1)
                    nc.scalar.activation(zT[:, 0:S], g.bank[0][:, :], ACT.Identity, bias=columns[:, 3:4],
                                         scale=columns[:, 2:3]).then_inc(s["zT_copied"], 1)
                    nc.scalar.activation(zT[:, S:TILES * P], g.bank[1][:, 0:2 * P], ACT.Identity, bias=columns[:, 1:2],
                                         scale=columns[:, 0:1]).then_inc(s["zT_copied"], 1)
                    act.wait_ge(s["qkv_ready"], b + 1)
                    for i, (t0, n) in enumerate(((0, QT), (QT, 2))):
                        nc.scalar.activation(v[:, t0:t0 + n, :, 0:WIDE],
                                             g.bank[5 + i][:, 0:n * P].rearrange("p (t h d) -> p t h d", t=n, h=HEADS),
                                             ACT.Copy).then_inc(s["v_copied"], 1)
                    act.wait_ge(s["qkT_ready"], b + 1)
                    act.wait_ge(s["setup"], 3)
                    nc.scalar.activation(qkT[:, 0:S], g.bank[0][:, :], ACT.Copy, scale=q_scale[:, 0:1]).then_inc(s["qkT_copied"], 1)
                    nc.scalar.activation(qkT[:, S:2 * S], g.bank[1][:, :], ACT.Copy, scale=columns[:, 5:6]).then_inc(s["qkT_copied"], 1)
                    nc.scalar.activation(qkT[:, 2 * S:2 * S + 2 * P], g.bank[2][:, 0:2 * P], ACT.Copy,
                                         scale=columns[:, 5:6]).then_inc(s["qkT_copied"], 1)
                    for i in range(UNITS):
                        u, n = i % 2, b * UNITS + i
                        act.wait_ge(s["minus_done"], n + 1)
                        act.wait_ge(s["probsT_ready"], n + 1)
                        nc.scalar.activation(probs[u][:, 0:SELF], g.bank[2 * u][:, 0:SELF], ACT.Exp,
                                             bias=minus_max[:, u:u + 1]).then_inc(s["exp_done"], 1)
                        nc.scalar.activation(probs[u][:, SELF:ALL], g.bank[2 * u + 1][:, 0:CTX], ACT.Exp,
                                             bias=minus_max[:, u:u + 1]).then_inc(s["exp_done"], 1)

            @block.vector
            def _(dve):
                nc.vector.tensor_scalar(key_bias[:, :], valid[:, :], 0.0, MASKED, ALU.is_equal, ALU.mult).then_inc(s["setup"], 1)
                nc.vector.tensor_scalar(q_scale[:, :], columns[:, 4:5], float(WIDE) ** -0.5, None, ALU.mult).then_inc(s["setup"], 1)
                dve.sem_inc(s["probsT_copied"], 3)
                dve.sem_inc(s["probsT_ready"], 2)
                dve.sem_inc(s["out_done"], 2)
                with dve.Fori(0, B) as b:
                    nc.vector.tensor_copy(z[:, 0:QT, :], g.x[:, ds(b * QT, QT), :]).then_inc(s["z_copied"], 1)
                    nc.vector.tensor_copy(z[:, QT, :], context[:, ds(b, 1), 0, :]).then_inc(s["z_copied"], 1)
                    nc.vector.memset(z[:, QT + 1, :], 0.0).then_inc(s["z_copied"], 1)
                    dve.wait_ge(s["z_copied"], b * 4 + 3)
                    nc.vector.tensor_copy(z[0:CTX - P, QT + 1, :], context[0:CTX - P, ds(b, 1), 1, :]).then_inc(s["z_copied"], 1)
                    hold(dve, s, s["z_copied"], b * 4 + 4)
                    for t in range(TILES):
                        nc.vector.bn_stats(stats[:, t, :], z[:, t, :]).then_inc(s["stats_done"], 1)
                    hold(dve, s, s["stats_done"], b * TILES + TILES)
                    for t in range(TILES):
                        nc.vector.bn_aggr(moments[:, t, :], stats[:, t, :]).then_inc(s["moments_done"], 1)
                    dve.wait_ge(s["moments_done"], b * TILES + TILES)
                    dve.wait_ge(s["rstd_done"], b + 1)
                    for t in range(TILES):
                        nc.vector.tensor_scalar(z[:, t, :], z[:, t, :], moments[:, t, 0:1], rstd[:, t:t + 1],
                                                ALU.subtract, ALU.mult).then_inc(s["normal_done"], 1)
                    dve.wait_ge(s["qkv_ready"], b + 1)
                    for i, (t0, n) in enumerate(((0, QT), (QT, QT), (2 * QT, 2))):
                        nc.vector.tensor_copy(qk[:, t0:t0 + n, :],
                                              g.bank[2 + i][:, 0:n * P].rearrange("p (t d) -> p t d", t=n)
                                              ).then_inc(s["qk_copied"], 1)
                    dve.wait_ge(s["qk_copied"], b * 3 + 3)
                    step = Chain(dve, s["square_chain"], b * 3).step
                    step(nc.vector.tensor_tensor(square[:, :, :], qk[:, :, :], qk[:, :, :], ALU.mult))
                    step(nc.vector.tensor_reduce(mean_sq[:, :], square[:, :, :].rearrange(
                        "p t (h d) -> p (t h) d", h=HEADS), AX.X, ALU.add))
                    step(nc.vector.tensor_scalar(mean_sq[:, :], mean_sq[:, :], 1.0 / WIDE, 1e-16, ALU.mult, ALU.max))
                    dve.wait_ge(s["inv_done"], b + 1)
                    view = qk[:, :, :].rearrange("p t (h d) -> p (t h) d", h=HEADS)
                    nc.vector.tensor_tensor(view, view, inv_rms[:, :].unsqueeze(2).to_broadcast([P, NG, WIDE]),
                                            ALU.mult).then_inc(s["qk_scaled"], 1)

                    def maximum(i):
                        u, n = i % 2, b * UNITS + i
                        dve.wait_ge(s["scores_ready"], n + 1)
                        dve.wait_ge(s["exp_done"], n * 2 + 2)
                        nc.vector.tensor_reduce(maxima[:, u, 0:1], g.bank[2 * u][:, 0:SELF], AX.X, ALU.max).then_inc(s["max_done"], 1)
                        nc.vector.tensor_reduce(maxima[:, u, 1:2], g.bank[2 * u + 1][:, 0:CTX], AX.X, ALU.max).then_inc(s["max_done"], 1)
                        dve.wait_ge(s["max_done"], n * 2 + 2)
                        nc.vector.tensor_reduce(minus_max[:, u:u + 1], maxima[:, u, :], AX.X, ALU.max,
                                                negate=True).then_inc(s["minus_done"], 1)

                    maximum(0)
                    for i in range(UNITS):
                        q, h, u, n = i // HEADS, i % HEADS, i % 2, b * UNITS + i
                        if i + 1 < UNITS:
                            maximum(i + 1)
                        dve.wait_ge(s["probsT_ready"], n + 3)
                        nc.vector.tensor_copy(probsT[u][:, 0:S], g.bank[4][:, :]).then_inc(s["probsT_copied"], 1)
                        nc.vector.tensor_copy(probsT[u][:, S:S + P], g.bank[5][:, 0:P]).then_inc(s["probsT_copied"], 1)
                        nc.vector.tensor_copy(probsT[u][0:CTX - P, S + P:S + 2 * P],
                                              g.bank[5][0:CTX - P, P:2 * P]).then_inc(s["probsT_copied"], 1)
                        dve.wait_ge(s["out_ready"], n + 1)
                        nc.vector.reciprocal(recip[:, u:u + 1], g.bank[6 + u][:, WIDE:WIDE + 1]).then_inc(s["recip_done"], 1)
                        dve.wait_ge(s["recip_done"], n + 1)
                        nc.vector.tensor_scalar(out[:, ds(b * QT + q, 1), h * WIDE:(h + 1) * WIDE],
                                                g.bank[6 + u][:, 0:WIDE], recip[:, u:u + 1], None,
                                                ALU.mult).then_inc(s["out_done"], 1)
        clear(nc, s)
        finish(nc, g, "heads", out, w_out, b_out)


def local_attention_layers_3(nc, g, io):
    LAYERS, HEADS, WIDE = 6, 16, 64
    HP = HEADS * WIDE // P
    QK, QKV = 2 * P, 3 * P
    INNER = 341
    CHUNKS = [(c, min(P, INNER - c)) for c in range(0, INNER, P)]
    NC = len(CHUNKS)
    KEYS = WINDOW + P
    SPAN = 2 * P
    PACK = 2 * INNER + NC * P + 2 * NC + 3
    half = WIDE // 2
    with ExitStack() as stack:
        sbuf = room(nc, stack)
        yT = sbuf("loc_yT", [P, T])
        y_b = sbuf("loc_y_b", [P, S])
        xs = sbuf("loc_shifted", [P, S])
        w_qkv, w_o = sbuf("loc_w_qkv", [P, HP * QKV]), sbuf("loc_w_o", [P, HP * P])
        scales, pack = sbuf("loc_scales", [P, 2 * QK]), sbuf("loc_pack", [P, PACK])
        base = sbuf("loc_base", [P, 2, QT, QK])
        table = sbuf("loc_table", [P, 2, QT, QK])
        square = sbuf("loc_square", [P, QT, QK])
        turned_q = sbuf("loc_cos_part", [P, QT, QK])
        sin_part = sbuf("loc_sin_part", [P, QT, QK])
        rotated = sbuf("loc_rotated", [P, QT, QK])
        norm_sq, floored = sbuf("loc_norm_sq", [P, QT * 4]), sbuf("loc_floored", [P, QT * 4])
        inv_norm = sbuf("loc_inv_norm", [P, QT * 4])
        qT = sbuf("loc_qT", [P, S])
        kT = sbuf("loc_kT", [P, 2, WINDOW + S])
        v = sbuf("loc_v", [P, (1 + QT) * P])
        minus_max = sbuf("loc_minus_max", [P, 2, 2])
        sums, recip = sbuf("loc_sums", [P, QT, 2]), sbuf("loc_recip", [P, QT, 2])
        probs = [sbuf(f"loc_probs{u}", [P, 2, SPAN]) for u in range(2)]
        probsT = [sbuf(f"loc_probsT{u}", [P, 2 * SPAN]) for u in range(2)]
        heads = sbuf("loc_heads", [P, S])
        headsT = sbuf("loc_headsT", [P, HP * S])
        stats, moments = sbuf("loc_stats", [P, QT, 6]), sbuf("loc_moments", [P, QT, 2])
        shift, rstd = sbuf("loc_shift", [P, QT]), sbuf("loc_rstd", [P, QT])
        z, zT = sbuf("loc_z", [P, QT, D]), sbuf("loc_zT", [P, S])
        gate = [sbuf(f"loc_gate{c}", [P, S]) for c in range(NC)]
        inner = [sbuf(f"loc_inner{c}", [P, S]) for c in range(NC)]
        W2_AT = 2 * INNER
        B1_AT = W2_AT + NC * P
        G_AT = B1_AT + 2 * NC
        load(nc, g, [(base[:, :, :, :], io["c_rotary"])],
             zeros=(kT[:, :, :], v[:, 0:P], probs[0][:, :, :], probs[1][:, :, :], xs[:, 0:1]))

        s = signals(nc, stack, "qkv_loaded", "scales_loaded", "o_loaded", "pack_loaded", "qkv_used",
                    "state_ready", "table_done", "y_b_copied", "xs_done", "qk_ready", "v_ready", "squared",
                    "rotary_done", "floored_done", "inverse_done", "summed", "rotated_done", "qT_ready",
                    "kT_ready", "qT_copied", "kT_copied", "v_copied", "scores_ready", "minus_done", "exp_done",
                    "probsT_ready", "even_copied", "odd_copied", "values_done", "recip_done", "heads_done",
                    "headsT_ready", "headsT_copied", "o_ready", "y_mid_done", "shift_ready", "stats_done",
                    "moments_done", "eps_done", "rstd_done", "z_done", "zT_ready", "zT_copied", "hidden_ready",
                    "gelu_done", "inner_done", "f_ready", "y_done")

        with nc.Block() as block:
            @block.sync
            def _(sp):
                with sp.Fori(0, LAYERS) as layer:
                    sp.wait_ge(s["table_done"], layer * 2 + 1)
                    sp.dma_start(scales[:, :], io["L3_ffn_scales"][ds(layer, 1)]).then_inc(s["scales_loaded"], 16)
                    sp.wait_ge(s["qkv_used"], layer * B + 1)
                    sp.dma_start(w_qkv[:, :], io["L3_ffn_Wqkv"][ds(layer, 1)]).then_inc(s["qkv_loaded"], 16)
                    sp.wait_ge(s["o_ready"], layer * B + 1)
                    sp.dma_start(w_o[:, :], io["L3_ffn_Wo"][ds(layer, 1)]).then_inc(s["o_loaded"], 16)
                    sp.wait_ge(s["y_done"], layer * B + 1)
                    sp.dma_start(pack[:, :], io["L3_ffn_pack"][ds(layer, 1)]).then_inc(s["pack_loaded"], 16)

            @block.gpsimd
            def _(pool):
                with pool.Fori(0, LAYERS * B) as k:
                    with pool.Fori(0, HP) as hp:
                        for j in range(2):
                            n = k * HP + hp
                            part = slice(8 * j, 8 * j + 8)
                            hold(pool, s, s["rotary_done"], n * 6 + (3 * j + 3 + 6))
                            nc.gpsimd.tensor_scalar(floored[:, part], norm_sq[:, part], 1e-24, None,
                                                    ALU.max).then_inc(s["floored_done"], 1)
                            hold(pool, s, s["floored_done"], n * 2 + (j + 1))
                            nc.gpsimd.tensor_tensor(inv_norm[:, part], floored[:, part], g.power[:, 0:8],
                                                    ALU.pow).then_inc(s["inverse_done"], 1)
                    hold(pool, s, s["moments_done"], k * QT + QT)
                    nc.gpsimd.tensor_scalar(shift[:, :], moments[:, :, 1], EPS, None, ALU.add).then_inc(s["eps_done"], 1)
                    hold(pool, s, s["eps_done"], k + 1)
                    nc.gpsimd.tensor_tensor(rstd[:, :], shift[:, :], g.power[:, 0:QT], ALU.pow).then_inc(s["rstd_done"], 1)

            @block.tensor
            def _(pe):
                def qkv(n, hp, j):
                    pe.wait_ge(s["rotary_done"], n * 6 + (3 * j + 3))
                    if j == 0:
                        pe.wait_ge(s["v_copied"], n + 1)
                    for t in (2 * j, 2 * j + 1):
                        lhs = xs[:, t * P:(t + 1) * P]
                        ins = nc.tensor.matmul(g.bank[j][:, (t % 2) * QK:(t % 2 + 1) * QK], lhs,
                                               w_qkv[:, ds(hp * QKV, QK)], start=True, stop=True)
                    ins.then_inc(s["qk_ready"], 1)
                    for t in (2 * j, 2 * j + 1):
                        lhs = xs[:, t * P:(t + 1) * P]
                        ins = nc.tensor.matmul(g.bank[2][:, t * P:(t + 1) * P], lhs,
                                               w_qkv[:, ds(hp * QKV + QK, P)], start=True, stop=True)
                    if j == 1:
                        ins.then_inc(s["v_ready"], 1)

                def turn_qk(n):
                    pe.wait_ge(s["rotated_done"], n * 2 + 2)
                    for t in range(QT):
                        ins = nc.tensor.transpose(g.bank[3][:, t * P:(t + 1) * P], rotated[:, t, 0:P], g.ident[:, :])
                    ins.then_inc(s["qT_ready"], 1)
                    for t in range(QT):
                        ins = nc.tensor.transpose(g.bank[4][:, t * P:(t + 1) * P], rotated[:, t, P:QK], g.ident[:, :])
                    ins.then_inc(s["kT_ready"], 1)

                def scores(n, t):
                    pe.wait_ge(s["exp_done"], n * 8 + (2 * t + 2))
                    if t == 0:
                        pe.wait_ge(s["qT_copied"], n + 1)
                        pe.wait_ge(s["kT_copied"], n * 2 + 2)
                    bank = g.bank[4 + t % 2]
                    dst = bank[:, 0:2 * KEYS].rearrange("p (h j) -> p h j", h=2)
                    nc.tensor.matmul(dst, qT[:, t * P:(t + 1) * P], kT[:, :, t * P:t * P + KEYS],
                                     start=True, stop=False)
                    nc.tensor.matmul(dst, g.ident_bf[:, :], g.band[:, 0 if t else 1, :, :],
                                     start=False, stop=True).then_inc(s["scores_ready"], 1)

                def turn_probs(n, t):
                    pe.wait_ge(s["exp_done"], n * 8 + (2 * t + 2 + 4))
                    pe.wait_ge(s["odd_copied"] if t % 2 else s["even_copied"], n * 2 + (t // 2 + 1))
                    if t == 0:
                        pe.wait_ge(s["headsT_copied"], n + 1)
                    bank = g.bank[3 if t % 2 else 6]
                    for h in range(2):
                        for i in range(2):
                            ins = nc.tensor.transpose(bank[:, (2 * h + i) * P:(2 * h + i + 1) * P],
                                                      probs[t % 2][:, h, i * P:(i + 1) * P], g.ident[:, :])
                    ins.then_inc(s["probsT_ready"], 1)

                def values(n, t):
                    pe.wait_ge(s["odd_copied"] if t % 2 else s["even_copied"], n * 2 + (t // 2 + 2))
                    if t == 0:
                        pe.wait_ge(s["heads_done"], n + 1)
                        pe.wait_ge(s["v_copied"], n + 2)
                    for h in range(2):
                        for i in range(2):
                            ins = nc.tensor.matmul(g.bank[7][:, t * P + h * WIDE:t * P + (h + 1) * WIDE],
                                                   probsT[t % 2][:, (2 * h + i) * P:(2 * h + i + 1) * P],
                                                   v[:, (t + i) * P + h * WIDE:(t + i) * P + (h + 1) * WIDE],
                                                   start=(i == 0), stop=(i == 1), skip_group_check=True)
                    ins.then_inc(s["values_done"], 1)

                def turn_heads(n):
                    pe.wait_ge(s["heads_done"], n + 2)
                    for t in range(QT):
                        ins = nc.tensor.transpose(g.bank[6][:, t * P:(t + 1) * P], heads[:, t * P:(t + 1) * P],
                                                  g.ident[:, :])
                    ins.then_inc(s["headsT_ready"], 1)

                def pair(n, hp, more):
                    scores(n, 0)
                    if more:
                        qkv(n + 1, hp + 1, 0)
                    scores(n, 1)
                    if more:
                        qkv(n + 1, hp + 1, 1)
                    turn_probs(n, 0)
                    scores(n, 2)
                    turn_probs(n, 1)
                    values(n, 0)
                    scores(n, 3)
                    values(n, 1)
                    turn_probs(n, 2)
                    turn_probs(n, 3)
                    values(n, 2)
                    values(n, 3)
                    if more:
                        turn_qk(n + 1)
                    turn_heads(n)

                def feed_forward(k):
                    pe.wait_ge(s["xs_done"], k * 4 + 4)
                    for t in range(QT):
                        ins = nc.tensor.transpose(g.bank[1][:, t * P:(t + 1) * P], xs[:, t * P:(t + 1) * P], g.ident[:, :])
                    ins.then_inc(s["shift_ready"], 1)
                    pe.wait_ge(s["z_done"], k * QT + QT)
                    for t in range(QT):
                        ins = nc.tensor.transpose(g.bank[2][:, t * P:(t + 1) * P], z[:, t, :], g.ident[:, :])
                    ins.then_inc(s["zT_ready"], 1)
                    pe.wait_ge(s["zT_copied"], k + 1)
                    for c, (first, width) in enumerate(CHUNKS):
                        for bank, at in ((g.bank[(6, 7, 0)[c]], INNER), (g.bank[3 + c], 0)):
                            nc.tensor.matmul(bank[0:width, :], pack[:, at + first:at + first + width], zT[:, :],
                                             start=True, stop=True).then_inc(s["hidden_ready"], 1)
                    for c, (first, width) in enumerate(CHUNKS):
                        pe.wait_ge(s["inner_done"], k * NC + (c + 1))
                        ins = nc.tensor.matmul(g.bank[1][:, :], pack[0:width, W2_AT + c * P:W2_AT + (c + 1) * P],
                                               inner[c][0:width, :], start=(c == 0), stop=(c == NC - 1))
                    ins.then_inc(s["f_ready"], 1)

                pe.sem_inc(s["qkv_used"], 1)
                pe.sem_inc(s["o_ready"], 1)
                pe.sem_inc(s["values_done"], 4)
                with pe.Fori(0, LAYERS) as layer:
                    pe.wait_ge(s["qkv_loaded"], layer * 16 + 16)
                    pe.wait_ge(s["o_loaded"], layer * 16 + 16)
                    hold(pe, s, s["pack_loaded"], layer * 16 + 16)
                    with pe.Fori(0, B) as b:
                        k = layer * B + b
                        pe.wait_ge(s["xs_done"], k * 4 + 2)
                        qkv(k * HP, 0, 0)
                        qkv(k * HP, 0, 1)
                        turn_qk(k * HP)
                        with pe.Fori(0, HP - 1) as hp:
                            pair(k * HP + hp, hp, True)
                        pe.sem_inc(s["qkv_used"], 1)
                        pair(k * HP + (HP - 1), HP - 1, False)
                        pe.wait_ge(s["headsT_copied"], k * HP + (HP + 1))
                        for hp in range(HP):
                            ins = nc.tensor.matmul(g.bank[0][:, :], w_o[:, hp * P:(hp + 1) * P],
                                                   headsT[:, hp * S:(hp + 1) * S], start=(hp == 0), stop=(hp == HP - 1))
                        ins.then_inc(s["o_ready"], 1)
                        feed_forward(k)

            @block.scalar
            def _(act):
                def square_part(n, j):
                    act.wait_ge(s["qk_ready"], n * 2 + (j + 1))
                    nc.scalar.activation(square[:, 2 * j:2 * j + 2, :].rearrange("p t d -> p (t d)"), g.bank[j][:, :],
                                         ACT.Square).then_inc(s["squared"], 1)

                def copies(n):
                    act.wait_ge(s["v_ready"], n + 1)
                    act.wait_ge(s["values_done"], n * 4 + 4)
                    nc.scalar.activation(v[:, P:(1 + QT) * P], g.bank[2][:, :], ACT.Copy).then_inc(s["v_copied"], 1)
                    act.wait_ge(s["qT_ready"], n + 1)
                    nc.scalar.activation(qT[:, :], g.bank[3][:, :], ACT.Copy).then_inc(s["qT_copied"], 1)
                    act.wait_ge(s["kT_ready"], n + 1)
                    nc.scalar.activation(kT[WIDE:P, 1, WINDOW:WINDOW + S], g.bank[4][WIDE:P, :],
                                         ACT.Copy).then_inc(s["kT_copied"], 1)

                def exps(n, t):
                    act.wait_ge(s["minus_done"], n * 4 + (t + 1))
                    for h in range(2):
                        nc.scalar.activation(probs[t % 2][:, h, P - WINDOW:SPAN],
                                             g.bank[4 + t % 2][:, h * KEYS:(h + 1) * KEYS], ACT.Exp,
                                             bias=minus_max[:, t % 2, h:h + 1],
                                             accum_out=sums[:, t, h:h + 1]).then_inc(s["exp_done"], 1)

                def odd_copy(n, t):
                    act.wait_ge(s["probsT_ready"], n * 4 + (t + 1))
                    act.wait_ge(s["values_done"], n * 4 + (t + 3))
                    nc.scalar.activation(probsT[1][:, :], g.bank[3][:, :], ACT.Copy).then_inc(s["odd_copied"], 1)

                def pair(n, hp, more):
                    exps(n, 0)
                    if more:
                        square_part(n + 1, 0)
                    exps(n, 1)
                    if more:
                        square_part(n + 1, 1)
                    exps(n, 2)
                    odd_copy(n, 1)
                    exps(n, 3)
                    odd_copy(n, 3)
                    if more:
                        copies(n + 1)
                    act.wait_ge(s["headsT_ready"], n + 1)
                    nc.scalar.activation(headsT[:, ds(hp * S, S)], g.bank[6][:, :], ACT.Copy).then_inc(s["headsT_copied"], 1)

                act.sem_inc(s["v_copied"], 1)
                act.sem_inc(s["exp_done"], 4)
                act.sem_inc(s["odd_copied"], 1)
                act.sem_inc(s["headsT_copied"], 1)
                with act.Fori(0, LAYERS) as layer:
                    with act.Fori(0, B) as b:
                        k = layer * B + b
                        act.wait_ge(s["y_done"], k + 1)
                        act.wait_ge(s["state_ready"], 1)
                        nc.scalar.activation(xs[0:64, :], yT[0:64, ds(b * S, S)], ACT.Copy).then_inc(s["xs_done"], 1)
                        nc.scalar.activation(y_b[:, :], yT[:, ds(b * S, S)], ACT.Copy).then_inc(s["y_b_copied"], 1)
                        square_part(k * HP, 0)
                        square_part(k * HP, 1)
                        copies(k * HP)
                        with act.Fori(0, HP - 1) as hp:
                            pair(k * HP + hp, hp, True)
                        pair(k * HP + (HP - 1), HP - 1, False)
                        act.wait_ge(s["y_mid_done"], k + 1)
                        nc.scalar.activation(xs[0:64, :], y_b[0:64, :], ACT.Copy).then_inc(s["xs_done"], 1)
                        act.wait_ge(s["zT_ready"], k + 1)
                        nc.scalar.activation(zT[:, :], g.bank[2][:, :], ACT.Identity, bias=pack[:, G_AT + 1:G_AT + 2],
                                             scale=pack[:, G_AT:G_AT + 1]).then_inc(s["zT_copied"], 1)
                        for c, (first, width) in enumerate(CHUNKS):
                            act.wait_ge(s["hidden_ready"], k * 2 * NC + (2 * c + 1))
                            nc.scalar.activation(gate[c][0:width, :], g.bank[(6, 7, 0)[c]][0:width, :], ACT.Gelu,
                                                 bias=pack[0:width, B1_AT + NC + c:B1_AT + NC + c + 1]
                                                 ).then_inc(s["gelu_done"], 1)

            @block.vector
            def _(dve):
                def groups(view):
                    return view.rearrange("p t (e d) -> p (t e) d", d=WIDE)

                def rotary(n, j):
                    tiles, part = slice(2 * j, 2 * j + 2), slice(8 * j, 8 * j + 8)
                    dve.wait_ge(s["qk_ready"], n * 2 + (j + 1))
                    dve.wait_ge(s["squared"], n * 2 + (j + 1))
                    nc.vector.tensor_tensor(turned_q[:, tiles, :], g.bank[j][:, :].rearrange("p (t d) -> p t d", t=2),
                                            table[:, 0, tiles, :], ALU.mult).then_inc(s["rotary_done"], 1)
                    src = g.bank[j][:, :].rearrange("p (e two d) -> p e two d", two=2, d=half)[:, :, ::-1, :]
                    nc.vector.tensor_tensor(
                        sin_part[:, tiles, :].rearrange("p t (e two d) -> p (t e) two d", two=2, d=half), src,
                        table[:, 1, tiles, :].rearrange("p t (e two d) -> p (t e) two d", two=2, d=half),
                        ALU.mult).then_inc(s["rotary_done"], 1)
                    nc.vector.tensor_reduce(norm_sq[:, part], groups(square[:, tiles, :]), AX.X,
                                            ALU.add).then_inc(s["rotary_done"], 1)

                def add_parts(n, j):
                    tiles = slice(2 * j, 2 * j + 2)
                    dve.wait_ge(s["rotary_done"], n * 6 + (3 * j + 3 + 6))
                    nc.vector.tensor_tensor(turned_q[:, tiles, :], turned_q[:, tiles, :], sin_part[:, tiles, :],
                                            ALU.add).then_inc(s["summed"], 1)

                def normalise(n, j):
                    tiles, part = slice(2 * j, 2 * j + 2), slice(8 * j, 8 * j + 8)
                    dve.wait_ge(s["summed"], n * 2 + (j + 1))
                    dve.wait_ge(s["inverse_done"], n * 2 + (j + 1))
                    nc.vector.tensor_tensor(groups(rotated[:, tiles, :]), groups(turned_q[:, tiles, :]),
                                            inv_norm[:, part].unsqueeze(2).to_broadcast([P, 8, WIDE]),
                                            ALU.mult).then_inc(s["rotated_done"], 1)

                def keys_copy(n):
                    dve.wait_ge(s["kT_ready"], n + 1)
                    nc.vector.tensor_copy(kT[0:WIDE, 0, WINDOW:WINDOW + S], g.bank[4][0:WIDE, :]).then_inc(s["kT_copied"], 1)

                def maximum(n, t):
                    dve.wait_ge(s["scores_ready"], n * 4 + (t + 1))
                    nc.vector.tensor_reduce(minus_max[:, t % 2, :],
                                            g.bank[4 + t % 2][:, 0:2 * KEYS].rearrange("p (h j) -> p h j", h=2),
                                            AX.X, ALU.max, negate=True).then_inc(s["minus_done"], 1)

                def even_copy(n, t):
                    dve.wait_ge(s["probsT_ready"], n * 4 + (t + 1))
                    dve.wait_ge(s["values_done"], n * 4 + (t + 3))
                    nc.vector.tensor_copy(probsT[0][:, :], g.bank[6][:, :]).then_inc(s["even_copied"], 1)

                def heads_out(n):
                    dve.wait_ge(s["values_done"], n * 4 + 8)
                    dve.wait_ge(s["exp_done"], n * 8 + 12)
                    nc.vector.reciprocal(recip[:, :, :], sums[:, :, :]).then_inc(s["recip_done"], 1)
                    dve.wait_ge(s["recip_done"], n + 1)
                    nc.vector.tensor_tensor(heads[:, :].rearrange("p (e d) -> p e d", d=WIDE),
                                            g.bank[7][:, :].rearrange("p (e d) -> p e d", d=WIDE),
                                            recip[:, :, :].rearrange("p t h -> p (t h)").unsqueeze(2)
                                            .to_broadcast([P, 2 * QT, WIDE]), ALU.mult).then_inc(s["heads_done"], 1)

                def pair(n, more):
                    maximum(n, 0)
                    if more:
                        rotary(n + 1, 0)
                    maximum(n, 1)
                    if more:
                        add_parts(n + 1, 0)
                    even_copy(n, 0)
                    maximum(n, 2)
                    if more:
                        rotary(n + 1, 1)
                    maximum(n, 3)
                    if more:
                        add_parts(n + 1, 1)
                        normalise(n + 1, 0)
                    even_copy(n, 2)
                    if more:
                        normalise(n + 1, 1)
                    heads_out(n)
                    if more:
                        keys_copy(n + 1)
                        dve.wait_ge(s["rotated_done"], n * 2 + 4)
                    dve.wait_ge(s["heads_done"], n + 2)

                dve.sem_inc(s["table_done"], 1)
                dve.sem_inc(s["y_done"], 1)
                dve.sem_inc(s["rotary_done"], 6)
                dve.sem_inc(s["even_copied"], 1)
                dve.sem_inc(s["heads_done"], 1)
                nc.vector.tensor_copy(yT[:, :], g.xT[:, :]).then_inc(s["state_ready"], 1)
                dve.wait_ge(s["state_ready"], 1)
                with dve.Fori(0, LAYERS) as layer:
                    dve.wait_ge(s["scales_loaded"], layer * 16 + 16)
                    for i in range(2):
                        nc.vector.tensor_tensor(table[:, i], base[:, i],
                                                scales[:, i * QK:(i + 1) * QK].unsqueeze(1).to_broadcast([P, QT, QK]),
                                                ALU.mult).then_inc(s["table_done"], 1)
                    hold(dve, s, s["table_done"], layer * 2 + 3)
                    with dve.Fori(0, B) as b:
                        k = layer * B + b
                        dve.wait_ge(s["y_done"], k + 1)
                        nc.vector.tensor_copy(xs[64:P, 1:S], yT[64:P, ds(b * S, S - 1)]).then_inc(s["xs_done"], 1)
                        for j in range(2):
                            rotary(k * HP, j)
                        for j in range(2):
                            add_parts(k * HP, j)
                        for j in range(2):
                            normalise(k * HP, j)
                        keys_copy(k * HP)
                        hold(dve, s, s["rotated_done"], k * (2 * HP) + 2)
                        with dve.Fori(0, HP - 1) as hp:
                            pair(k * HP + hp, True)
                        pair(k * HP + (HP - 1), False)
                        dve.wait_ge(s["o_ready"], k + 2)
                        dve.wait_ge(s["y_b_copied"], k + 1)
                        nc.vector.tensor_tensor(y_b[:, :], y_b[:, :], g.bank[0][:, :], ALU.add).then_inc(s["y_mid_done"], 1)
                        dve.wait_ge(s["y_mid_done"], k + 1)
                        nc.vector.tensor_copy(xs[64:P, 1:S], y_b[64:P, 0:S - 1]).then_inc(s["xs_done"], 1)
                        dve.wait_ge(s["shift_ready"], k + 1)
                        for t in range(QT):
                            nc.vector.bn_stats(stats[:, t, :], g.bank[1][:, t * P:(t + 1) * P]).then_inc(s["stats_done"], 1)
                        hold(dve, s, s["stats_done"], k * QT + QT)
                        for t in range(QT):
                            nc.vector.bn_aggr(moments[:, t, :], stats[:, t, :]).then_inc(s["moments_done"], 1)
                        dve.wait_ge(s["moments_done"], k * QT + QT)
                        dve.wait_ge(s["rstd_done"], k + 1)
                        for t in range(QT):
                            nc.vector.tensor_scalar(z[:, t, :], g.bank[1][:, t * P:(t + 1) * P], moments[:, t, 0:1],
                                                    rstd[:, t:t + 1], ALU.subtract, ALU.mult).then_inc(s["z_done"], 1)
                        for c, (first, width) in enumerate(CHUNKS):
                            dve.wait_ge(s["gelu_done"], k * NC + (c + 1))
                            dve.wait_ge(s["hidden_ready"], k * (2 * NC) + (2 * c + 2))
                            nc.vector.scalar_tensor_tensor(inner[c][0:width, :], g.bank[3 + c][0:width, :],
                                                           pack[0:width, B1_AT + c:B1_AT + c + 1],
                                                           gate[c][0:width, :], ALU.add, ALU.mult).then_inc(s["inner_done"], 1)
                        dve.wait_ge(s["f_ready"], k + 1)
                        nc.vector.scalar_tensor_tensor(yT[:, ds(b * S, S)], g.bank[1][:, :], pack[:, G_AT + 2:G_AT + 3],
                                                       y_b[:, :], ALU.add, ALU.add).then_inc(s["y_done"], 1)
        clear(nc, s)
        finish(nc, g, "transposed", yT)


SUBLAYERS = (sparse_or_soft_attention_0, context_attention_0, grouped_experts_0, causal_attention_1, remembered_attention_1, fixed_experts_1, differential_attention_2, context_attention_2, limited_experts_2, linear_attention_3, latent_attention_3, local_attention_layers_3)


def build(nc, io, out):
    _USED.clear()
    with ExitStack() as stack:
        g = open_chip(nc, stack)
        load_chip(nc, g, io)
        for n, sublayer in enumerate(SUBLAYERS):
            if n in STAGES:
                sublayer(nc, g, io)
        s = signals(nc, stack, "stored")
        with nc.Block() as block:
            @block.sync
            def _(sp):
                sp.dma_start(out.rearrange("b (t p) d -> p (b t) d", p=P), g.x[:, :, :]).then_inc(s["stored"], 16)
                sp.wait_ge(s["stored"], 16)



_TURNED = ("L0_xattn_w_q", "L0_xattn_w_k", "L0_xattn_w_v", "L0_xattn_w_o",
           "L1_attn_q_proj_weight", "L1_attn_k_proj_weight", "L1_attn_v_proj_weight", "L1_attn_o_proj_weight",
           "L1_xattn_Wq", "L1_xattn_Wc", "L0_ffn_gate_weight", "L3_attn_Wqkv", "L3_attn_Wproj",
           "L0_attn_Wq", "L0_attn_Wk", "L0_attn_Wv")


def _constants(np):
    c = {"c_ident": np.eye(P, dtype=np.float32)}
    for name, pieces in (("c_select_q", Q_PIECES), ("c_select_k", K_PIECES)):
        sel = np.zeros((P, 3, PAIRS, P), np.float32)
        for a in range(PAIRS):
            for e in range(2):
                for p, part in enumerate(pieces):
                    for d in range(DH):
                        sel[(2 * a + e) * DH + d, part, a, 64 * e + DH * p + d] = 1
        c[name] = sel.reshape(P, 3, PAIRS * P)
    ones = np.zeros((1, P), np.float32)
    top = np.zeros((6, P), np.float32)
    for e in range(2):
        for part in range(3):
            ones[0, 64 * e + MAX_ROW + part] = 1
            top[2 * part + e, 64 * e + MAX_ROW + part] = 1
    c["c_ones_pattern"], c["c_max_pattern"] = ones, top
    later = np.triu(np.full((P, P), MASKED, np.float32), 1)
    for name, e, pairs in (("c_select16", 16, 8), ("c_select65", 65, 34)):
        sel = np.zeros((e, pairs, 2, P // 2), np.float32)
        for a in range(pairs):
            for i in range(2):
                sel[min(2 * a + i, 64), a, i] = 1
        c[name] = sel.reshape(e, pairs * P)
    for e in (16, 64):
        on = np.ones((P, NT, e), np.float32)
        on[:, :, 0] = 0
        c[f"c_goes_on{e}"] = on
    c["c_before"] = np.triu(np.ones((P, P), np.float32), 1)
    c["c_same_head"] = np.kron(np.eye(H, dtype=np.float32), np.ones((DH, DH), np.float32))
    c["c_iota"] = np.broadcast_to(np.arange(CTX, dtype=np.float32), (P, CTX))
    wide = 64
    even = np.arange(0, wide, 2, dtype=np.float32)
    at = np.arange(S, dtype=np.float32)
    angle = at[:, None] * (1.0 / 10000.0 ** (even / wide))[None, :].astype(np.float32)
    grow = (((even + 0.4 * wide) / (1.4 * wide))[None, :] ** ((at - S // 2) / 16)[:, None]).astype(np.float32)
    rotary = np.zeros((2, S, 2, 2, 2, wide // 2), np.float32)
    for i, factor in enumerate((8.0 * grow, 1.0 / grow)):
        rotary[0, :, i] = (np.cos(angle) * factor)[:, None, None, :]
        rotary[1, :, i] = (np.sin(angle) * factor)[:, None, None, :] * np.array([-1, 1], np.float32)[None, None, :, None]
    c["c_rotary"] = rotary.reshape(2, QT, P, 4 * wide).transpose(2, 0, 1, 3)
    key, query = np.arange(32 + P)[None, :], np.arange(P)[:, None]
    seen = (key >= query) & (key <= query + 32)
    band = np.stack([np.where(seen, 0, MASKED), np.where(seen & (key >= 32), 0, MASKED)], axis=1).astype(np.float32)
    c["c_band"] = np.stack([band, band], axis=2)
    c["c_causal_q"], c["c_causal_k"] = later, np.ascontiguousarray(later.T)
    return c


def _lay_out(lay, np):
    wkv = lay.pop("L1_xattn_Wkv")
    lay["L1_xattn_Wk16"] = np.tile(wkv[:DH].T, (1, H))
    lay["L1_xattn_Wv16"] = np.tile(wkv[DH:].T, (1, H))
    for n in ("q1", "k1", "q2", "k2", "v"):
        lay[f"L2_attn_w{n}"] = lay[f"L2_attn_w{n}"].transpose(1, 0, 2).reshape(D, D)
    for n in ("ln_gamma", "ln_beta"):
        lay[f"L2_attn_{n}"] = np.broadcast_to(lay[f"L2_attn_{n}"], (P, D))
    lay["L2_attn_lamb"] = np.broadcast_to(lay["L2_attn_lamb"], (P, 1))
    wkv = lay.pop("L2_xattn_W_kv").reshape(D, H, 2, DH)
    bkv = lay.pop("L2_xattn_b_kv").reshape(H, 2, DH)
    for i, n in enumerate("kv"):
        lay[f"L2_xattn_W_{n}"] = wkv[:, :, i].reshape(D, D)
        lay[f"L2_xattn_b_{n}"] = bkv[:, i].reshape(D)
    lay["L0_ffn_e_bias"] = np.broadcast_to(lay["L0_ffn_e_bias"], (P, 16))
    lay["L0_ffn_pairs"] = np.concatenate(
        [lay.pop(f"L0_ffn_{n}_proj").reshape(8, P, D).transpose(0, 2, 1) for n in ("gate", "up")] +
        [lay.pop("L0_ffn_down_proj").reshape(8, 2, D, 64).transpose(0, 1, 3, 2).reshape(8, P, D)], axis=2)
    gate_up = lay.pop("L2_ffn_expert_gate_up_w").reshape(32, 2, D, 2, 64).transpose(0, 3, 2, 1, 4).reshape(32, 2, D, P)
    shared = lay.pop("L2_ffn_shared_gate_up_w").reshape(D, 2, 2, P).transpose(2, 1, 0, 3)
    gate_up = np.concatenate([gate_up, shared])
    down = np.concatenate([lay.pop("L2_ffn_expert_down_w").reshape(32, P, D),
                           lay.pop("L2_ffn_shared_down_w").reshape(2, P, D)])
    lay["L2_ffn_pairs"] = np.concatenate([gate_up[:, 0], gate_up[:, 1], down], axis=2)
    lay["L2_ffn_router"] = np.concatenate([lay.pop("L2_ffn_gate_w"), lay.pop("L2_ffn_shared_gate_w")], axis=1)
    lay["L1_ffn_columns"] = np.stack([lay.pop(f"L1_ffn_{n}") for n in ("ln_g", "ln_b", "attn_b", "next_b")], axis=1)
    lay["L1_ffn_experts"] = np.concatenate(
        [lay.pop("L1_ffn_w1"), lay.pop("L1_ffn_w2").reshape(8, 4, P, D).transpose(0, 2, 1, 3).reshape(8, P, 4 * D),
         lay.pop("L1_ffn_b1").reshape(8, 4, P).transpose(0, 2, 1), lay.pop("L1_ffn_b2").reshape(8, P, 1)], axis=2)
    lay["L3_attn_columns"] = np.concatenate(
        [lay.pop("L3_attn_bqkv").reshape(3, D), lay.pop("L3_attn_bproj").reshape(1, D),
         np.broadcast_to(lay.pop("L3_attn_scale"), (1, D))]).T
    lay["L3_xattn_columns"] = np.stack(
        [lay.pop(f"L3_xattn_ln_{n}") for n in ("x_g", "x_b", "l_g", "l_b")] +
        [np.tile(lay.pop(f"L3_xattn_{n}_gamma"), 2) for n in "qk"], axis=1)
    qkv = lay["L3_ffn_Wqkv"].reshape(6, D, 3, 8, P).transpose(0, 1, 3, 2, 4)
    lay["L3_ffn_Wqkv"] = qkv.reshape(6, D, 8 * 3 * P)
    lay["L3_ffn_Wo"] = lay["L3_ffn_Wo"].reshape(6, 8, P, D).transpose(0, 2, 1, 3).reshape(6, P, 8 * D)
    own = [np.tile(lay[f"L3_ffn_{n}_scale"], (1, 2)) for n in "qk"]
    other = [np.tile(np.roll(lay.pop(f"L3_ffn_{n}_scale"), 32, axis=1), (1, 2)) for n in "qk"]
    lay["L3_ffn_scales"] = np.broadcast_to(np.concatenate(own + other, axis=1)[:, None, :], (6, P, 4 * P))
    w2 = lay.pop("L3_ffn_W2")
    w2 = np.concatenate([w2, w2[:, :43]], axis=1).reshape(6, 3, P, D).transpose(0, 2, 1, 3).reshape(6, P, 3 * D)
    b1 = lay.pop("L3_ffn_b1").reshape(6, 2, 341)
    b1 = np.concatenate([b1, b1[:, :, :43]], axis=2).reshape(6, 6, P).transpose(0, 2, 1)
    lay["L3_ffn_pack"] = np.concatenate([lay.pop("L3_ffn_W1"), w2, b1] +
                                        [lay.pop(f"L3_ffn_{n}")[:, :, None] for n in ("ln_g", "ln_b", "b2")], axis=2)
    lay["mask_turned"] = lay.pop("mask_BxSxS2_ik0").transpose(2, 0, 1).reshape(CTX, T)


def kernel(**inputs):
    import numpy as np
    import concourse.bacc as _bacc
    from concourse import mybir as _mybir
    from concourse.bass_utils import run_bass_kernel_spmd as _run

    nc = _bacc.Bacc("TRN2", target_bir_lowering=False, num_devices=1)
    lay = {name: np.asarray(a) for name, a in inputs.items()}
    lay["xT"] = lay["x"].reshape(T, D).T
    lay["ctxT"] = lay["ctx_1024"].reshape(B * CTX, D).T
    for name in _TURNED:
        lay[name] = lay[name].T
    _lay_out(lay, np)
    lay.update(_constants(np))
    arrays, io = {}, {}
    for name, a in lay.items():
        a = np.ascontiguousarray(a)
        if a.ndim == 0:
            a = a.reshape(1)
        arrays[f"in_{name}_dram"] = a
        io[name] = nc.dram_tensor(f"in_{name}_dram", a.shape, _mybir.dt.from_np(a.dtype), kind="ExternalInput").ap()
    out = nc.dram_tensor("out_0_dram", (B, S, D), F32, kind="ExternalOutput").ap()
    build(nc, io, out)
    r = _run(nc, [arrays], core_ids=[0])
    return r.results[0]["out_0_dram"]
```
